# Optimizing a Trainium2 kernel written in Bass

```python
import numpy as np
import jax
import jax.numpy as jnp

def _softmax(x, axis=-1):
    return jax.nn.softmax(x, axis=axis)

def _gelu(x):
    return jax.nn.gelu(x, approximate=True)

def _silu(x):
    return jax.nn.silu(x)

def _sigmoid(x):
    return jax.nn.sigmoid(x)

def _layernorm(x, axis=-1, eps=1e-05):
    m = jnp.mean(x, axis=axis, keepdims=True)
    v = jnp.var(x, axis=axis, keepdims=True)
    return (x - m) / jnp.sqrt(v + eps)

def _scatter_add(tgt, idx, src, axis=0):
    return tgt.at[idx].add(src)

def _segment_sum(src, seg, n):
    return jax.ops.segment_sum(src, seg, n)
kernel_name = 'mk_early_fusion_embed_d1_tok_img256_r4_ea58ef'

def setup_inputs(seed: int=0):
    np.random.seed(seed)
    _w = jnp.asarray

    def _rec_inputs():
        import jax
        import jax.numpy as jnp
        _rk = jax.random.key(seed)
        x = -0.000125008 + 0.999885 * jax.random.normal(jax.random.fold_in(_rk, 1), (2, 64, 64, 64), jnp.float32)
        x_txt = jax.random.randint(jax.random.fold_in(_rk, 51), (2, 512), 0, 64, jnp.int32)
        fside_BS_continuous_positions = jax.random.uniform(jax.random.fold_in(_rk, 71), (2, 512), jnp.float32, 0.0, 0.999927)
        return (x, x_txt, fside_BS_continuous_positions)
    x, x_txt, fside_BS_continuous_positions = _rec_inputs()

    def _L0_tok_setup():
        import jax, jax.numpy as jnp
        import numpy as np
        DIM = 64
        NH = 8
        WH, WW = (8, 8)

        def _rope_axis(x, axis):
            half = x.shape[-1]
            inv_freq = 1.0 / 10000.0 ** (jnp.arange(0, half, 2, dtype=jnp.float32) / half)
            pos = jnp.arange(x.shape[axis], dtype=jnp.float32)
            ang = pos[:, None] * inv_freq
            cos, sin = (jnp.cos(ang), jnp.sin(ang))
            shape = [1, 1, 1, ang.shape[-1]]
            shape[axis] = ang.shape[0]
            cos = cos.reshape(shape).astype(x.dtype)
            sin = sin.reshape(shape).astype(x.dtype)
            x1, x2 = (x[..., 0::2], x[..., 1::2])
            r1 = x1 * cos - x2 * sin
            r2 = x1 * sin + x2 * cos
            return jnp.stack([r1, r2], axis=-1).reshape(x.shape)

        def _rope2(x):
            half = x.shape[-1] // 2
            return jnp.concatenate([_rope_axis(x[..., :half], 1), _rope_axis(x[..., half:], 2)], axis=-1)
        key = jax.random.key(seed)
        ks = jax.random.split(key, 5)
        B, H, W, C = (32, 64, 64, DIM)
        s = 1.0 / np.sqrt(C)
        return {'x': jax.random.normal(ks[0], (B, H, W, C), dtype=jnp.float32), 'qkv_w': jax.random.uniform(ks[1], (3 * C, C), jnp.float32, -s, s), 'qkv_b': jax.random.uniform(ks[2], (3 * C,), jnp.float32, -s, s), 'proj_w': jax.random.uniform(ks[3], (C, C), jnp.float32, -s, s), 'proj_b': jax.random.uniform(ks[4], (C,), jnp.float32, -s, s)}
    _L0_tok_all = _L0_tok_setup()
    _L0_tok_in = {k: v for k, v in _L0_tok_all.items() if k in ('qkv_w', 'qkv_b', 'proj_w', 'proj_b')}
    del _L0_tok_all

    def _L0_txt_setup():
        import jax, jax.numpy as jnp
        import numpy as np
        N_SCALES = 4

        def _conv1d(x, w, b, pad):
            y = jax.lax.conv_general_dilated(x, w, window_strides=(1,), padding=[(pad, pad)], dimension_numbers=('NCH', 'OIH', 'NCH'))
            return y + b[None, :, None]
        key = jax.random.key(seed)
        ks = jax.random.split(key, 12)
        B, S, P, D = (8, 512, 512, 64)
        byte_sequence = jax.random.randint(ks[0], (B, S), 0, 64, dtype=jnp.int64)
        continuous_positions = jax.random.uniform(ks[1], (B, P), dtype=jnp.float32)
        emb = jax.random.normal(ks[2], (64, D), dtype=jnp.float32)
        locality_shapes = jax.random.normal(ks[3], (64, 4), dtype=jnp.float32)
        w1 = jax.random.normal(ks[4], (128, 64, 7), dtype=jnp.float32) * 0.02
        b1 = jnp.zeros((128,), dtype=jnp.float32)
        w2 = jax.random.normal(ks[5], (64, 128, 5), dtype=jnp.float32) * 0.02
        b2 = jnp.zeros((64,), dtype=jnp.float32)
        w3 = jax.random.normal(ks[6], (1, 64, 3), dtype=jnp.float32) * 0.02
        b3 = jnp.zeros((1,), dtype=jnp.float32)
        multiscale_widths = jnp.array([0.01, 0.02, 0.05, 0.1], dtype=jnp.float32)
        scale_weights = jnp.ones((4,), dtype=jnp.float32)
        return {'byte_sequence': byte_sequence, 'continuous_positions': continuous_positions, 'emb': emb, 'locality_shapes': locality_shapes, 'w1': w1, 'b1': b1, 'w2': w2, 'b2': b2, 'w3': w3, 'b3': b3, 'multiscale_widths': multiscale_widths, 'scale_weights': scale_weights}
    _L0_txt_all = _L0_txt_setup()
    _L0_txt_in = {k: v for k, v in _L0_txt_all.items() if k in ('emb', 'locality_shapes', 'w1', 'b1', 'w2', 'b2', 'w3', 'b3', 'multiscale_widths', 'scale_weights')}
    del _L0_txt_all

    def _L0_attn_setup():
        import jax, jax.numpy as jnp
        import numpy as np
        H = 8
        M = 64
        PINV_ITERS = 6
        PAD = 16

        def layernorm(x, g, b, eps=1e-05):
            mu = x.mean(-1, keepdims=True)
            var = ((x - mu) ** 2).mean(-1, keepdims=True)
            return (x - mu) * jax.lax.rsqrt(var + eps) * g + b

        def moore_penrose_pinv(x, iters=PINV_ITERS):
            abs_x = jnp.abs(x)
            col = abs_x.sum(-1)
            row = abs_x.sum(-2)
            z = jnp.swapaxes(x, -1, -2) / (jnp.max(col) * jnp.max(row))
            eye = jnp.eye(x.shape[-1], dtype=x.dtype)
            for _ in range(iters):
                xz = x @ z
                z = 0.25 * z @ (13.0 * eye - xz @ (15.0 * eye - xz @ (7.0 * eye - xz)))
            return z

        def attn_block(y, ln1_g, ln1_b, w_qkv, w_out, b_out, res_w, ln2_g, ln2_b, w1, b1, w2, b2):
            B, N, D = y.shape
            inner = w_qkv.shape[1] // 3
            dh = inner // H
            xn = layernorm(y, ln1_g, ln1_b)
            qkv = xn @ w_qkv
            q, k, v = jnp.split(qkv, 3, axis=-1)
            to_heads = lambda t: t.reshape(B, N, H, dh).transpose(0, 2, 1, 3)
            q, k, v = map(to_heads, (q, k, v))
            q = q * dh ** (-0.5)
            l = N // M
            q_l = q.reshape(B, H, M, l, dh).mean(3)
            k_l = k.reshape(B, H, M, l, dh).mean(3)
            attn1 = jax.nn.softmax(jnp.einsum('bhnd,bhmd->bhnm', q, k_l), axis=-1)
            attn2 = jax.nn.softmax(jnp.einsum('bhid,bhjd->bhij', q_l, k_l), axis=-1)
            attn3 = jax.nn.softmax(jnp.einsum('bhmd,bhnd->bhmn', q_l, k), axis=-1)
            attn2_inv = moore_penrose_pinv(attn2)
            out = attn1 @ attn2_inv @ (attn3 @ v)
            res = jax.lax.conv_general_dilated(v, res_w, window_strides=(1, 1), padding=[(PAD, PAD), (0, 0)], dimension_numbers=('NCHW', 'OIHW', 'NCHW'), feature_group_count=H)
            out = out + res
            out = out.transpose(0, 2, 1, 3).reshape(B, N, inner)
            y = y + out @ w_out + b_out
            yn = layernorm(y, ln2_g, ln2_b)
            hdn = jax.nn.gelu(yn @ w1 + b1, approximate=False)
            return y + hdn @ w2 + b2
        key = jax.random.key(seed)
        ks = jax.random.split(key, 8)
        B, N, D, NB = (4, 1024, 64, 2)
        inner = D
        p = lambda k, shp: jax.random.normal(k, shp, jnp.float32) * 0.02
        return {'x': jax.random.normal(ks[0], (B, N, D), jnp.float32), 'ln1_g': jnp.ones((NB, D), jnp.float32), 'ln1_b': jnp.zeros((NB, D), jnp.float32), 'w_qkv': p(ks[1], (NB, D, 3 * inner)), 'w_out': p(ks[2], (NB, inner, D)), 'b_out': jnp.zeros((NB, D), jnp.float32), 'res_w': p(ks[3], (NB, H, 1, 33, 1)), 'ln2_g': jnp.ones((NB, D), jnp.float32), 'ln2_b': jnp.zeros((NB, D), jnp.float32), 'w1': p(ks[4], (NB, D, 2 * D)), 'b1': jnp.zeros((NB, 2 * D), jnp.float32), 'w2': p(ks[5], (NB, 2 * D, D)), 'b2': jnp.zeros((NB, D), jnp.float32)}
    _L0_attn_all = _L0_attn_setup()
    _L0_attn_in = {k: v for k, v in _L0_attn_all.items() if k in ('ln1_g', 'ln1_b', 'w_qkv', 'w_out', 'b_out', 'res_w', 'ln2_g', 'ln2_b', 'w1', 'b1', 'w2', 'b2')}
    del _L0_attn_all

    def _L0_ffn_setup():
        import jax, jax.numpy as jnp
        import numpy as np
        D_MODEL = 64
        N_EXPERTS = 16
        HIDDEN = 128
        SCALE = 0.02
        key = jax.random.key(seed)
        ks = jax.random.split(key, 5)
        x = jax.random.normal(ks[0], (4, 2048, D_MODEL), dtype=jnp.float32)
        gate_w = jax.random.normal(ks[1], (D_MODEL, N_EXPERTS), dtype=jnp.float32) * SCALE
        gate_b = jnp.zeros((N_EXPERTS,), dtype=jnp.float32)
        w1 = jax.random.normal(ks[2], (N_EXPERTS, D_MODEL, HIDDEN), dtype=jnp.float32) * SCALE
        w2 = jax.random.normal(ks[3], (N_EXPERTS, D_MODEL, HIDDEN), dtype=jnp.float32) * SCALE
        w3 = jax.random.normal(ks[4], (N_EXPERTS, HIDDEN, D_MODEL), dtype=jnp.float32) * SCALE
        return {'x': x, 'gate_w': gate_w, 'gate_b': gate_b, 'w1': w1, 'w2': w2, 'w3': w3}
    _L0_ffn_all = _L0_ffn_setup()
    _L0_ffn_in = {k: v for k, v in _L0_ffn_all.items() if k in ('gate_w', 'gate_b', 'w1', 'w2', 'w3')}
    del _L0_ffn_all
    return {'x': x, 'x_txt': x_txt, 'fside_BS_continuous_positions': fside_BS_continuous_positions, 'L0_tok_qkv_w': _L0_tok_in['qkv_w'], 'L0_tok_qkv_b': _L0_tok_in['qkv_b'], 'L0_tok_proj_w': _L0_tok_in['proj_w'], 'L0_tok_proj_b': _L0_tok_in['proj_b'], 'L0_txt_emb': _L0_txt_in['emb'], 'L0_txt_locality_shapes': _L0_txt_in['locality_shapes'], 'L0_txt_w1': _L0_txt_in['w1'], 'L0_txt_b1': _L0_txt_in['b1'], 'L0_txt_w2': _L0_txt_in['w2'], 'L0_txt_b2': _L0_txt_in['b2'], 'L0_txt_w3': _L0_txt_in['w3'], 'L0_txt_b3': _L0_txt_in['b3'], 'L0_txt_multiscale_widths': _L0_txt_in['multiscale_widths'], 'L0_txt_scale_weights': _L0_txt_in['scale_weights'], 'L0_attn_ln1_g': _L0_attn_in['ln1_g'], 'L0_attn_ln1_b': _L0_attn_in['ln1_b'], 'L0_attn_w_qkv': _L0_attn_in['w_qkv'], 'L0_attn_w_out': _L0_attn_in['w_out'], 'L0_attn_b_out': _L0_attn_in['b_out'], 'L0_attn_res_w': _L0_attn_in['res_w'], 'L0_attn_ln2_g': _L0_attn_in['ln2_g'], 'L0_attn_ln2_b': _L0_attn_in['ln2_b'], 'L0_attn_w1': _L0_attn_in['w1'], 'L0_attn_b1': _L0_attn_in['b1'], 'L0_attn_w2': _L0_attn_in['w2'], 'L0_attn_b2': _L0_attn_in['b2'], 'L0_ffn_gate_w': _L0_ffn_in['gate_w'], 'L0_ffn_gate_b': _L0_ffn_in['gate_b'], 'L0_ffn_w1': _L0_ffn_in['w1'], 'L0_ffn_w2': _L0_ffn_in['w2'], 'L0_ffn_w3': _L0_ffn_in['w3']}

def reference(x, x_txt, fside_BS_continuous_positions, L0_tok_qkv_w, L0_tok_qkv_b, L0_tok_proj_w, L0_tok_proj_b, L0_txt_emb, L0_txt_locality_shapes, L0_txt_w1, L0_txt_b1, L0_txt_w2, L0_txt_b2, L0_txt_w3, L0_txt_b3, L0_txt_multiscale_widths, L0_txt_scale_weights, L0_attn_ln1_g, L0_attn_ln1_b, L0_attn_w_qkv, L0_attn_w_out, L0_attn_b_out, L0_attn_res_w, L0_attn_ln2_g, L0_attn_ln2_b, L0_attn_w1, L0_attn_b1, L0_attn_w2, L0_attn_b2, L0_ffn_gate_w, L0_ffn_gate_b, L0_ffn_w1, L0_ffn_w2, L0_ffn_w3):
    import jax
    import jax.numpy as jnp

    def _L0_tok_ref(x, qkv_w, qkv_b, proj_w, proj_b):
        import jax, jax.numpy as jnp
        import numpy as np
        DIM = 64
        NH = 8
        WH, WW = (8, 8)

        def _rope_axis(x, axis):
            half = x.shape[-1]
            inv_freq = 1.0 / 10000.0 ** (jnp.arange(0, half, 2, dtype=jnp.float32) / half)
            pos = jnp.arange(x.shape[axis], dtype=jnp.float32)
            ang = pos[:, None] * inv_freq
            cos, sin = (jnp.cos(ang), jnp.sin(ang))
            shape = [1, 1, 1, ang.shape[-1]]
            shape[axis] = ang.shape[0]
            cos = cos.reshape(shape).astype(x.dtype)
            sin = sin.reshape(shape).astype(x.dtype)
            x1, x2 = (x[..., 0::2], x[..., 1::2])
            r1 = x1 * cos - x2 * sin
            r2 = x1 * sin + x2 * cos
            return jnp.stack([r1, r2], axis=-1).reshape(x.shape)

        def _rope2(x):
            half = x.shape[-1] // 2
            return jnp.concatenate([_rope_axis(x[..., :half], 1), _rope_axis(x[..., half:], 2)], axis=-1)
        B, H, W, C = x.shape
        hd = C // NH
        N = WH * WW
        xw = x.reshape(B, H // WH, WH, W // WW, WW, C).transpose(0, 1, 3, 2, 4, 5).reshape(-1, N, C)
        qkv = xw @ qkv_w.T + qkv_b
        qkv = qkv.reshape(-1, N, 3, NH, hd).transpose(2, 0, 3, 1, 4)
        q, k, v = (qkv[0], qkv[1], qkv[2])
        q = _rope2(q.reshape(-1, WH, WW, hd)).reshape(-1, NH, N, hd)
        k = _rope2(k.reshape(-1, WH, WW, hd)).reshape(-1, NH, N, hd)
        scale = hd ** (-0.5)
        attn = jax.nn.softmax(q * scale @ jnp.swapaxes(k, -2, -1), axis=-1)
        out = (attn @ v).transpose(0, 2, 1, 3).reshape(-1, N, C)
        out = out.reshape(B, H // WH, W // WW, WH, WW, C).transpose(0, 1, 3, 2, 4, 5).reshape(B, H * W, C)
        return out @ proj_w.T + proj_b

    def _L0_txt_ref(byte_sequence, continuous_positions, emb, locality_shapes, w1, b1, w2, b2, w3, b3, multiscale_widths, scale_weights):
        import jax, jax.numpy as jnp
        import numpy as np
        N_SCALES = 4

        def _conv1d(x, w, b, pad):
            y = jax.lax.conv_general_dilated(x, w, window_strides=(1,), padding=[(pad, pad)], dimension_numbers=('NCH', 'OIH', 'NCH'))
            return y + b[None, :, None]
        B, S = byte_sequence.shape
        P = continuous_positions.shape[1]
        amps = emb[byte_sequence]
        onehot = jax.nn.one_hot(byte_sequence, 64, dtype=jnp.float32)
        onehot = jnp.transpose(onehot, (0, 2, 1))
        h = jax.nn.gelu(_conv1d(onehot, w1, b1, 3), approximate=False)
        h = jax.nn.gelu(_conv1d(h, w2, b2, 2), approximate=False)
        ctx = jax.nn.sigmoid(_conv1d(h, w3, b3, 1))[:, 0, :]
        amps = amps * ctx[:, :, None]
        lp = locality_shapes[byte_sequence]
        byte_pos = jnp.linspace(0.0, 1.0, S, dtype=jnp.float32)
        center = byte_pos[None, :] + lp[..., 0] * 0.05
        xd = continuous_positions[:, None, :] - center[..., None]
        amp_scale = jax.nn.sigmoid(lp[..., 2])
        phase = lp[..., 3] * jnp.pi
        abs_w = jnp.abs(lp[..., 1])
        TWO_PI = 2.0 * jnp.pi
        basis_total = jnp.zeros((B, S, P), dtype=jnp.float32)
        for s in range(N_SCALES):
            width = abs_w * multiscale_widths[s] + 1e-05
            z = xd / width[..., None]
            basis = jnp.exp(-0.5 * z * z) * jnp.cos(phase[..., None] + TWO_PI * z)
            basis_total = basis_total + basis * (amp_scale[..., None] * scale_weights[s] ** 2)
        semantic_field = jnp.einsum('bsp,bsd->bpd', basis_total, amps)
        return semantic_field

    def _L0_attn_ref(x, ln1_g, ln1_b, w_qkv, w_out, b_out, res_w, ln2_g, ln2_b, w1, b1, w2, b2):
        import jax, jax.numpy as jnp
        import numpy as np
        H = 8
        M = 64
        PINV_ITERS = 6
        PAD = 16

        def layernorm(x, g, b, eps=1e-05):
            mu = x.mean(-1, keepdims=True)
            var = ((x - mu) ** 2).mean(-1, keepdims=True)
            return (x - mu) * jax.lax.rsqrt(var + eps) * g + b

        def moore_penrose_pinv(x, iters=PINV_ITERS):
            abs_x = jnp.abs(x)
            col = abs_x.sum(-1)
            row = abs_x.sum(-2)
            z = jnp.swapaxes(x, -1, -2) / (jnp.max(col) * jnp.max(row))
            eye = jnp.eye(x.shape[-1], dtype=x.dtype)
            for _ in range(iters):
                xz = x @ z
                z = 0.25 * z @ (13.0 * eye - xz @ (15.0 * eye - xz @ (7.0 * eye - xz)))
            return z

        def attn_block(y, ln1_g, ln1_b, w_qkv, w_out, b_out, res_w, ln2_g, ln2_b, w1, b1, w2, b2):
            B, N, D = y.shape
            inner = w_qkv.shape[1] // 3
            dh = inner // H
            xn = layernorm(y, ln1_g, ln1_b)
            qkv = xn @ w_qkv
            q, k, v = jnp.split(qkv, 3, axis=-1)
            to_heads = lambda t: t.reshape(B, N, H, dh).transpose(0, 2, 1, 3)
            q, k, v = map(to_heads, (q, k, v))
            q = q * dh ** (-0.5)
            l = N // M
            q_l = q.reshape(B, H, M, l, dh).mean(3)
            k_l = k.reshape(B, H, M, l, dh).mean(3)
            attn1 = jax.nn.softmax(jnp.einsum('bhnd,bhmd->bhnm', q, k_l), axis=-1)
            attn2 = jax.nn.softmax(jnp.einsum('bhid,bhjd->bhij', q_l, k_l), axis=-1)
            attn3 = jax.nn.softmax(jnp.einsum('bhmd,bhnd->bhmn', q_l, k), axis=-1)
            attn2_inv = moore_penrose_pinv(attn2)
            out = attn1 @ attn2_inv @ (attn3 @ v)
            res = jax.lax.conv_general_dilated(v, res_w, window_strides=(1, 1), padding=[(PAD, PAD), (0, 0)], dimension_numbers=('NCHW', 'OIHW', 'NCHW'), feature_group_count=H)
            out = out + res
            out = out.transpose(0, 2, 1, 3).reshape(B, N, inner)
            y = y + out @ w_out + b_out
            yn = layernorm(y, ln2_g, ln2_b)
            hdn = jax.nn.gelu(yn @ w1 + b1, approximate=False)
            return y + hdn @ w2 + b2
        y = x
        for i in range(ln1_g.shape[0]):
            y = attn_block(y, ln1_g[i], ln1_b[i], w_qkv[i], w_out[i], b_out[i], res_w[i], ln2_g[i], ln2_b[i], w1[i], b1[i], w2[i], b2[i])
        return y

    def _L0_ffn_ref(x, gate_w, gate_b, w1, w2, w3):
        import jax, jax.numpy as jnp
        import numpy as np
        D_MODEL = 64
        N_EXPERTS = 16
        HIDDEN = 128
        SCALE = 0.02
        n_experts = w1.shape[0]
        logits = jnp.einsum('bsd,de->bse', x, gate_w) + gate_b
        probs = jax.nn.softmax(logits, axis=-1)
        top_probs, top_idx = jax.lax.top_k(probs, 2)
        top_probs = top_probs / jnp.sum(top_probs, axis=-1, keepdims=True)
        dispatch = jnp.sum(jax.nn.one_hot(top_idx, n_experts, dtype=x.dtype) * top_probs[..., None], axis=-2)
        h1 = jnp.einsum('bsd,edh->bseh', x, w1)
        h2 = jnp.einsum('bsd,edh->bseh', x, w2)
        hidden = jax.nn.silu(h1) * h2
        expert_out = jnp.einsum('bseh,eho->bseo', hidden, w3)
        return jnp.einsum('bseo,bse->bso', expert_out, dispatch)
    h = _L0_tok_ref(x, L0_tok_qkv_w, L0_tok_qkv_b, L0_tok_proj_w, L0_tok_proj_b)
    h = jnp.concatenate([h, _L0_txt_ref(x_txt, fside_BS_continuous_positions, L0_txt_emb, L0_txt_locality_shapes, L0_txt_w1, L0_txt_b1, L0_txt_w2, L0_txt_b2, L0_txt_w3, L0_txt_b3, L0_txt_multiscale_widths, L0_txt_scale_weights)], axis=1)
    h = h + _L0_attn_ref(_layernorm(h, axis=-1), L0_attn_ln1_g, L0_attn_ln1_b, L0_attn_w_qkv, L0_attn_w_out, L0_attn_b_out, L0_attn_res_w, L0_attn_ln2_g, L0_attn_ln2_b, L0_attn_w1, L0_attn_b1, L0_attn_w2, L0_attn_b2)
    h = h + _L0_ffn_ref(_layernorm(h, axis=-1), L0_ffn_gate_w, L0_ffn_gate_b, L0_ffn_w1, L0_ffn_w2, L0_ffn_w3)
    return h

_drawn_inputs = setup_inputs


def setup_inputs(seed=0):
    import zlib

    import numpy as np

    out = dict(_drawn_inputs(seed))
    spreads = {'L0_txt_b1': (0.0, 0.8),
     'L0_txt_b2': (0.0, 0.8),
     'L0_txt_scale_weights': (1.0, 0.2),
     'L0_attn_ln1_g': (1.0, 0.6),
     'L0_attn_ln1_b': (0.0, 0.8),
     'L0_attn_b_out': (0.0, 0.1),
     'L0_attn_ln2_g': (1.0, 0.6),
     'L0_attn_ln2_b': (0.0, 0.8),
     'L0_attn_b1': (0.0, 0.77),
     'L0_attn_b2': (0.0, 0.1),
     'L0_ffn_gate_b': (0.0, 0.8)}
    factors = {'L0_txt_w1': 8.0,
     'L0_txt_w2': 8.0,
     'L0_txt_w3': 8.0,
     'L0_attn_w_qkv': 2.67,
     'L0_attn_w_out': 2.729,
     'L0_attn_res_w': 8.0,
     'L0_attn_w1': 3.242,
     'L0_attn_w2': 2.684,
     'L0_ffn_gate_w': 8.0,
     'L0_ffn_w1': 8.0,
     'L0_ffn_w2': 8.0,
     'L0_ffn_w3': 8.0}
    for name, (base, spread) in spreads.items():
        noise = np.random.default_rng([zlib.crc32(name.encode()), seed]).standard_normal(out[name].shape)
        drawn = base * np.exp(spread * noise) if base else spread * noise
        out[name] = jnp.asarray(drawn.astype(out[name].dtype))
    for name, factor in factors.items():
        out[name] = (out[name] * factor).astype(out[name].dtype)
    return out
```

```python
from contextlib import ExitStack

import numpy as np

import concourse.bass as bass
from concourse import mybir

F32 = mybir.dt.float32
I32 = mybir.dt.int32
ALU = mybir.AluOpType
ACT = mybir.ActivationFunctionType
AX = mybir.AxisListType

P = 128
B = 2
C = 64
NH = 8
HD = C // NH
IMG = 64
WIN = 8
NT_IMG = IMG * IMG // P
S_TXT = 512
NT = NT_IMG + S_TXT // P
N_TOK = NT * P
M = 64
GROUP = N_TOK // M
CHUNK = 512
NCH = N_TOK // CHUNK
TPC = CHUNK // P
NS = 4
ROUND = 1.5 * 2.0 ** 23


class Columns:

    def __init__(self):
        self.at, self.width, self.parts = {}, 0, []

    def add(self, name, rows, array):
        array = np.asarray(array)
        self.at[name] = (rows, self.width, array.shape[1])
        self.parts.append((rows, self.width, array))
        self.width += array.shape[1]

    def array(self):
        out = np.zeros((P, self.width), np.float32)
        for (r0, r1), at, a in self.parts:
            out[r0:r1, at:at + a.shape[1]] = a
        return out

    def view(self, tile, name):
        (r0, r1), at, w = self.at[name]
        return tile[r0:r1, at:at + w]


def wait_alone(eng, sem, value, passed):
    eng.wait_ge(sem, value)
    eng.sem_inc(passed, 1)


class Steps:

    def __init__(self, eng, sem):
        self.eng, self.sem, self.base, self.n = eng, sem, 0, 0

    def tick(self, ins):
        ins.then_inc(self.sem, 1)
        self.n += 1

    def hold(self):
        self.eng.wait_ge(self.sem, self.base + self.n)

    def enter(self, i, per):
        self.outer, self.per = (self.base, self.n), per
        self.base, self.n = self.base + self.n + i * per, 0

    def leave(self, turns):
        assert self.n == self.per, (self.n, self.per)
        base, n = self.outer
        self.base, self.n = base, n + turns * self.per



def image_attention(nc, ctx, ps, x, wa, cols, h_img):
    NROW = IMG // WIN
    NW = NROW * WIN
    SCALE = float(HD) ** -0.5
    HP = NH // 2
    sb = lambda n, s: ctx.enter_context(nc.sbuf_tensor(n, s, F32))
    sem = lambda n: ctx.enter_context(nc.semaphore(n))
    x_in = sb("x_in", [P, 2, TPC, B, C])
    xT = sb("xT", [P, NROW, CHUNK])
    qT = sb("qT", [P, NROW, CHUNK])
    kT = sb("kT", [P, NROW, CHUNK])
    rope_a = sb("rope_a", [P, 2, CHUNK])
    rope_b = sb("rope_b", [P, 2, CHUNK])
    W = lambda n: cols.view(wa, n)
    ident = W("ident")
    over_windows = lambda n: W(n).rearrange("p (w n) -> p w n", w=1).broadcast_to([P, WIN, WIN * WIN])

    s_x = [sem("x_loaded_0"), sem("x_loaded_1")]
    s_xu = sem("x_used")
    s_tr = sem("x_transposed")
    s_xT = sem("xT_ready")
    s_qk = sem("qk_projected")
    s_ra = sem("rope_terms_ready")
    s_rd = sem("rope_done")

    with nc.Block() as block:
        @block.sync
        def _(sp):
            with sp.Fori(0, NROW // 2) as i:
                for u in range(2):
                    sp.wait_ge(s_xu, 2 * i + u + 1)
                    for b in range(B):
                        rows = x[b].rearrange("(i u t y) x c -> i u (y x) t c", u=2, t=TPC, y=2)
                        sp.dma_start(x_in[:, u, :, b, :], rows[i, u]).then_inc(s_x[u], 16)

        @block.tensor
        def _(pe):
            pe.sem_inc(s_xu, 2)
            pe.sem_inc(s_ra, 4)
            with pe.Fori(0, NROW // 2) as i:
                for u in range(2):
                    pe.wait_ge(s_x[u], 32 * i + 32)
                    for t in range(TPC):
                        ins = pe.transpose(ps[:, 0, t * P:(t + 1) * P],
                                           x_in[:, u, t].rearrange("p b c -> p (b c)"), ident)
                    ins.then_inc(s_tr, 1)
                    pe.wait_ge(s_tr, 2 * i + u + 1)
                    pe.sem_inc(s_xu, 1)
                    pe.wait_ge(s_xT, 2 * i + u + 1)
                    pe.wait_ge(s_ra, 4 * (2 * i + u) + 4)
                    chunk = xT[:, :, :].rearrange("p (i u) n -> p i u n", u=2)[:, i, u]
                    for n, name in enumerate(("wq", "wq_pair", "wk", "wk_pair")):
                        pe.matmul(ps[:, 1 + n, :], W(name), chunk, start=True, stop=True).then_inc(s_qk, 1)

        @block.scalar
        def _(act):
            with act.Fori(0, NROW // 2) as i:
                for u in range(2):
                    act.wait_ge(s_tr, 2 * i + u + 1)
                    out = xT[:, :, :].rearrange("p (i u) (w y x) -> p i u y w x", u=2, y=WIN, x=WIN)[:, i, u]
                    for y in range(WIN):
                        ins = act.activation(out[:, y], ps[:, 0, y * IMG:(y + 1) * IMG].rearrange(
                            "p (w x) -> p w x", x=WIN), ACT.Copy)
                    ins.then_inc(s_xT, 1)

        @block.vector
        def _(dve):
            dve.sem_inc(s_rd, 1)
            with dve.Fori(0, NROW // 2) as i:
                for u in range(2):
                    for n in range(4):
                        dve.wait_ge(s_qk, 4 * (2 * i + u) + n + 1)
                        if n == 0:
                            dve.wait_ge(s_rd, 2 * i + u + 1)
                        out = (rope_a, rope_b)[n % 2][:, n // 2, :].rearrange("p (w n) -> p w n", w=WIN)
                        dve.scalar_tensor_tensor(
                            out=out, in0=ps[:, 1 + n, :].rearrange("p (w n) -> p w n", w=WIN),
                            scalar=W("bias")[:, n:n + 1], in1=over_windows(("cos", "sin")[n % 2]),
                            op0=ALU.add, op1=ALU.mult).then_inc(s_ra, 1)

        @block.gpsimd
        def _(pool):
            with pool.Fori(0, NROW // 2) as i:
                for u in range(2):
                    pool.wait_ge(s_ra, 4 * (2 * i + u) + 8)
                    for n, dst in enumerate((qT, kT)):
                        out = dst[:, :, :].rearrange("p (i u) n -> p i u n", u=2)[:, i, u]
                        ins = pool.tensor_tensor(out, rope_a[:, n], rope_b[:, n], ALU.add)
                    ins.then_inc(s_rd, 1)

    q_diag = sb("q_diag", [P, 2, B, C])
    k_diag = sb("k_diag", [P, 2, NH, C])
    x_twice = sb("x_twice", [P, 2, 2, C])
    scores = sb("scores", [P, 2, NH * C])
    probs = sb("probs", [P, 2, NH * C])
    probsT = sb("probsT", [P, 2, NH * C])
    V1 = HD + 1
    v_diag = sb("v_diag", [P, 2, HP, B, 2, V1])
    row_max = sb("row_max", [P, 2, NH])
    row_inv = sb("row_inv", [P, 2, NH])
    att = sb("att", [P, 2, NH, HD])
    attT = sb("attT", [P, P])
    proj = sb("proj", [P, NROW, WIN, C])
    s_op = sem("window_operands")
    s_opu = sem("window_operands_used")
    s_s = sem("window_scores")
    s_v = sem("window_values")
    s_vd = sem("window_v_diag")
    s_mx = sem("window_max")
    s_sub = sem("window_sub")
    s_e = sem("window_exp")
    s_pt = sem("window_probsT")
    s_ptc = sem("window_probsT_copied")
    s_pv = sem("window_pv")
    s_iv = sem("window_inverse")
    s_at = sem("window_att")
    s_ot = sem("window_attT")
    s_otc = sem("window_attT_copied")
    s_pr = sem("window_projected")
    s_prc = sem("window_projected_copied")
    s_init = sem("window_init")
    s_out = sem("h_img_stored")
    nturn = NW // 2
    unit = lambda i, u: 2 * i + u

    with nc.Block() as block:
        @block.gpsimd
        def _(pool):
            batches = W("batch_of").rearrange("p (b n) -> p b n", n=1).broadcast_to([P, B, C])
            heads = W("head_of").rearrange("p (h n) -> p h n", n=1).broadcast_to([P, NH, C])
            with pool.Fori(0, nturn) as i:
                for u in range(2):
                    win = lambda t: t[:, :, :].rearrange("p r (w n) -> p (r w) n", n=C).rearrange(
                        "p (i u) n -> p i u n", u=2)[:, i, u]
                    pool.wait_ge(s_opu, unit(i, u) + 1)
                    pool.tensor_tensor(q_diag[:, u], win(qT).rearrange("p (a n) -> p a n", a=1).broadcast_to(
                        [P, B, C]), batches, ALU.mult)
                    pool.tensor_copy(x_twice[:, u], win(xT).rearrange("p (a n) -> p a n", a=1).broadcast_to([P, 2, C]))
                    pool.tensor_tensor(k_diag[:, u], win(kT).rearrange("p (a n) -> p a n", a=1).broadcast_to(
                        [P, NH, C]), heads, ALU.mult).then_inc(s_op, 1)

        @block.tensor
        def _(pe):
            pe.sem_inc(s_opu, 2)
            pe.wait_ge(s_init, 2)
            with pe.Fori(0, nturn) as i:
                for u in range(2):
                    pe.wait_ge(s_op, unit(i, u) + 1)
                    pe.matmul(ps[:, u, :], q_diag[:, u].rearrange("p b n -> p (b n)"),
                              k_diag[:, u].rearrange("p h n -> p (h n)"), start=True, stop=True).then_inc(s_s, 1)
                    pe.matmul(ps[:, 2 + u, 0:P], x_twice[:, u].rearrange("p a n -> p (a n)"), W("wv"),
                              start=True, stop=True).then_inc(s_v, 1)
                for u in range(2):
                    pe.wait_ge(s_v, unit(i, u) + 1)
                    pe.sem_inc(s_opu, 1)
                    pe.wait_ge(s_e, unit(i, u) + 1)
                    for n in range(HP):
                        ins = pe.transpose(ps[:, u, n * P:(n + 1) * P], probs[:, u, n * P:(n + 1) * P], ident)
                    ins.then_inc(s_pt, 1)
                for u in range(2):
                    pe.wait_ge(s_vd, unit(i, u) + 1)
                    pe.wait_ge(s_ptc, unit(i, u) + 1)
                    for n in range(HP):
                        ins = pe.matmul(ps[:, 4 + u, n * 4 * V1:(n + 1) * 4 * V1], probsT[:, u, n * P:(n + 1) * P],
                                        v_diag[:, u, n].rearrange("p b h e -> p (b h e)"), start=True, stop=True)
                    ins.then_inc(s_pv, 1)
                pe.wait_ge(s_at, 2 * i + 2)
                pe.transpose(ps[:, 6, 0:P], att[:, :].rearrange("p u h d -> p (u h d)"), ident).then_inc(s_ot, 1)
                pe.wait_ge(s_otc, i + 1)
                pe.matmul(ps[:, 7, 0:P], attT[:], W("wproj"), start=True, stop=True).then_inc(s_pr, 1)
                pe.wait_ge(s_prc, i + 1)

        @block.vector
        def _(dve):
            dve.memset(v_diag[:], 0.0).then_inc(s_init, 1)
            dve.wait_ge(s_init, 1)
            for hp in range(2):
                ins = dve.memset(v_diag[hp * C:(hp + 1) * C, :, :, :, hp, HD:V1], 1.0)
            ins.then_inc(s_init, 1)
            dve.wait_ge(s_init, 2)
            bias_v = W("bias_v").rearrange("p (b n e h d) -> p b n e h d", b=B, n=HP, e=1, h=2)
            with dve.Fori(0, nturn) as i:
                for u in range(2):
                    dve.wait_ge(s_s, unit(i, u) + 1)
                    s3 = ps[:, u, :].rearrange("p (h n) -> p h n", h=NH)
                    dve.tensor_reduce(row_max[:, u], s3, AX.X, ALU.max).then_inc(s_mx, 1)
                for u in range(2):
                    dve.wait_ge(s_v, unit(i, u) + 1)
                    for hp in range(2):
                        rows = slice(hp * C, (hp + 1) * C)
                        src = ps[rows, 2 + u, 0:P].rearrange("p (b n h d) -> p b n h d", b=B, n=HP, h=2)
                        ins = dve.tensor_tensor(v_diag[rows, u, :, :, hp, 0:HD].rearrange("p n b d -> p b n d"),
                                                src[:, :, :, hp], bias_v[rows, :, :, 0, hp], ALU.add)
                    ins.then_inc(s_vd, 1)
                for u in range(2):
                    s3 = ps[:, u, :].rearrange("p (h n) -> p h n", h=NH)
                    dve.wait_ge(s_mx, unit(i, u) + 1)
                    mx = row_max[:, u].rearrange("p (h n) -> p h n", n=1).broadcast_to([P, NH, C])
                    dve.tensor_tensor(scores[:, u].rearrange("p (h n) -> p h n", h=NH), s3, mx,
                                      ALU.subtract).then_inc(s_sub, 1)
                for u in range(2):
                    dve.wait_ge(s_pv, unit(i, u) + 1)
                    out = ps[:, 4 + u, 0:HP * 4 * V1].rearrange("p (n b h e) -> p n b h e", n=HP, b=B, h=2)
                    for b in range(B):
                        rows = slice(b * C, (b + 1) * C)
                        ins = dve.reciprocal(row_inv[rows, u].rearrange("p (n h) -> p n h", h=2), out[rows, :, b, :, HD])
                    ins.then_inc(s_iv, 1)
                for u in range(2):
                    dve.wait_ge(s_iv, unit(i, u) + 1)
                    out = ps[:, 4 + u, 0:HP * 4 * V1].rearrange("p (n b h e) -> p n b h e", n=HP, b=B, h=2)
                    for b in range(B):
                        rows = slice(b * C, (b + 1) * C)
                        inv = row_inv[rows, u].rearrange("p (n h e) -> p n h e", h=2, e=1).broadcast_to([C, HP, 2, HD])
                        ins = dve.tensor_tensor(att[rows, u].rearrange("p (n h) d -> p n h d", h=2),
                                                out[rows, :, b, :, 0:HD], inv, ALU.mult)
                    ins.then_inc(s_at, 1)
                dve.wait_ge(s_pr, i + 1)
                dst = proj[:, :, :, :].rearrange("p r w c -> p (r w c)").rearrange("p (i n) -> p i n", n=2 * C)
                dve.tensor_tensor(dst[:, i], ps[:, 7, 0:P], W("bias_proj"), ALU.add).then_inc(s_prc, 1)

        @block.scalar
        def _(act):
            with act.Fori(0, nturn) as i:
                for u in range(2):
                    act.wait_ge(s_sub, unit(i, u) + 1)
                    act.activation(probs[:, u], scores[:, u], ACT.Exp, scale=SCALE).then_inc(s_e, 1)
                for u in range(2):
                    act.wait_ge(s_pt, unit(i, u) + 1)
                    act.activation(probsT[:, u], ps[:, u, :], ACT.Copy).then_inc(s_ptc, 1)
                act.wait_ge(s_ot, i + 1)
                act.activation(attT[:], ps[:, 6, 0:P], ACT.Copy).then_inc(s_otc, 1)

        @block.sync
        def _(sp):
            with sp.Fori(0, NROW) as r:
                sp.wait_ge(s_prc, (r + 1) * (WIN // 2))
                for b in range(B):
                    dst = h_img[b].rearrange("(r y w x) c -> r y x w c", r=NROW, y=WIN, w=WIN)
                    for y in range(WIN):
                        p0 = b * C + y * WIN
                        sp.dma_start(dst[r, y], proj[p0:p0 + WIN, r]).then_inc(s_out, 16)
            sp.wait_ge(s_out, 16 * B * WIN * NROW)



def text_field(nc, ctx, ps, bytes_rep, positions_rep, wt, cols, hh):
    TT = S_TXT // P
    TILES = B * TT
    E = C + 4
    TWO_PI = 6.283185
    K1, K2, K3 = 7, 5, 3
    sb = lambda n, s, d=F32: ctx.enter_context(nc.sbuf_tensor(n, s, d))
    sem = lambda n: ctx.enter_context(nc.semaphore(n))
    W = lambda n: cols.view(wt, n)
    byte = sb("byte", [C, B, S_TXT], I32)
    pos = sb("pos", [P, B, S_TXT])
    onehot = sb("onehot", [C, B, S_TXT + K1 - 1])
    conv1 = sb("conv1", [P, B, S_TXT + K2 - 1])
    conv2 = sb("conv2", [C, B, S_TXT + K3 - 1])
    ctxw = sb("context", [P, TILES])
    gath = sb("gathered", [P, TILES, E])
    amp_scale = sb("amp_scale", [P, TILES])
    center = sb("center", [P, TILES])
    phase = sb("phase", [P, TILES])
    inv_width = sb("inv_width", [P, NS, TILES])
    sw2 = sb("scale_weight_squared", [P, NS])
    z = sb("z", [P, 2, NS, S_TXT])
    assert TILES * C == S_TXT
    amps = z[:, 0].rearrange("p s (t c) -> p s t c", c=C)
    turns = sb("turns", [P, 2, NS, S_TXT])
    env = sb("envelope", [P, TT, B, NS, S_TXT])
    wave = sb("wave", [P, TT, B, NS, S_TXT])
    packet = turns

    s_in = sem("text_loaded")
    s_cl = sem("text_cleared")
    s_oh = sem("onehot_ready")
    s_c1 = sem("conv1_ready")
    s_g1 = sem("gelu1_ready")
    s_c2 = sem("conv2_ready")
    s_g2 = sem("gelu2_ready")
    s_c3 = sem("conv3_ready")
    s_ga = sem("gather_ready")
    s_gc = sem("gathered_copied")
    s_sg = sem("sigmoids_ready")
    s_sc = sem("text_scalars")
    s_z = sem("z_ready")
    s_a = sem("turns_shifted")
    s_d = sem("turns_ready")
    s_r = sem("wave_arg_ready")
    s_sq = sem("z_squared")
    s_ex = sem("envelope_ready")
    s_si = sem("sine_ready")
    s_pk = sem("packet_ready")
    s_pm = sem("packet_summed")
    s_h = sem("text_h_ready")
    tile = lambda st, b: b * TT + st

    with nc.Block() as block:
        @block.sync
        def _(sp):
            sp.dma_start(byte[:, :, :], bytes_rep).then_inc(s_in, 16)
            sp.dma_start(pos[:, :, :], positions_rep).then_inc(s_in, 16)

        @block.vector
        def _(dve):
            step = Steps(dve, s_sc)
            dve.memset(onehot[:], 0.0).then_inc(s_cl, 1)
            dve.memset(conv1[:], 0.0).then_inc(s_cl, 1)
            dve.memset(conv2[:], 0.0).then_inc(s_cl, 1)
            dve.wait_ge(s_in, 32)
            dve.wait_ge(s_cl, 3)
            dve.tensor_scalar(onehot[:, :, K1 // 2:K1 // 2 + S_TXT], byte[:], W("iota"), None,
                              ALU.is_equal).then_inc(s_oh, 1)
            for half in range(2):
                dve.wait_ge(s_ga, half + 1)
                n = TILES // 2
                dve.tensor_copy(gath[:, half * n:(half + 1) * n], ps[:, 2 + half, 0:n * E].rearrange(
                    "p (t e) -> p t e", e=E)).then_inc(s_gc, 1)
            dve.wait_ge(s_gc, 2)
            lp = lambda k: gath[:, :, C + k]
            step.tick(dve.scalar_tensor_tensor(center[:], lp(0), 0.05, W("byte_pos"), ALU.mult, ALU.add))
            step.tick(dve.tensor_scalar(phase[:], lp(3), 0.5, 0.25, ALU.mult, ALU.add))
            step.tick(dve.tensor_tensor(sw2[:], W("scale_weights"), W("scale_weights"), ALU.mult))
            step.tick(dve.scalar_tensor_tensor(inv_width[:, 0], lp(1), -1.0, lp(1), ALU.mult, ALU.max))
            step.hold()
            for s in reversed(range(NS)):
                step.tick(dve.tensor_scalar(inv_width[:, s], inv_width[:, 0], W("widths")[:, s:s + 1], 1e-5,
                                            ALU.mult, ALU.add))
            step.hold()
            step.tick(dve.reciprocal(inv_width[:], inv_width[:]))
            step.hold()
            for st in range(TT):
                for b in range(B):
                    t, n = tile(st, b), B * st + b
                    if n >= 2:
                        dve.wait_ge(s_sq, n - 1)
                        dve.wait_ge(s_r, n - 1)
                    for s in range(NS):
                        ins = dve.tensor_scalar(z[:, b, s], pos[:, b], center[:, t:t + 1], inv_width[:, s, t:t + 1],
                                                ALU.subtract, ALU.mult)
                    ins.then_inc(s_z, 1)
                    dve.wait_ge(s_z, n + 1)
                    dve.tensor_scalar(turns[:, b], z[:, b], phase[:, t:t + 1], None, ALU.add).then_inc(s_a, 1)
                    dve.wait_ge(s_a, n + 1)
                    dve.tensor_scalar(wave[:, st, b], turns[:, b], ROUND, ROUND, ALU.add,
                                      ALU.subtract).then_inc(s_d, 1)
                    dve.wait_ge(s_d, n + 1)
                    dve.tensor_tensor(wave[:, st, b], turns[:, b], wave[:, st, b], ALU.subtract).then_inc(s_r, 1)
            dve.wait_ge(s_sg, 2)
            step.tick(dve.tensor_tensor(amp_scale[:], amp_scale[:], ctxw[:], ALU.mult))
            step.hold()
            wide = amp_scale[:].rearrange("p (t c) -> p t c", c=1).broadcast_to([P, TILES, C])
            step.tick(dve.tensor_tensor(gath[:, :, 0:C], gath[:, :, 0:C], wide, ALU.mult))
            step.hold()
            dve.wait_ge(s_sq, TILES)
            dve.wait_ge(s_d, TILES)
            for s in range(NS):
                step.tick(dve.tensor_scalar(amps[:, s], gath[:, :, 0:C], sw2[:, s:s + 1], None, ALU.mult))
            for st in range(TT):
                for b in range(B):
                    n = B * st + b
                    dve.wait_ge(s_si, n + 1)
                    dve.wait_ge(s_ex, n + 1)
                    if n == 0:
                        dve.wait_ge(s_r, TILES)
                    if n >= 2:
                        dve.wait_ge(s_pm, n - 1)
                    dve.tensor_tensor(packet[:, b], env[:, st, b], wave[:, st, b], ALU.mult).then_inc(s_pk, 1)
            for b in range(B):
                dve.wait_ge(s_pm, TILES - 1 + b)
                for p in range(TT):
                    ins = dve.tensor_copy(hh[:, NT_IMG + p, b, :], ps[:, b * TT + p, 0:C])
            ins.then_inc(s_h, 1)

        @block.tensor
        def _(pe):
            pe.wait_ge(s_oh, 1)
            w1 = W("conv1").rearrange("i (k o) -> i k o", k=K1)
            for b in range(B):
                for k in range(K1):
                    ins = pe.matmul(ps[:, b, :], w1[:, k], onehot[:, b, k:k + S_TXT], start=k == 0, stop=k == K1 - 1)
                ins.then_inc(s_c1, 1)
            for t in range(TILES):
                b, st = divmod(t, TT)
                ins = pe.matmul(ps[:, 2 + b, st * E:(st + 1) * E], onehot[:, b, K1 // 2 + st * P:K1 // 2 + (st + 1) * P],
                                W("embed"), start=True, stop=True)
                if st == TT - 1:
                    ins.then_inc(s_ga, 1)
            w2 = W("conv2").rearrange("i (k o) -> i k o", k=K2)
            for b in range(B):
                pe.wait_ge(s_g1, b + 1)
                for k in range(K2):
                    ins = pe.matmul(ps[0:C, 4 + b, :], w2[:, k], conv1[:, b, k:k + S_TXT], start=k == 0, stop=k == K2 - 1)
                ins.then_inc(s_c2, 1)
            pe.wait_ge(s_g2, B)
            for t in range(TILES):
                b, st = divmod(t, TT)
                for k in range(K3):
                    ins = pe.matmul(ps[:, 6, t:t + 1], conv2[:, b, k + st * P:k + (st + 1) * P], W("conv3")[:, k:k + 1],
                                    start=k == 0, stop=k == K3 - 1)
            ins.then_inc(s_c3, 1)
            for st in range(TT):
                for b in range(B):
                    pe.wait_ge(s_pk, B * st + b + 1)
                    if st == 0 and b == 0:
                        pe.wait_ge(s_sg, 2)
                    for p in range(TT):
                        for s in range(NS):
                            ins = pe.matmul(ps[:, b * TT + p, 0:C], packet[:, b, s, p * P:(p + 1) * P],
                                            amps[:, s, tile(st, b)], start=st == 0 and s == 0,
                                            stop=st == TT - 1 and s == NS - 1)
                    ins.then_inc(s_pm, 1)

        @block.scalar
        def _(act):
            act.wait_ge(s_cl, 3)
            for b in range(B):
                act.wait_ge(s_c1, b + 1)
                act.activation(conv1[:, b, K2 // 2:K2 // 2 + S_TXT], ps[:, b, :], ACT.Gelu,
                               bias=W("bias1")).then_inc(s_g1, 1)
            for b in range(B):
                act.wait_ge(s_c2, b + 1)
                act.activation(conv2[:, b, K3 // 2:K3 // 2 + S_TXT], ps[0:C, 4 + b, :], ACT.Gelu,
                               bias=W("bias2")).then_inc(s_g2, 1)
            act.wait_ge(s_gc, 2)
            act.wait_ge(s_c3, 1)
            act.activation(ctxw[:], ps[:, 6, 0:TILES], ACT.Sigmoid, bias=W("bias3")).then_inc(s_sg, 1)
            act.activation(amp_scale[:], gath[:, :, C + 2], ACT.Sigmoid).then_inc(s_sg, 1)
            for st in range(TT):
                for b in range(B):
                    n = B * st + b
                    act.wait_ge(s_z, n + 1)
                    act.activation(env[:, st, b], z[:, b], ACT.Square).then_inc(s_sq, 1)
                    act.wait_ge(s_sq, n + 1)
                    act.activation(env[:, st, b], env[:, st, b], ACT.Exp, scale=-0.5).then_inc(s_ex, 1)
            for st in range(TT):
                for b in range(B):
                    act.wait_ge(s_r, B * st + b + 1)
                    act.activation(wave[:, st, b], wave[:, st, b], ACT.Sin, scale=TWO_PI).then_inc(s_si, 1)


def text_columns(i):
    c = Columns()
    rep = lambda a: np.tile(np.asarray(a).reshape(1, -1), (P, 1))
    c.add("conv1", (0, C), i["L0_txt_w1"].transpose(1, 2, 0).reshape(C, -1))
    c.add("conv2", (0, P), i["L0_txt_w2"].transpose(1, 2, 0).reshape(P, -1))
    c.add("conv3", (0, C), i["L0_txt_w3"][0])
    c.add("embed", (0, C), np.concatenate([i["L0_txt_emb"], i["L0_txt_locality_shapes"]], 1))
    c.add("bias1", (0, P), i["L0_txt_b1"][:, None])
    c.add("bias2", (0, C), i["L0_txt_b2"][:, None])
    c.add("bias3", (0, P), rep(i["L0_txt_b3"]))
    c.add("widths", (0, P), rep(i["L0_txt_multiscale_widths"]))
    c.add("scale_weights", (0, P), rep(i["L0_txt_scale_weights"]))
    c.add("iota", (0, C), np.arange(C, dtype=np.float32)[:, None])
    at = np.linspace(0.0, 1.0, S_TXT, dtype=np.float32).reshape(-1, P).T
    c.add("byte_pos", (0, P), np.tile(at, (1, B)))
    return c



class Norm:

    PARTS = 3
    EPS = 1e-5

    def __init__(self, nc, ctx, name):
        sb = lambda n, s: ctx.enter_context(nc.sbuf_tensor(f"{name}_{n}", s, F32))
        self.nc = nc
        self.mean = sb("mean", [P, NT, B])
        self.centred = sb("centred", [P, NT, B, C])
        self.square = sb("square", [P, NT, B, C])
        self.rstd = sb("rstd", [P, NT, B])
        sem = lambda n: ctx.enter_context(nc.semaphore(f"{name}_{n}"))
        self.s_dve, self.s_c, self.s_sq, self.s_var, self.s_sd = map(sem, ("dve", "centred", "squared", "var", "dev"))

    def wide(self, a, part):
        n = NT // self.PARTS * B
        v = a[:, :, :].rearrange("p t b -> p (t b)")[:, part * n:(part + 1) * n]
        return v.rearrange("p (n c) -> p n c", c=1).broadcast_to([P, n, C])

    def rows(self, a, part):
        n = NT // self.PARTS * B
        return a[:, :, :, :].rearrange("p t b c -> p (t b) c")[:, part * n:(part + 1) * n]

    def run(self, src, turn):
        PT, n = self.PARTS, NT // self.PARTS * B
        small = lambda a, k: a[:, :, :].rearrange("p t b -> p (t b)")[:, k * n:(k + 1) * n]
        with self.nc.Block() as block:
            @block.vector
            def _(dve):
                step = Steps(dve, self.s_dve)
                step.enter(turn, 4 * PT)
                for k in range(PT):
                    step.tick(dve.tensor_reduce(small(self.mean, k), self.rows(src, k), AX.X, ALU.add))
                step.hold()
                for k in range(PT):
                    step.tick(dve.tensor_scalar(small(self.mean, k), small(self.mean, k), 1.0 / C, None, ALU.mult))
                step.hold()
                for k in range(PT):
                    dve.tensor_tensor(self.rows(self.centred, k), self.rows(src, k), self.wide(self.mean, k),
                                      ALU.subtract).then_inc(self.s_c, 1)
                for k in range(PT):
                    dve.wait_ge(self.s_sq, PT * turn + k + 1)
                    step.tick(dve.tensor_reduce(small(self.rstd, k), self.rows(self.square, k), AX.X, ALU.add))
                step.hold()
                for k in range(PT):
                    dve.tensor_scalar(small(self.rstd, k), small(self.rstd, k), 1.0 / C, self.EPS, ALU.mult,
                                      ALU.add).then_inc(self.s_var, 1)
                for k in range(PT):
                    dve.wait_ge(self.s_sd, PT * turn + k + 1)
                    step.tick(dve.reciprocal(small(self.rstd, k), small(self.rstd, k)))
                step.leave(1)

            @block.scalar
            def _(act):
                for k in range(PT):
                    act.wait_ge(self.s_c, PT * turn + k + 1)
                    act.activation(self.rows(self.square, k), self.rows(self.centred, k), ACT.Square).then_inc(self.s_sq, 1)
                for k in range(PT):
                    act.wait_ge(self.s_var, PT * turn + k + 1)
                    act.activation(small(self.rstd, k), small(self.rstd, k), ACT.Sqrt).then_inc(self.s_sd, 1)



class Layer:

    HP = NH // 2
    V1 = HD + 1
    VP = 2 * HD + 1
    ITERS = 6
    U = 3

    def __init__(self, nc, ctx, ps, hh, weights, cols):
        self.nc, self.ctx, self.ps, self.hh = nc, ctx, ps, hh
        self.W = lambda n: cols.view(weights, n)
        self.y = self.sb("y", [P, NT, B, C])
        self.sems = {}

    def sb(self, n, s, ctx=None):
        return (ctx or self.ctx).enter_context(self.nc.sbuf_tensor(n, s, F32))

    def sem(self, name):
        if name not in self.sems:
            self.sems[name] = self.ctx.enter_context(self.nc.semaphore(name))
        return self.sems[name]


def chunk_of(t, i, u):
    return t[:, :, :, :].rearrange("p (i u t) b c -> p i u t b c", u=Layer.U, t=TPC)[:, i, u]


def cols_of(t, i, u):
    return t[:, :].rearrange("p (i u n) -> p i u n", u=Layer.U, n=CHUNK)[:, i, u]


def normed(eng, norm, out, i, u):
    r = norm.rstd[:, :, :].rearrange("p (i u t) (b c) -> p i u t b c", u=Layer.U, t=TPC, c=1)[:, i, u]
    return eng.tensor_tensor(out, chunk_of(norm.centred, i, u), r.broadcast_to([P, TPC, B, C]), ALU.mult)


def first_norm(nc, ctx, norm, y, turn):
    s_y = ctx.enter_context(nc.semaphore("y_ready"))
    with nc.Block() as block:
        @block.vector
        def _(dve):
            with dve.Fori(0, NCH // Layer.U) as i:
                for u in range(Layer.U):
                    normed(dve, norm, chunk_of(y, i, u), i, u).then_inc(s_y, 1)
            dve.wait_ge(s_y, NCH)


def project_values(L, turn, norm, xnT, V, V_padded):
    nc, ps, W, U = L.nc, L.ps, L.W, L.U
    sem = L.sem
    s_n, s_nu, s_t, s_xT, s_xu, s_v, s_vc = (sem("norm1_" + n) for n in (
        "ready", "used", "transposed", "xT_ready", "xT_copied", "values", "values_copied"))
    at = lambda i, u: NCH * turn + U * i + u
    credit = lambda i, u: (NCH + U) * turn + U * i + u + 1
    with ExitStack() as stage:
        xn = L.sb("xn", [P, U, TPC, B, C], stage)
        xs = L.sb("xs", [P, U, CHUNK], stage)
        with nc.Block() as block:
            @block.vector
            def _(dve):
                for pad in (0, NT + 1):
                    dve.memset(V_padded[:, pad], 0.0)
                dve.memset(V[:, :, :, :, 2 * HD:], 1.0)
                with dve.Fori(0, NCH // U) as i:
                    for u in range(U):
                        dve.wait_ge(s_nu, credit(i, u))
                        normed(dve, norm, xn[:, u], i, u).then_inc(s_n, 1)
                    for u in range(U):
                        dve.wait_ge(s_v, at(i, u) + 1)
                        out = V[:, :, :, :, 0:2 * HD].rearrange("p (i u t) b n e -> p i u (t b n) e", u=U, t=TPC)[:, i, u]
                        dve.tensor_copy(out, ps[:, U + u, :].rearrange("p (n e) -> p n e", e=2 * HD)).then_inc(s_vc, 1)

            @block.tensor
            def _(pe):
                pe.sem_inc(s_nu, U)
                with pe.Fori(0, NCH // U) as i:
                    for u in range(U):
                        pe.wait_ge(s_n, at(i, u) + 1)
                        for t in range(TPC):
                            ins = pe.transpose(ps[:, u, t * P:(t + 1) * P],
                                               xn[:, u, t].rearrange("p b c -> p (b c)"), W("ident"))
                        ins.then_inc(s_t, 1)
                    for u in range(U):
                        pe.wait_ge(s_t, at(i, u) + 1)
                        pe.sem_inc(s_nu, 1)
                        pe.wait_ge(s_xT, at(i, u) + 1)
                        for t in range(TPC):
                            ins = pe.matmul(ps[:, U + u, t * P:(t + 1) * P], xs[:, u, t * P:(t + 1) * P], W("wv"),
                                            start=True, stop=True)
                        ins.then_inc(s_v, 1)
                    pe.wait_ge(s_vc, at(i, 0) + U)

            @block.scalar
            def _(act):
                with act.Fori(0, NCH // U) as i:
                    for u in range(U):
                        act.wait_ge(s_t, at(i, u) + 1)
                        act.wait_ge(s_xu, (NCH + U) * turn + U * i + u + 1)
                        act.activation(xs[:, u], ps[:, u, :], ACT.Identity, bias=W("ln1_b"),
                                       scale=W("ln1_g")).then_inc(s_xT, 1)

            @block.gpsimd
            def _(pool):
                pool.sem_inc(s_xu, U)
                with pool.Fori(0, NCH // U) as i:
                    for u in range(U):
                        pool.wait_ge(s_xT, at(i, u) + 1)
                        pool.wait_ge(s_v, at(i, u) + 1)
                        pool.tensor_copy(cols_of(xnT, i, u), xs[:, u]).then_inc(s_xu, 1)


def landmarks(L, turn, xnT, ql_diag, kl_diag, X, XT, Z, ZT):
    nc, ps, W, sem = L.nc, L.ps, L.W, L.sem
    G = B * NH
    SCALE = float(HD) ** -0.5
    s_s, s_pr, s_b, s_at, s_e, s_tr, s_tc, s_mx, s_ar, s_m2 = (sem("lm_" + n) for n in (
        "dve", "projected", "diag", "scores", "exp", "transposed", "copied", "max", "all_max", "inputs"))
    with ExitStack() as stage:
        xl = L.sb("xl", [P, M], stage)
        ql = L.sb("ql", [C, B, M], stage)
        kl = L.sb("kl", [C, B, M], stage)
        kd = L.sb("kl_unscaled", [C, B, NH, M], stage)
        mx = L.sb("lm_max", [M, G], stage)
        sm = L.sb("lm_sum", [M, 2, G], stage)
        am = L.sb("lm_peak", [M, 2], stage)
        ar = L.sb("lm_peak_all", [M, 2], stage)
        inv = L.sb("lm_inv", [M, 1], stage)
        with nc.Block() as block:
            @block.vector
            def _(dve):
                st = Steps(dve, s_s)
                st.enter(turn, 21)
                st.tick(dve.tensor_reduce(xl[:], xnT[:, :].rearrange("p (m l) -> p m l", l=GROUP), AX.X, ALU.add))
                st.hold()
                dve.tensor_scalar(xl[:], xl[:], 1.0 / GROUP, None, ALU.mult).then_inc(s_m2, 1)
                dve.wait_ge(s_pr, turn + 1)
                q = ps[0:C, 0, 0:B * M].rearrange("p (b m) -> p b m", b=B)
                k = ps[0:C, 1, 0:B * M].rearrange("p (b m) -> p b m", b=B)
                st.tick(dve.tensor_scalar(ql[:], q, SCALE, None, ALU.mult))
                st.tick(dve.tensor_copy(kl[:], k))
                st.hold()
                heads = W("head_of")[0:C].rearrange("p (h n) -> p h n", n=1).broadcast_to([C, NH, M])
                for b in range(B):
                    over = lambda a: a[:, b].rearrange("p (h m) -> p h m", h=1).broadcast_to([C, NH, M])
                    st.tick(dve.tensor_tensor(ql_diag[:, b], over(ql), heads, ALU.mult))
                    st.tick(dve.tensor_tensor(kd[:, b], over(kl), heads, ALU.mult))
                st.hold()
                dve.tensor_scalar(kl_diag[:], kd[:], SCALE, None, ALU.mult).then_inc(s_b, 1)
                dve.wait_ge(s_b, turn + 1)
                dve.wait_ge(s_at, turn + 1)
                wide = lambda a: a.rearrange("p (g n) -> p g n", n=1).broadcast_to([M, NH, M])
                S = lambda b: ps[0:M, 2 + b, :].rearrange("p (g n) -> p g n", n=M)
                half = lambda b: slice(b * NH, (b + 1) * NH)
                for b in range(B):
                    st.tick(dve.tensor_reduce(mx[:, half(b)], S(b), AX.X, ALU.max))
                st.hold()
                for b in range(B):
                    st.tick(dve.tensor_tensor(X[:, half(b)], S(b), wide(mx[:, half(b)]), ALU.subtract))
                dve.wait_ge(s_e, turn + 1)
                st.tick(dve.tensor_reduce(sm[:, 0], X[:], AX.X, ALU.add))
                st.hold()
                st.tick(dve.reciprocal(sm[:, 1], sm[:, 0]))
                st.hold()
                wide16 = lambda a: a.rearrange("p (g n) -> p g n", n=1).broadcast_to([M, G, M])
                dve.tensor_tensor(X[:], X[:], wide16(sm[:, 1]), ALU.mult).then_inc(s_mx, 1)
                dve.wait_ge(s_mx, turn * 2 + 1)
                st.tick(dve.tensor_reduce(sm[:, 0], X[:], AX.X, ALU.add, apply_absolute_value=True))
                dve.wait_ge(s_tr, turn + 1)
                for b in range(B):
                    st.tick(dve.tensor_copy(XT[:, half(b)], ps[0:M, 4 + b, :].rearrange("p (g n) -> p g n", n=M)))
                st.hold()
                st.tick(dve.tensor_reduce(sm[:, 1], XT[:], AX.X, ALU.add, apply_absolute_value=True))
                st.hold()
                dve.tensor_reduce(am[:], sm[:], AX.X, ALU.max).then_inc(s_mx, 1)
                dve.wait_ge(s_ar, turn + 1)
                st.tick(dve.tensor_tensor(inv[:], ar[:, 0:1], ar[:, 1:2], ALU.mult))
                st.hold()
                st.tick(dve.reciprocal(inv[:], inv[:]))
                st.hold()
                st.tick(dve.tensor_scalar(Z[:], XT[:], inv[:], None, ALU.mult))
                st.tick(dve.tensor_scalar(ZT[:], X[:], inv[:], None, ALU.mult))
                st.leave(1)

            @block.gpsimd
            def _(pool):
                wait_alone(pool, s_mx, 2 * turn + 2, L.sem("waits_passed"))
                pool.partition_all_reduce(ar[:], am[:], M, bass.bass_isa.ReduceOp.max).then_inc(s_ar, 1)

            @block.scalar
            def _(act):
                act.wait_ge(s_s, turn * 21 + 11)
                act.activation(X[:], X[:], ACT.Exp).then_inc(s_e, 1)

            @block.tensor
            def _(pe):
                pe.wait_ge(s_m2, turn + 1)
                for b in range(B):
                    pe.matmul(ps[0:C, 0, b * M:(b + 1) * M], W(f"wq{b}"), xl[:], start=True, stop=True)
                    ins = pe.matmul(ps[0:C, 1, b * M:(b + 1) * M], W(f"wk{b}"), xl[:], start=True, stop=True)
                ins.then_inc(s_pr, 1)
                wait_alone(pe, s_b, turn + 1, L.sem("waits_passed"))
                for b in range(B):
                    ins = pe.matmul(ps[0:M, 2 + b, :], ql[:, b], kd[:, b].rearrange("p h m -> p (h m)"),
                                    start=True, stop=True)
                ins.then_inc(s_at, 1)
                wait_alone(pe, s_mx, 2 * turn + 1, L.sem("waits_passed"))
                for g in range(G):
                    b, h = divmod(g, NH)
                    ins = pe.transpose(ps[0:M, 4 + b, h * M:(h + 1) * M], X[:, g], W("ident")[0:M, 0:M])
                ins.then_inc(s_tr, 1)


def pseudo_inverse(L, turn, X, XT, Z, ZT):
    nc, ps, W, sem = L.nc, L.ps, L.W, L.sem
    G = B * NH
    s_p = sem("pinv_product")
    s_c = sem("pinv_copied")
    with ExitStack() as stage:
        A = L.sb("XZ", [M, G, M], stage)
        T = L.sb("pinv_T", [M, 2, G, M], stage)
        eye = W("ident")[0:M, 0:M].rearrange("p (g n) -> p g n", g=1).broadcast_to([M, NH, M])
        at = lambda i, k: 4 * (L.ITERS * turn + i) + k
        half = lambda b: slice(b * NH, (b + 1) * NH)
        bank = lambda b: ps[0:M, b, :].rearrange("p (g n) -> p g n", n=M)
        with nc.Block() as block:
            @block.tensor
            def _(pe):
                with pe.Fori(0, L.ITERS) as i:
                    def product(k, lhsT, rhs, banks=0, last=True):
                        for g in range(G):
                            ins = pe.matmul(ps[0:M, banks + g // NH, g % NH * M:(g % NH + 1) * M], lhsT(g), rhs(g),
                                            start=True, stop=True)
                        if last:
                            ins.then_inc(s_p, 1)
                    wait_alone(pe, s_c, at(i, 0) + 1, L.sem("waits_passed"))
                    product(0, lambda g: XT[:, g], lambda g: Z[:, g])
                    wait_alone(pe, s_c, at(i, 1) + 1, L.sem("waits_passed"))
                    product(1, lambda g: A[:, g], lambda g: T[:, 0, g])
                    wait_alone(pe, s_c, at(i, 2) + 1, L.sem("waits_passed"))
                    product(2, lambda g: A[:, g], lambda g: T[:, 1, g])
                    wait_alone(pe, s_c, at(i, 3) + 1, L.sem("waits_passed"))
                    product(3, lambda g: ZT[:, g], lambda g: T[:, 0, g], last=False)
                    product(3, lambda g: T[:, 0, g], lambda g: ZT[:, g], banks=2)

            @block.vector
            def _(dve):
                with dve.Fori(0, L.ITERS) as i:
                    dve.wait_ge(s_p, at(i, 1))
                    for b in range(B):
                        dve.tensor_copy(A[:, half(b)], bank(b))
                    for k, (c, t) in enumerate(((7.0, 0), (15.0, 1), (13.0, 0))):
                        dve.wait_ge(s_p, at(i, k + 1))
                        for b in range(B):
                            ins = dve.scalar_tensor_tensor(T[:, t, half(b)], eye, c, bank(b), ALU.mult, ALU.subtract)
                        ins.then_inc(s_c, 1)
                    dve.wait_ge(s_p, at(i, 4))
                    for b in range(B):
                        dve.tensor_scalar(Z[:, half(b)], bank(b), 0.25, None, ALU.mult)
                    for b in range(B):
                        ins = dve.tensor_scalar(ZT[:, half(b)], bank(2 + b), 0.25, None, ALU.mult)
                    ins.then_inc(s_c, 1)


def landmark_values(L, turn, xnT, V, ql_diag, O):
    nc, ps, W, sem = L.nc, L.ps, L.W, L.sem
    HP, VP, G = L.HP, L.VP, B * L.HP
    s_kp, s_kc, s_s, s_cm, s_nm, s_e, s_al, s_t, s_tc, s_td, s_pv, s_o, s_i = (sem("lv_" + n) for n in (
        "k_projected", "k_copied", "scores", "chunk_max", "new_max", "exp", "alpha", "transposed", "copied_act",
        "copied_dve", "pv", "summed", "init"))
    with ExitStack() as stage:
        kT = L.sb("lv_kT", [C, B, CHUNK], stage)
        pr = L.sb("lv_probs", [P, B, HP, CHUNK], stage)
        prT = L.sb("lv_probsT", [P, B, HP, TPC, P], stage)
        cm = L.sb("lv_chunk_max", [P, B, HP], stage)
        mx = L.sb("lv_max", [P, B, HP], stage)
        neg = L.sb("lv_neg_max", [P, B, HP], stage)
        dl = L.sb("lv_delta", [P, B, HP], stage)
        al = L.sb("lv_alpha", [P, B, HP], stage)
        n = lambda c, b: B * (NCH * turn + c) + b
        with nc.Block() as block:
            @block.tensor
            def _(pe):
                with pe.Fori(0, NCH) as c:
                    for b in range(B):
                        wait_alone(pe, s_o, n(c, 0) + 1, L.sem("waits_passed"))
                        chunk = xnT[:, :].rearrange("p (c n) -> p c n", n=CHUNK)[:, c]
                        pe.matmul(ps[0:C, 4 * b, :], W(f"wk{b}"), chunk, start=True, stop=True).then_inc(s_kp, 1)
                    for b in range(B):
                        pe.wait_ge(s_kc, n(c, b) + 1)
                        for p in range(HP):
                            ins = pe.matmul(ps[:, 4 * b + p, :],
                                            ql_diag[:, b, 2 * p:2 * p + 2].rearrange("p h m -> p (h m)"),
                                            kT[:, b], start=True, stop=True)
                            ins.then_inc(s_s, 1)
                    for b in range(B):
                        for p in range(HP):
                            pe.wait_ge(s_e, HP * n(c, b) + p + 1)
                            for t in range(TPC):
                                ins = pe.transpose(ps[:, 4 * b + p, t * P:(t + 1) * P],
                                                   pr[:, b, p, t * P:(t + 1) * P], W("ident"))
                            ins.then_inc(s_t, 1)
                    for b in range(B):
                        pe.wait_ge(s_tc, HP // 2 * n(c, b) + HP // 2)
                        pe.wait_ge(s_td, HP // 2 * n(c, b) + HP // 2)
                        for p in range(HP):
                            for t in range(TPC):
                                vals = V[:, :, b, p, :].rearrange("p (c t) e -> p c t e", t=TPC)[:, c, t]
                                ins = pe.matmul(ps[:, 4 * b, p * VP:(p + 1) * VP], prT[:, b, p, t], vals,
                                                start=t == 0, stop=t == TPC - 1)
                        ins.then_inc(s_pv, 1)

            @block.vector
            def _(dve):
                dve.memset(mx[:], -1e30)
                dve.memset(O[:], 0.0).then_inc(s_i, 1)
                wait_alone(dve, s_i, (B * NCH + 1) * turn + 1, L.sem("waits_passed"))
                with dve.Fori(0, NCH) as c:
                    dve.wait_ge(s_nm, 3 * n(c, 0) + 1)
                    for b in range(B):
                        for p in range(HP):
                            dve.wait_ge(s_s, HP * n(c, b) + p + 1)
                            ins = dve.tensor_reduce(cm[:, b, p:p + 1], ps[:, 4 * b + p, :], AX.X, ALU.max)
                        ins.then_inc(s_cm, 1)
                        dve.wait_ge(s_cm, n(c, b) + 1)
                        dve.tensor_tensor(cm[:, b], cm[:, b], mx[:, b], ALU.max).then_inc(s_nm, 1)
                        dve.wait_ge(s_nm, 3 * n(c, b) + 2)
                        dve.tensor_tensor(dl[:, b], mx[:, b], cm[:, b], ALU.subtract)
                        dve.tensor_scalar(neg[:, b], cm[:, b], -1.0, None, ALU.mult).then_inc(s_nm, 1)
                        dve.wait_ge(s_nm, 3 * n(c, b) + 3)
                        dve.tensor_copy(mx[:, b], cm[:, b]).then_inc(s_nm, 1)
                    for b in range(B):
                        for p in range(HP):
                            dve.wait_ge(s_t, HP * n(c, b) + p + 1)
                            if p % 2:
                                dve.tensor_copy(prT[:, b, p], ps[:, 4 * b + p, :].rearrange(
                                    "p (t n) -> p t n", n=P)).then_inc(s_td, 1)
                    for b in range(B):
                        dve.wait_ge(s_al, n(c, b) + 1)
                        dve.wait_ge(s_o, n(c, 0) + 1)
                        alw = al[:, b].rearrange("p (h e) -> p h e", e=1).broadcast_to([P, HP, VP])
                        dve.tensor_tensor(O[:, b], O[:, b], alw, ALU.mult).then_inc(s_i, 1)
                    for b in range(B):
                        dve.wait_ge(s_pv, n(c, b) + 1)
                        dve.wait_ge(s_i, n(c, b) + turn + 2)
                        dve.tensor_tensor(O[:, b], O[:, b], ps[:, 4 * b, 0:HP * VP].rearrange(
                            "p (h e) -> p h e", e=VP), ALU.add).then_inc(s_o, 1)

            @block.scalar
            def _(act):
                with act.Fori(0, NCH) as c:
                    for b in range(B):
                        act.wait_ge(s_kp, n(c, b) + 1)
                        act.activation(kT[:, b], ps[0:C, 4 * b, :], ACT.Copy).then_inc(s_kc, 1)
                    for b in range(B):
                        act.wait_ge(s_nm, 3 * n(c, b) + 4)
                        for p in range(HP):
                            act.activation(pr[:, b, p], ps[:, 4 * b + p, :], ACT.Exp,
                                           bias=neg[:, b, p:p + 1]).then_inc(s_e, 1)
                        act.activation(al[:, b], dl[:, b], ACT.Exp).then_inc(s_al, 1)
                    for b in range(B):
                        for p in range(HP):
                            act.wait_ge(s_t, HP * n(c, b) + p + 1)
                            if p % 2 == 0:
                                act.activation(prT[:, b, p], ps[:, 4 * b + p, :].rearrange(
                                    "p (t n) -> p t n", n=P), ACT.Copy).then_inc(s_tc, 1)


def landmark_weights(L, turn, O, ZT, w_diag):
    nc, ps, W, sem = L.nc, L.ps, L.W, L.sem
    HP, V1, G = L.HP, L.V1, B * L.HP
    s_i, s_o, s_p, s_d = (sem("lw_" + n) for n in ("init", "o_ready", "product", "diag"))
    with ExitStack() as stage:
        inv = L.sb("lw_inv", [P, G], stage)
        On = L.sb("lw_o", [P, G, HD], stage)
        O0 = L.sb("lw_o0", [M, 2, G, HD], stage)
        with nc.Block() as block:
            @block.vector
            def _(dve):
                st = Steps(dve, s_i)
                st.enter(turn, 8)
                st.tick(dve.memset(w_diag[:], 0.0))
                O3 = O[:, :, :, :].rearrange("p b h e -> p (b h) e")
                st.tick(dve.reciprocal(inv[:], O3[:, :, 2 * HD]))
                st.hold()
                for q in range(2):
                    rows = slice(q * M, (q + 1) * M)
                    st.tick(dve.memset(w_diag[rows, :, :, q, HD:V1], 1.0))
                    wide = inv[rows].rearrange("p (g e) -> p g e", e=1).broadcast_to([M, G, HD])
                    st.tick(dve.tensor_tensor(On[rows], O3[rows, :, q * HD:(q + 1) * HD], wide, ALU.mult))
                st.hold()
                for q in range(2):
                    st.tick(dve.tensor_copy(O0[:, q], On[q * M:(q + 1) * M]))
                st.hold()
                st.leave(1)
                dve.wait_ge(s_p, turn + 1)
                for q in range(2):
                    ins = dve.tensor_copy(w_diag[q * M:(q + 1) * M, :, :, q, 0:HD].rearrange("p b h d -> p (b h) d"),
                                          ps[0:M, q, 0:G * HD].rearrange("p (g d) -> p g d", d=HD))
                ins.then_inc(s_d, 1)

            @block.tensor
            def _(pe):
                wait_alone(pe, s_i, 8 * turn + 8, L.sem("waits_passed"))
                for q in range(2):
                    for g in range(G):
                        b, p = divmod(g, HP)
                        ins = pe.matmul(ps[0:M, q, g * HD:(g + 1) * HD], ZT[:, b * NH + 2 * p + q], O0[:, q, g],
                                        start=True, stop=True)
                ins.then_inc(s_p, 1)


def value_convolution(L, turn, V, res):
    nc, ps, W, sem = L.nc, L.ps, L.W, L.sem
    s_c, s_cc = sem("conv_product"), sem("conv_copied")
    NU = NH * B
    near = W("band").rearrange("p (h n) -> p h n", h=NH)
    before = W("band_before").rearrange("p (h n) -> p h n", h=NH)
    after = W("band_after").rearrange("p (h n) -> p h n", h=NH)
    with nc.Block() as block:
        @block.tensor
        def _(pe):
            for n in range(NU):
                h, b = divmod(n, B)
                p, q = divmod(h, 2)
                vals = V[:, :, b, p, q * HD:(q + 1) * HD]
                if n >= 8:
                    pe.wait_ge(s_cc, NU * turn + n - 7)
                out = ps[:, n % 8, 0:NT * HD].rearrange("p (t d) -> p t d", d=HD)
                pe.matmul(out, near[:, h], vals[:, 1:NT + 1], start=True, stop=False)
                pe.matmul(out, before[:, h], vals[:, 0:NT], start=False, stop=False)
                pe.matmul(out, after[:, h], vals[:, 2:NT + 2], start=False, stop=True).then_inc(s_c, 1)

        def copy(eng, fn, parity):
            for n in range(NU):
                h, b = divmod(n, B)
                eng.wait_ge(s_c, NU * turn + n + 1)
                fn(res[:, :, b, h * HD:(h + 1) * HD], ps[:, n % 8, 0:NT * HD].rearrange(
                    "p (t d) -> p t d", d=HD)).then_inc(s_cc, 1)

        @block.vector
        def _(dve):
            copy(dve, dve.tensor_copy, 0)


def attend(L, turn, xnT, kl_diag, w_diag, res, y):
    nc, ps, W, sem = L.nc, L.ps, L.W, L.sem
    HP, V1 = L.HP, L.V1
    s_qp, s_qc, s_s, s_mx, s_sub, s_e, s_t, s_tc, s_pv, s_iv, s_a, s_ar, s_ot, s_otc, s_pr, s_y, s_b = (
        sem("at_" + n) for n in ("q_projected", "q_copied", "scores", "max", "sub", "exp", "transposed", "copied",
                                 "pv", "inverse", "normalised", "with_res", "outT", "outT_copied", "projected", "y",
                                 "bias_added"))
    H = TPC // 2
    with ExitStack() as stage:
        qT = L.sb("at_qT", [C, B, CHUNK], stage)
        sc = L.sb("at_scores", [P, 4, NH * M], stage)
        prT = L.sb("at_probsT", [P, 4, HP, P], stage)
        mx = L.sb("at_max", [P, 4, NH], stage)
        inv = L.sb("at_inv", [P, 2, B * NH], stage)
        o = L.sb("at_out", [P, 2, B, NH, HD], stage)
        oT = L.sb("at_outT", [P, 2, P], stage)
        n = lambda c, half, k: 4 * H * (NCH * turn + c) + 4 * half + k
        m = lambda c, half, t: 2 * H * (NCH * turn + c) + 2 * half + t
        with nc.Block() as block:
            @block.tensor
            def _(pe):
                with pe.Fori(0, NCH) as c:
                    chunk = xnT[:, :].rearrange("p (c n) -> p c n", n=CHUNK)[:, c]
                    for b in range(B):
                        pe.matmul(ps[0:C, b, :], W(f"wq{b}"), chunk, start=True, stop=True).then_inc(s_qp, 1)
                    for half in range(H):
                        pe.wait_ge(s_qc, B * (NCH * turn + c) + B)
                        for k in range(4):
                            t, b = divmod(k, B)
                            tok = (2 * half + t) * P
                            pe.matmul(ps[:, k, :], qT[:, b, tok:tok + P],
                                      kl_diag[:, b].rearrange("p h m -> p (h m)"), start=True, stop=True).then_inc(s_s, 1)
                        for k in range(4):
                            pe.wait_ge(s_e, n(c, half, k) + 1)
                            for p in range(HP):
                                ins = pe.transpose(ps[:, k, p * P:(p + 1) * P], sc[:, k, p * P:(p + 1) * P], W("ident"))
                            ins.then_inc(s_t, 1)
                        for k in range(4):
                            t, b = divmod(k, B)
                            pe.wait_ge(s_tc, n(c, half, k) + 1)
                            for p in range(HP):
                                ins = pe.matmul(ps[:, 4 + t, (b * HP + p) * 2 * V1:(b * HP + p + 1) * 2 * V1], prT[:, k, p],
                                                w_diag[:, b, p].rearrange("p q e -> p (q e)"), start=True, stop=True)
                            ins.then_inc(s_pv, 1)
                        for t in range(2):
                            pe.wait_ge(s_ar, m(c, half, t) + 1)
                            pe.transpose(ps[:, 6 + t, 0:P], o[:, t].rearrange("p b h d -> p (b h d)"),
                                         W("ident")).then_inc(s_ot, 1)
                        for t in range(2):
                            pe.wait_ge(s_otc, m(c, half, t) + 1)
                            pe.matmul(ps[:, 6 + t, 0:P], oT[:, t], W("w_out"), start=True, stop=True).then_inc(s_pr, 1)
                        pe.wait_ge(s_y, m(c, half, 0) + 2)

            @block.vector
            def _(dve):
                wait_alone(dve, s_b, NCH * turn + NCH, L.sem("waits_passed"))
                with dve.Fori(0, NCH) as c:
                    tile = lambda a, half, t: a[:, :, :, :].rearrange(
                        "p (c t) b e -> p c t b e", t=TPC)[:, c, 2 * half + t]
                    for half in range(H):
                        s3 = lambda k: ps[:, k, :].rearrange("p (h m) -> p h m", h=NH)
                        for k in range(4):
                            dve.wait_ge(s_s, n(c, half, k) + 1)
                            dve.tensor_reduce(mx[:, k], s3(k), AX.X, ALU.max).then_inc(s_mx, 1)
                        for k in range(4):
                            dve.wait_ge(s_mx, n(c, half, k) + 1)
                            wide = mx[:, k].rearrange("p (h m) -> p h m", m=1).broadcast_to([P, NH, M])
                            dve.tensor_tensor(sc[:, k].rearrange("p (h m) -> p h m", h=NH), s3(k), wide,
                                              ALU.subtract).then_inc(s_sub, 1)
                        pv = lambda t: ps[:, 4 + t, 0:B * NH * V1].rearrange("p (g e) -> p g e", e=V1)
                        for t in range(2):
                            dve.wait_ge(s_pv, n(c, half, 2 * t) + 2)
                            dve.reciprocal(inv[:, t], pv(t)[:, :, HD]).then_inc(s_iv, 1)
                        for t in range(2):
                            dve.wait_ge(s_iv, m(c, half, t) + 1)
                            wide = inv[:, t].rearrange("p (g e) -> p g e", e=1).broadcast_to([P, B * NH, HD])
                            dve.tensor_tensor(o[:, t].rearrange("p b h d -> p (b h) d"), pv(t)[:, :, 0:HD], wide,
                                              ALU.mult).then_inc(s_a, 1)
                        for t in range(2):
                            dve.wait_ge(s_a, m(c, half, t) + 1)
                            dve.tensor_tensor(o[:, t].rearrange("p b h d -> p b (h d)"),
                                              o[:, t].rearrange("p b h d -> p b (h d)"), tile(res, half, t),
                                              ALU.add).then_inc(s_ar, 1)
                        for t in range(2):
                            dve.wait_ge(s_pr, m(c, half, t) + 1)
                            dve.tensor_tensor(tile(y, half, t), tile(y, half, t), ps[:, 6 + t, 0:P].rearrange(
                                "p (b e) -> p b e", b=B), ALU.add).then_inc(s_y, 1)

            @block.gpsimd
            def _(pool):
                wide = W("b_out").rearrange("p (t b c) -> p t b c", t=1, b=1).broadcast_to([P, TPC, B, C])
                with pool.Fori(0, NCH) as c:
                    rows = y[:, :, :, :].rearrange("p (c t) b e -> p c t b e", t=TPC)[:, c]
                    pool.tensor_tensor(rows, rows, wide, ALU.add).then_inc(s_b, 1)

            @block.scalar
            def _(act):
                with act.Fori(0, NCH) as c:
                    for b in range(B):
                        act.wait_ge(s_qp, B * (NCH * turn + c) + b + 1)
                        act.activation(qT[:, b], ps[0:C, b, :], ACT.Copy).then_inc(s_qc, 1)
                    for half in range(H):
                        for k in range(4):
                            act.wait_ge(s_sub, n(c, half, k) + 1)
                            act.activation(sc[:, k], sc[:, k], ACT.Exp).then_inc(s_e, 1)
                        for k in range(4):
                            act.wait_ge(s_t, n(c, half, k) + 1)
                            act.activation(prT[:, k], ps[:, k, :].rearrange("p (h n) -> p h n", n=P),
                                           ACT.Copy).then_inc(s_tc, 1)
                        for t in range(2):
                            act.wait_ge(s_ot, m(c, half, t) + 1)
                            act.activation(oT[:, t], ps[:, 6 + t, 0:P], ACT.Copy).then_inc(s_otc, 1)


def feed_forward(L, turn, norm, y):
    nc, ps, W, sem, U = L.nc, L.ps, L.W, L.sem, L.U
    s_n, s_t, s_x, s_h, s_g, s_o, s_b, s_y = (sem("ff_" + n) for n in (
        "ready", "transposed", "xT_ready", "hidden", "gelu", "out", "bias_added", "y"))
    at = lambda i, u: NCH * turn + U * i + u
    with ExitStack() as stage:
        xn = L.sb("ff_xn", [P, U, TPC, B, C], stage)
        xs = L.sb("ff_xs", [P, U, CHUNK], stage)
        hd = L.sb("ff_hidden", [P, U, B, CHUNK], stage)
        with nc.Block() as block:
            @block.gpsimd
            def _(pool):
                wide = W("b2").rearrange("p (t b c) -> p t b c", t=1, b=1).broadcast_to([P, TPC, B, C])
                with pool.Fori(0, NCH // U) as i:
                    for u in range(U):
                        pool.tensor_tensor(chunk_of(y, i, u), chunk_of(y, i, u), wide, ALU.add).then_inc(s_b, 1)

            @block.vector
            def _(dve):
                with dve.Fori(0, NCH // U) as i:
                    for u in range(U):
                        normed(dve, norm, xn[:, u], i, u).then_inc(s_n, 1)
                    for u in range(U):
                        dve.wait_ge(s_o, at(i, u) + 1)
                        dve.wait_ge(s_b, at(i, u) + 1)
                        dve.tensor_tensor(chunk_of(y, i, u), chunk_of(y, i, u), ps[:, 6 + u % 2, :].rearrange(
                            "p (t b c) -> p t b c", t=TPC, b=B), ALU.add).then_inc(s_y, 1)

            @block.tensor
            def _(pe):
                with pe.Fori(0, NCH // U) as i:
                    for u in range(U):
                        pe.wait_ge(s_n, at(i, u) + 1)
                        for t in range(TPC):
                            ins = pe.transpose(ps[:, u, t * P:(t + 1) * P],
                                               xn[:, u, t].rearrange("p b c -> p (b c)"), W("ident"))
                        ins.then_inc(s_t, 1)
                    for u in range(U):
                        pe.wait_ge(s_x, at(i, u) + 1)
                        for b in range(B):
                            k = B * u + b
                            bank = (3, 4, 5)[k % 3]
                            if k >= 3:
                                pe.wait_ge(s_g, B * at(i, 0) + k - 2)
                            pe.matmul(ps[:, bank, :], W(f"w1_{b}"), xs[:, u], start=True, stop=True).then_inc(s_h, 1)
                    for u in range(U):
                        pe.wait_ge(s_g, B * at(i, u) + B)
                        if u == 2:
                            pe.wait_ge(s_y, at(i, 0) + 1)
                        for t in range(TPC):
                            for b in range(B):
                                ins = pe.matmul(ps[:, 6 + u % 2, (t * B + b) * C:(t * B + b + 1) * C],
                                                hd[:, u, b, t * P:(t + 1) * P], W("w2"), start=True, stop=True)
                        ins.then_inc(s_o, 1)
                    pe.wait_ge(s_y, at(i, 0) + U)

            @block.scalar
            def _(act):
                with act.Fori(0, NCH // U) as i:
                    for u in range(U):
                        act.wait_ge(s_t, at(i, u) + 1)
                        act.activation(xs[:, u], ps[:, u, :], ACT.Identity, bias=W("ln2_b"),
                                       scale=W("ln2_g")).then_inc(s_x, 1)
                    for u in range(U):
                        for b in range(B):
                            k = B * u + b
                            act.wait_ge(s_h, B * at(i, 0) + k + 1)
                            act.activation(hd[:, u, b], ps[:, (3, 4, 5)[k % 3], :], ACT.Gelu,
                                           bias=W("b1")).then_inc(s_g, 1)


def attention_layer(L, turn, norm):
    y, HP = L.y, L.HP
    with ExitStack() as stage:
        norm.run(y, 1 + 2 * turn)
        xnT = L.sb("xnT", [P, N_TOK], stage)
        V_padded = L.sb("V", [P, NT + 2, B, HP, L.VP], stage)
        V = V_padded[:, 1:NT + 1]
        w_diag = L.sb("w_diag", [P, B, HP, 2, L.V1], stage)
        kl_diag = L.sb("kl_diag", [C, B, NH, M], stage)
        res = L.sb("res", [P, NT, B, C], stage)
        project_values(L, turn, norm, xnT, V, V_padded)
        with ExitStack() as inner:
            X, XT, Z, ZT = (L.sb(n, [M, B * NH, M], inner) for n in ("X", "XT", "Z", "ZT"))
            ql_diag = L.sb("ql_diag", [C, B, NH, M], inner)
            O = L.sb("O", [P, B, HP, L.VP], inner)
            landmarks(L, turn, xnT, ql_diag, kl_diag, X, XT, Z, ZT)
            pseudo_inverse(L, turn, X, XT, Z, ZT)
            landmark_values(L, turn, xnT, V, ql_diag, O)
            landmark_weights(L, turn, O, ZT, w_diag)
        value_convolution(L, turn, V_padded, res)
        attend(L, turn, xnT, kl_diag, w_diag, res, y)
    norm.run(y, 2 + 2 * turn)
    feed_forward(L, turn, norm, y)



NE = 16
HID = 128
TOP = 2


def route(nc, ctx, ps, norm, xT, gate, W):
    U = Layer.U
    sem = lambda n: ctx.enter_context(nc.semaphore("route_" + n))
    s_n, s_nu, s_t, s_x, s_xu, s_l, s_lg = map(sem, ("ready", "used", "transposed", "xT_ready", "xT_copied",
                                                    "logits", "logits_copied"))
    s_d, s_e = sem("dve"), sem("exp")
    with ExitStack() as stage:
        sb = lambda n, s: stage.enter_context(nc.sbuf_tensor("rt_" + n, s, F32))
        xn = sb("xn", [P, U, TPC, B, C])
        xs = sb("xs", [P, U, CHUNK])
        prob = sb("prob", [P, NT * B, NE])
        rest = sb("rest", [P, NT * B, NE])
        cand = sb("cand", [P, NT * B, NE])
        small = sb("small", [P, 6, NT * B])
        g = gate[:, :, :, :].rearrange("p t b e -> p (t b) e")
        with nc.Block() as block:
            @block.vector
            def _(dve):
                with dve.Fori(0, NCH // U) as i:
                    for u in range(U):
                        dve.wait_ge(s_nu, U * i + u + 1)
                        normed(dve, norm, xn[:, u], i, u).then_inc(s_n, 1)
                    for u in range(U):
                        dve.wait_ge(s_l, U * i + u + 1)
                        out = prob[:, :, :].rearrange("p (i u n) e -> p i u (n e)", u=U, n=TPC * B)[:, i, u]
                        dve.tensor_tensor(out.rearrange("p (t e) -> p t e", t=TPC),
                                          ps[:, U + u, 0:TPC * B * NE].rearrange("p (t e) -> p t e", t=TPC),
                                          W("gate_b").rearrange("p (t e) -> p t e", t=1).broadcast_to(
                                              [P, TPC, B * NE]), ALU.add).then_inc(s_lg, 1)
                dve.wait_ge(s_lg, NCH)
                st = Steps(dve, s_d)

                def do(ins):
                    st.tick(ins)
                    st.hold()
                wide = lambda k: small[:, k].rearrange("p (n e) -> p n e", e=1).broadcast_to([P, NT * B, NE])
                iota = W("expert_iota").rearrange("p (n e) -> p n e", n=1).broadcast_to([P, NT * B, NE])
                do(dve.tensor_reduce(small[:, 0], prob[:], AX.X, ALU.max))
                do(dve.tensor_tensor(prob[:], prob[:], wide(0), ALU.subtract))
                dve.wait_ge(s_e, 1)
                do(dve.tensor_reduce(small[:, 0], prob[:], AX.X, ALU.add))
                do(dve.reciprocal(small[:, 0], small[:, 0]))
                do(dve.tensor_tensor(prob[:], prob[:], wide(0), ALU.mult))
                for k, src in enumerate((prob, rest)):
                    do(dve.tensor_reduce(small[:, 1 + k], src[:], AX.X, ALU.max))
                    do(dve.tensor_tensor(cand[:], src[:], wide(1 + k), ALU.is_equal))
                    do(dve.scalar_tensor_tensor(cand[:], cand[:], -64.0, iota, ALU.mult, ALU.add))
                    do(dve.tensor_reduce(small[:, 3], cand[:], AX.X, ALU.min))
                    do(dve.tensor_tensor(cand[:], cand[:], wide(3), ALU.is_equal))
                    if k == 0:
                        do(dve.scalar_tensor_tensor(rest[:], cand[:], -2.0, prob[:], ALU.mult, ALU.add))
                        do(dve.tensor_tensor(g, cand[:], wide(1), ALU.mult))
                    else:
                        do(dve.tensor_tensor(cand[:], cand[:], wide(2), ALU.mult))
                do(dve.tensor_tensor(small[:, 4], small[:, 1], small[:, 2], ALU.add))
                do(dve.reciprocal(small[:, 4], small[:, 4]))
                do(dve.tensor_tensor(g, g, cand[:], ALU.add))
                do(dve.tensor_tensor(g, g, wide(4), ALU.mult))

            @block.tensor
            def _(pe):
                pe.sem_inc(s_nu, U)
                with pe.Fori(0, NCH // U) as i:
                    for u in range(U):
                        pe.wait_ge(s_n, U * i + u + 1)
                        for t in range(TPC):
                            ins = pe.transpose(ps[:, u, t * P:(t + 1) * P],
                                               xn[:, u, t].rearrange("p b c -> p (b c)"), W("ident"))
                        ins.then_inc(s_t, 1)
                    for u in range(U):
                        pe.wait_ge(s_t, U * i + u + 1)
                        pe.sem_inc(s_nu, 1)
                        pe.wait_ge(s_x, U * i + u + 1)
                        for t in range(TPC):
                            ins = pe.matmul(ps[:, U + u, t * B * NE:(t + 1) * B * NE], xs[:, u, t * P:(t + 1) * P],
                                            W("gate_w"), start=True, stop=True)
                        ins.then_inc(s_l, 1)
                    pe.wait_ge(s_lg, U * i + U)

            @block.scalar
            def _(act):
                with act.Fori(0, NCH // U) as i:
                    for u in range(U):
                        act.wait_ge(s_t, U * i + u + 1)
                        act.wait_ge(s_xu, U * i + u + 1)
                        act.activation(xs[:, u], ps[:, u, :], ACT.Copy).then_inc(s_x, 1)
                act.wait_ge(s_d, 2)
                act.activation(prob[:], prob[:], ACT.Exp).then_inc(s_e, 1)

            @block.gpsimd
            def _(pool):
                pool.sem_inc(s_xu, U)
                with pool.Fori(0, NCH // U) as i:
                    for u in range(U):
                        pool.wait_ge(s_x, U * i + u + 1)
                        pool.wait_ge(s_l, U * i + u + 1)
                        pool.tensor_copy(cols_of(xT, i, u), xs[:, u]).then_inc(s_xu, 1)


def experts(nc, ctx, ps, xT, gate, w1, w2, w3, hh):
    sem = lambda n: ctx.enter_context(nc.semaphore("moe_" + n))
    s_w = [sem("weights_0"), sem("weights_1")]
    s_h1, s_h2, s_sl, s_hd, s_z, s_g, s_gu, s_acc, s_zero = map(sem, (
        "h1", "h2", "silu", "hidden", "out", "gated", "out_used", "summed", "cleared"))
    sb = lambda n, s: ctx.enter_context(nc.sbuf_tensor("moe_" + n, s, F32))
    up = sb("up", [P, 2, 2, B, HID])
    down = sb("down", [P, 2, C])
    silu = sb("silu", [P, B, CHUNK])
    hid = sb("hidden", [P, B, CHUNK])
    gated = sb("gated", [P, B, TPC, C])
    unit = lambda e, c, b: B * NCH * e + B * c + b
    NDMA = 2 * B + 1
    with nc.Block() as block:
        @block.sync
        def _(sp):
            def fetch(e, s):
                for b in range(B):
                    for n, w in enumerate((w1, w2)):
                        sp.dma_start(up[b * C:(b + 1) * C, s, n, b, :], w[e]).then_inc(s_w[s], 16)
                sp.dma_start(down[:, s, :], w3[e]).then_inc(s_w[s], 16)
            sp.wait_ge(s_zero, 1)
            for s in range(2):
                fetch(s, s)
            pairs = [w.rearrange("(i s) c h -> i s c h", s=2) for w in (w1, w2, w3)]
            with sp.Fori(1, NE // 2) as i:
                for s in range(2):
                    sp.wait_ge(s_z, unit(2 * i + s, 0, 0) - B * NCH)
                    for b in range(B):
                        for n in range(2):
                            sp.dma_start(up[b * C:(b + 1) * C, s, n, b, :], pairs[n][i, s]).then_inc(s_w[s], 16)
                    sp.dma_start(down[:, s, :], pairs[2][i, s]).then_inc(s_w[s], 16)

        @block.tensor
        def _(pe):
            def hidden(s, c, b):
                chunk = xT[:, :].rearrange("p (c n) -> p c n", n=CHUNK)[:, c]
                pe.matmul(ps[:, b, :], up[:, s, 0, b], chunk, start=True, stop=True).then_inc(s_h1, 1)
                pe.matmul(ps[:, 2 + b, :], up[:, s, 1, b], chunk, start=True, stop=True).then_inc(s_h2, 1)

            def output(e, s, c, b):
                pe.wait_ge(s_hd, unit(e, c, b) + 1)
                pe.wait_ge(s_gu, unit(e, c, b) + 1)
                for t in range(TPC):
                    ins = pe.matmul(ps[:, 4 + b, t * C:(t + 1) * C], hid[:, b, t * P:(t + 1) * P], down[:, s],
                                    start=True, stop=True)
                ins.then_inc(s_z, 1)
            with pe.Fori(0, NE // 2) as i:
                for s in range(2):
                    e = 2 * i + s
                    pe.wait_ge(s_w[s], 16 * NDMA * i + 16 * NDMA)
                    hidden(s, 0, 0)
                    with pe.Fori(0, NCH - 1) as c:
                        hidden(s, c, 1)
                        output(e, s, c, 0)
                        hidden(s, c + 1, 0)
                        output(e, s, c, 1)
                    hidden(s, NCH - 1, 1)
                    output(e, s, NCH - 1, 0)
                    output(e, s, NCH - 1, 1)

        @block.scalar
        def _(act):
            with act.Fori(0, NE) as e:
                with act.Fori(0, NCH) as c:
                    for b in range(B):
                        act.wait_ge(s_h1, unit(e, c, b) + 1)
                        act.activation(silu[:, b], ps[:, b, :], ACT.Silu).then_inc(s_sl, 1)

        @block.vector
        def _(dve):
            dve.memset(up[:], 0.0).then_inc(s_zero, 1)
            dve.sem_inc(s_gu, 2)

            def multiply(e, c, b):
                dve.wait_ge(s_h2, unit(e, c, b) + 1)
                dve.wait_ge(s_sl, unit(e, c, b) + 1)
                dve.tensor_tensor(hid[:, b], ps[:, 2 + b, :], silu[:, b], ALU.mult).then_inc(s_hd, 1)

            def weigh(e, c, b):
                dve.wait_ge(s_z, unit(e, c, b) + 1)
                dve.wait_ge(s_acc, unit(e, c, b) + 1)
                gt = gate[:, :, :, :].rearrange("p (c t) b (e n) -> p e c b t n", t=TPC, n=1)[:, e, c, b]
                dve.tensor_tensor(gated[:, b], ps[:, 4 + b, 0:TPC * C].rearrange("p (t n) -> p t n", n=C),
                                  gt.broadcast_to([P, TPC, C]), ALU.mult).then_inc(s_gu, 1)
            with dve.Fori(0, NE) as e:
                multiply(e, 0, 0)
                with dve.Fori(0, NCH - 1) as c:
                    multiply(e, c, 1)
                    weigh(e, c, 0)
                    multiply(e, c + 1, 0)
                    weigh(e, c, 1)
                multiply(e, NCH - 1, 1)
                weigh(e, NCH - 1, 0)
                weigh(e, NCH - 1, 1)

        @block.gpsimd
        def _(pool):
            pool.sem_inc(s_acc, 2)
            with pool.Fori(0, NE) as e:
                with pool.Fori(0, NCH) as c:
                    for b in range(B):
                        pool.wait_ge(s_gu, unit(e, c, b) + 3)
                        pool.wait_ge(s_acc, unit(e, c, b) + 2)
                        rows = hh[:, :, :, :].rearrange("p (c t) b n -> p c b t n", t=TPC)[:, c, b]
                        pool.tensor_tensor(rows, rows, gated[:, b], ALU.add).then_inc(s_acc, 1)
            pool.wait_ge(s_acc, unit(NE, 0, 0) + 2)


def moe_columns(i):
    c = Columns()
    c.add("ident", (0, P), np.eye(P, dtype=np.float32))
    c.add("gate_w", (0, P), both(i["L0_ffn_gate_w"]))
    c.add("gate_b", (0, P), np.tile(i["L0_ffn_gate_b"], (P, B)))
    c.add("expert_iota", (0, P), np.tile(np.arange(NE, dtype=np.float32), (P, 1)))
    return c


def layer_columns(i, l):
    c = Columns()
    zero = np.zeros((C, C), np.float32)
    w = i["L0_attn_w_qkv"][l]
    rep = lambda a: np.tile(np.asarray(a).reshape(1, -1), (P, 1))
    twice = lambda a: np.tile(np.asarray(a).reshape(-1, 1), (B, 1))
    c.add("ident", (0, P), np.eye(P, dtype=np.float32))
    c.add("head_of", (0, P), np.tile(np.repeat(np.eye(NH, dtype=np.float32), HD, 0), (B, 1)))
    for b in range(B):
        one = lambda a: np.concatenate([a if k == b else np.zeros_like(a) for k in range(B)], 0)
        c.add(f"wq{b}", (0, P), one(w[:, 0:C]))
        c.add(f"wk{b}", (0, P), one(w[:, C:2 * C]))
        c.add(f"w1_{b}", (0, P), one(i["L0_attn_w1"][l]))
    c.add("wv", (0, P), both(w[:, 2 * C:]))
    c.add("w_out", (0, P), both(i["L0_attn_w_out"][l]))
    c.add("w2", (0, P), i["L0_attn_w2"][l])
    for n in ("ln1_g", "ln1_b", "ln2_g", "ln2_b"):
        c.add(n, (0, P), twice(i["L0_attn_" + n][l]))
    c.add("b1", (0, P), i["L0_attn_b1"][l][:, None])
    c.add("b_out", (0, P), rep(i["L0_attn_b_out"][l]))
    c.add("b2", (0, P), rep(i["L0_attn_b2"][l]))
    taps = i["L0_attn_res_w"][l][:, 0, :, 0]
    K = taps.shape[1]
    pad = K // 2
    line = np.zeros((NH, 3 * P), np.float32)
    line[:, P + P // 2 - pad:P + P // 2 - pad + K] = taps
    j, o = np.meshgrid(np.arange(P), np.arange(P), indexing="ij")
    banded = lambda shift: line[:, np.clip(j + shift - o + P + P // 2, 0, 3 * P - 1)]
    near, before, after = (banded(s).transpose(1, 0, 2) for s in (0, -P, P))
    for name, m in (("band", near), ("band_before", before), ("band_after", after)):
        c.add(name, (0, P), m.reshape(P, -1))
    return c


def build(nc, x, bytes_rep, positions_rep, w_img, w_txt, w_att, w_moe, w1, w2, w3, h_img, out, cols):
    with ExitStack() as ctx:
        ps = ctx.enter_context(nc.psum_tensor("ps", [P, 8, 512], F32))
        hh = ctx.enter_context(nc.sbuf_tensor("hh", [P, NT, B, C], F32))
        sem = lambda n: ctx.enter_context(nc.semaphore(n))
        s_w = sem("weights_loaded")
        s_h = sem("h_loaded")

        def load(stage, name, src, n):
            tile = stage.enter_context(nc.sbuf_tensor(name, list(src.shape), F32))
            with nc.Block() as block:
                @block.sync
                def _(sp):
                    sp.dma_start(tile[:], src).then_inc(s_w, 16)
                    sp.wait_ge(s_w, 16 * n)
            return tile

        with ExitStack() as stage:
            wt = load(stage, "weights_txt", w_txt, 1)
            text_field(nc, stage, ps, bytes_rep, positions_rep, wt, cols["txt"], hh)
        with ExitStack() as stage:
            wa = load(stage, "weights_img", w_img, 2)
            image_attention(nc, stage, ps, x, wa, cols["img"], h_img)
        with nc.Block() as block:
            @block.sync
            def _(sp):
                for b in range(B):
                    sp.dma_start(hh[:, 0:NT_IMG, b, :], h_img[b].rearrange("(t p) c -> p t c", p=P)).then_inc(s_h, 16)
                sp.wait_ge(s_h, 16 * B)
        norm = Norm(nc, ctx, "norm")
        norm.run(hh, 0)
        s_l = sem("layer_weights_loaded")
        with ExitStack() as stage:
            weights = stage.enter_context(nc.sbuf_tensor("weights_att", [P, cols["att"].width], F32))
            L = Layer(nc, stage, ps, hh, weights, cols["att"])
            first_norm(nc, stage, norm, L.y, 0)
            with nc.Block() as block:
                @block.gpsimd
                def _(pool):
                    for name in ("lv_summed", "lv_new_max", "pinv_copied"):
                        pool.sem_inc(L.sem(name), 1)
            with nc.Fori(0, 2) as turn:
                with nc.Block() as block:
                    @block.sync
                    def _(sp):
                        sp.dma_start(weights[:], w_att[turn]).then_inc(s_l, 16)
                        wait_alone(sp, s_l, 16 * turn + 16, L.sem("waits_passed"))
                attention_layer(L, turn, norm)
            s_r = sem("residual_added")
            with nc.Block() as block:
                @block.vector
                def _(dve):
                    dve.tensor_tensor(hh[:], hh[:], L.y[:], ALU.add).then_inc(s_r, 1)
                    dve.wait_ge(s_r, 1)
        norm.run(hh, 5)
        with ExitStack() as stage:
            wm = load(stage, "weights_moe", w_moe, 3)
            xT = stage.enter_context(nc.sbuf_tensor("moe_xT", [P, N_TOK], F32))
            gate = stage.enter_context(nc.sbuf_tensor("gate", [P, NT, B, NE], F32))
            route(nc, stage, ps, norm, xT, gate, lambda n: cols["moe"].view(wm, n))
            experts(nc, stage, ps, xT, gate, w1, w2, w3, hh)
        s_o = sem("out_stored")
        with nc.Block() as block:
            @block.sync
            def _(sp):
                for b in range(B):
                    sp.dma_start(out[b].rearrange("(t p) c -> p t c", p=P), hh[:, :, b, :]).then_inc(s_o, 16)
                sp.wait_ge(s_o, 16 * B)


def both(a):
    z = np.zeros_like(a)
    return np.block([[a, z], [z, a]])


def image_columns(i):
    c = Columns()
    w, bias = i["L0_tok_qkv_w"], i["L0_tok_qkv_b"]
    pair = np.arange(C) ^ 1
    wq, wk, wv = w[0:C], w[C:2 * C], w[2 * C:3 * C]
    bq, bk, bv = bias[0:C], bias[C:2 * C], bias[2 * C:3 * C]
    all_rows = (0, P)
    c.add("ident", all_rows, np.eye(P, dtype=np.float32))
    for name, m in (("wq", wq), ("wq_pair", wq[pair]), ("wk", wk), ("wk_pair", wk[pair]), ("wv", wv)):
        c.add(name, all_rows, both(m.T))
    c.add("bias", all_rows, np.stack([np.tile(m, B) for m in (bq, bq[pair], bk, bk[pair])], 1))
    c.add("bias_v", all_rows, np.tile(bv, (P, B)))
    c.add("wproj", all_rows, both(i["L0_tok_proj_w"].T))
    c.add("bias_proj", all_rows, np.tile(i["L0_tok_proj_b"], (P, 2)))
    half = HD // 2
    freq = (1.0 / 10000.0 ** (np.arange(0, half, 2, dtype=np.float32) / np.float32(half))).astype(np.float32)
    d = np.arange(C) % HD
    y, xx = np.divmod(np.arange(WIN * WIN), WIN)
    pos = np.where((d < half)[:, None], y[None], xx[None]).astype(np.float32)
    ang = pos * freq[(d % half) // 2][:, None]
    sign = np.where(d % 2 == 0, -1.0, 1.0).astype(np.float32)[:, None]
    c.add("cos", all_rows, np.tile(np.cos(ang), (B, 1)))
    c.add("sin", all_rows, np.tile(np.sin(ang) * sign, (B, 1)))
    c.add("batch_of", all_rows, np.repeat(np.eye(B, dtype=np.float32), C, 0))
    c.add("head_of", all_rows, np.tile(np.repeat(np.eye(NH, dtype=np.float32), HD, 0), (B, 1)))
    return c


def kernel(**inputs):
    import concourse.bacc as bacc
    from concourse.bass_utils import run_bass_kernel_spmd

    i = {k: np.asarray(v) for k, v in inputs.items()}
    layers = [layer_columns(i, l) for l in range(i["L0_attn_ln1_g"].shape[0])]
    cols = {"img": image_columns(i), "txt": text_columns(i), "att": layers[0], "moe": moe_columns(i)}
    arrays = {
        "x": i["x"],
        "bytes_rep": np.broadcast_to(i["x_txt"], (C, B, S_TXT)),
        "positions_rep": np.broadcast_to(i["fside_BS_continuous_positions"], (P, B, S_TXT)),
        "w_img": cols["img"].array(), "w_txt": cols["txt"].array(),
        "w_att": np.stack([c.array() for c in layers]), "w_moe": cols["moe"].array(),
        "w1": i["L0_ffn_w1"], "w2": i["L0_ffn_w2"], "w3": i["L0_ffn_w3"],
    }
    arrays = {n: np.ascontiguousarray(a) for n, a in arrays.items()}
    nc = bacc.Bacc("TRN2", target_bir_lowering=False, num_devices=1)
    args = {n: nc.dram_tensor(n, a.shape, mybir.dt.from_np(a.dtype), kind="ExternalInput").ap()
            for n, a in arrays.items()}
    h_img = nc.dram_tensor("h_img", (B, IMG * IMG, C), F32, kind="Internal").ap()
    out = nc.dram_tensor("out_0_dram", (B, N_TOK, C), F32, kind="ExternalOutput").ap()
    build(nc, **args, h_img=h_img, out=out, cols=cols)
    r = run_bass_kernel_spmd(nc, [arrays], core_ids=[0])
    return r.results[0]["out_0_dram"]
```

```python
from contextlib import ExitStack

import numpy as np

import concourse.bass as bass
from concourse import mybir

F32 = mybir.dt.float32
F16 = mybir.dt.float16
I32 = mybir.dt.int32
ALU = mybir.AluOpType
ACT = mybir.ActivationFunctionType
AX = mybir.AxisListType

P = 128
B = 2
C = 64
NH = 8
HD = C // NH
IMG = 64
WIN = 8
NT_IMG = IMG * IMG // P
S_TXT = 512
NT = NT_IMG + S_TXT // P
N_TOK = NT * P
M = 64
GROUP = N_TOK // M
CHUNK = 512
NCH = N_TOK // CHUNK
TPC = CHUNK // P
NS = 4
ROUND = 1.5 * 2.0 ** 23


def pipelined(eng, n, stages):
    deepest = max(lag for lag, _ in stages)
    turns = max(1, (deepest + 1) // 2)

    def peeled(h):
        for lag, emit in stages:
            if 0 <= h - lag < n:
                emit(*divmod(h - lag, 2))
    for h in range(2 * turns):
        peeled(h)
    with eng.Fori(0, n // 2 - turns) as i:
        for lane in range(2):
            for lag, emit in stages:
                back, k = divmod(lane - lag, 2)
                emit(i + turns + back, k)
    for h in range(n, n + deepest):
        peeled(h)


class Columns:

    def __init__(self):
        self.at, self.width, self.parts = {}, 0, []

    def add(self, name, rows, array):
        array = np.asarray(array)
        self.at[name] = (rows, self.width, array.shape[1])
        self.parts.append((rows, self.width, array))
        self.width += array.shape[1]

    def array(self):
        out = np.zeros((P, self.width), np.float32)
        for (r0, r1), at, a in self.parts:
            out[r0:r1, at:at + a.shape[1]] = a
        return out

    def view(self, tile, name):
        (r0, r1), at, w = self.at[name]
        return tile[r0:r1, at:at + w]


def wait_alone(eng, sem, value, passed):
    eng.wait_ge(sem, value)
    eng.sem_inc(passed, 1)


class Steps:

    def __init__(self, eng, sem):
        self.eng, self.sem, self.base, self.n = eng, sem, 0, 0

    def tick(self, ins):
        ins.then_inc(self.sem, 1)
        self.n += 1

    def hold(self):
        self.eng.wait_ge(self.sem, self.base + self.n)

    def enter(self, i, per):
        self.outer, self.per = (self.base, self.n), per
        self.base, self.n = self.base + self.n + i * per, 0

    def leave(self, turns):
        assert self.n == self.per, (self.n, self.per)
        base, n = self.outer
        self.base, self.n = base, n + turns * self.per



def image_attention(nc, ctx, ps, x, wa, cols, h_img, load_more):
    NROW = IMG // WIN
    NW = NROW * WIN
    SCALE = float(HD) ** -0.5
    HP = NH // 2
    sb = lambda n, s: ctx.enter_context(nc.sbuf_tensor(n, s, F32))
    sem = lambda n: ctx.enter_context(nc.semaphore(n))
    x_in = sb("x_in", [P, 2, TPC, B, C])
    xT = sb("xT", [P, NROW, CHUNK])
    qT = sb("qT", [P, NROW, CHUNK])
    kT = sb("kT", [P, NROW, CHUNK])
    rope_a = sb("rope_a", [P, 2, CHUNK])
    rope_b = sb("rope_b", [P, 2, CHUNK])
    W = lambda n: cols.view(wa, n)
    ident = W("ident")
    over_windows = lambda n: W(n).rearrange("p (w n) -> p w n", w=1).broadcast_to([P, WIN, WIN * WIN])

    s_x = [sem("x_loaded_0"), sem("x_loaded_1")]
    s_xu = sem("x_used")
    s_tr = sem("x_transposed")
    s_xT = sem("xT_ready")
    s_qk = sem("qk_projected")
    s_ra = sem("rope_terms_ready")
    s_rd = sem("rope_done")

    with nc.Block() as block:
        @block.sync
        def _(sp):
            with sp.Fori(0, NROW // 2) as i:
                for u in range(2):
                    sp.wait_ge(s_xu, 2 * i + u + 1)
                    for b in range(B):
                        rows = x[b].rearrange("(i u t y) x c -> i u (y x) t c", u=2, t=TPC, y=2)
                        sp.dma_start(x_in[:, u, :, b, :], rows[i, u]).then_inc(s_x[u], 16)

        @block.tensor
        def _(pe):
            pe.sem_inc(s_xu, 2)
            pe.sem_inc(s_ra, 4)
            with pe.Fori(0, NROW // 2) as i:
                for u in range(2):
                    pe.wait_ge(s_x[u], 32 * i + 32)
                    for t in range(TPC):
                        ins = pe.transpose(ps[:, 0, t * P:(t + 1) * P],
                                           x_in[:, u, t].rearrange("p b c -> p (b c)"), ident)
                    ins.then_inc(s_tr, 1)
                    pe.wait_ge(s_tr, 2 * i + u + 1)
                    pe.sem_inc(s_xu, 1)
                    pe.wait_ge(s_xT, 2 * i + u + 1)
                    pe.wait_ge(s_ra, 4 * (2 * i + u) + 4)
                    chunk = xT[:, :, :].rearrange("p (i u) n -> p i u n", u=2)[:, i, u]
                    for n, name in enumerate(("wq", "wq_pair", "wk", "wk_pair")):
                        pe.matmul(ps[:, 1 + n, :], W(name), chunk, start=True, stop=True).then_inc(s_qk, 1)

        @block.scalar
        def _(act):
            with act.Fori(0, NROW // 2) as i:
                for u in range(2):
                    act.wait_ge(s_tr, 2 * i + u + 1)
                    out = xT[:, :, :].rearrange("p (i u) (w y x) -> p i u y w x", u=2, y=WIN, x=WIN)[:, i, u]
                    for y in range(WIN):
                        ins = act.activation(out[:, y], ps[:, 0, y * IMG:(y + 1) * IMG].rearrange(
                            "p (w x) -> p w x", x=WIN), ACT.Copy)
                    ins.then_inc(s_xT, 1)

        @block.vector
        def _(dve):
            dve.sem_inc(s_rd, 1)
            with dve.Fori(0, NROW // 2) as i:
                for u in range(2):
                    for n in range(4):
                        dve.wait_ge(s_qk, 4 * (2 * i + u) + n + 1)
                        if n == 0:
                            dve.wait_ge(s_rd, 2 * i + u + 1)
                        out = (rope_a, rope_b)[n % 2][:, n // 2, :].rearrange("p (w n) -> p w n", w=WIN)
                        dve.scalar_tensor_tensor(
                            out=out, in0=ps[:, 1 + n, :].rearrange("p (w n) -> p w n", w=WIN),
                            scalar=W("bias")[:, n:n + 1], in1=over_windows(("cos", "sin")[n % 2]),
                            op0=ALU.add, op1=ALU.mult).then_inc(s_ra, 1)

        @block.gpsimd
        def _(pool):
            with pool.Fori(0, NROW // 2) as i:
                for u in range(2):
                    pool.wait_ge(s_ra, 4 * (2 * i + u) + 8)
                    for n, dst in enumerate((qT, kT)):
                        out = dst[:, :, :].rearrange("p (i u) n -> p i u n", u=2)[:, i, u]
                        ins = pool.tensor_tensor(out, rope_a[:, n], rope_b[:, n], ALU.add)
                    ins.then_inc(s_rd, 1)

    q_diag = sb("q_diag", [P, 4, B, C])
    k_diag = sb("k_diag", [P, 4, NH, C])
    x_twice = sb("x_twice", [P, 4, 2, C])
    scores = sb("scores", [P, 4, NH * C])
    probs = sb("probs", [P, 4, NH * C])
    probsT = sb("probsT", [P, 4, NH * C])
    V1 = HD + 1
    v_diag = sb("v_diag", [P, 4, HP, B, 2, V1])
    row_max = sb("row_max", [P, 4, NH])
    row_inv = sb("row_inv", [P, 2, 2, NH])
    att = sb("att", [P, 2, 2, NH, HD])
    attT = sb("attT", [P, 2, P])
    proj = sb("proj", [P, NROW, WIN, C])
    warm = sb("warm_exp", [P, 1])
    s_op = sem("window_operands")
    s_xt = sem("window_x_twice")
    s_opu = sem("window_operands_used")
    s_vu = sem("window_x_twice_used")
    s_s = sem("window_scores")
    s_v = sem("window_values")
    s_vd = sem("window_v_diag")
    s_mx = sem("window_max")
    s_sub = sem("window_sub")
    s_e = sem("window_exp")
    s_pt = sem("window_probsT")
    s_ptc = sem("window_probsT_copied")
    s_pv = sem("window_pv")
    s_iv = sem("window_inverse")
    s_at = sem("window_att")
    s_ot = sem("window_attT")
    s_otc = sem("window_attT_copied")
    s_pr = sem("window_projected")
    s_prc = sem("window_projected_copied")
    s_init = sem("window_init")
    s_out = sem("h_img_stored")
    turns = NW // 4
    pair = lambda i, lane: 2 * i + lane
    win = lambda i, lane, u: 4 * i + 2 * lane + u

    def window(t, i, lane, u):
        v = t[:, :, :].rearrange("p r (w n) -> p (r w) n", n=C).rearrange("p (i k) n -> p i k n", k=4)
        return v[:, i, 2 * lane + u].rearrange("p (a n) -> p a n", a=1)

    with nc.Block() as block:
        @block.gpsimd
        def _(pool):
            batches = W("batch_of").rearrange("p (b n) -> p b n", n=1).broadcast_to([P, B, C])
            heads = W("head_of").rearrange("p (h n) -> p h n", n=1).broadcast_to([P, NH, C])
            with pool.Fori(0, turns) as i:
                for lane in range(2):
                    for u in range(2):
                        k = 2 * lane + u
                        pool.wait_ge(s_opu, win(i, lane, u) + 1)
                        pool.tensor_tensor(q_diag[:, k], window(qT, i, lane, u).broadcast_to([P, B, C]), batches,
                                           ALU.mult)
                        pool.tensor_tensor(k_diag[:, k], window(kT, i, lane, u).broadcast_to([P, NH, C]), heads,
                                           ALU.mult).then_inc(s_op, 1)

        @block.tensor
        def _(pe):
            pe.sem_inc(s_opu, 4)
            pe.sem_inc(s_vu, 2)
            pe.sem_inc(s_prc, 2)
            pe.wait_ge(s_init, 2)

            def product(i, lane):
                for u in range(2):
                    k = 2 * lane + u
                    pe.wait_ge(s_op, win(i, lane, u) + 1)
                    pe.matmul(ps[:, k, :], q_diag[:, k].rearrange("p b n -> p (b n)"),
                              k_diag[:, k].rearrange("p h n -> p (h n)"), start=True, stop=True).then_inc(s_s, 1)

            def values(i, lane):
                pe.wait_ge(s_xt, win(i, lane, 0) + 2)
                for u in range(2):
                    ins = pe.matmul(ps[:, 4 + lane, u * P:(u + 1) * P],
                                    x_twice[:, 2 * lane + u].rearrange("p a n -> p (a n)"), W("wv"),
                                    start=True, stop=True)
                ins.then_inc(s_v, 1)

            def transposes(i, lane):
                for u in range(2):
                    k = 2 * lane + u
                    pe.wait_ge(s_e, win(i, lane, u) + 1)
                    for n in range(HP):
                        ins = pe.transpose(ps[:, k, n * P:(n + 1) * P], probs[:, k, n * P:(n + 1) * P], ident)
                    ins.then_inc(s_pt, 1)

            def outputs(i, lane):
                pe.wait_ge(s_vd, pair(i, lane) + 1)
                pe.wait_ge(s_prc, pair(i, lane) + 1)
                for u in range(2):
                    k = 2 * lane + u
                    pe.wait_ge(s_ptc, win(i, lane, u) + 1)
                    for n in range(HP):
                        ins = pe.matmul(ps[:, 6 + lane, (u * HP + n) * 4 * V1:(u * HP + n + 1) * 4 * V1],
                                        probsT[:, k, n * P:(n + 1) * P],
                                        v_diag[:, k, n].rearrange("p b h e -> p (b h e)"), start=True, stop=True)
                ins.then_inc(s_pv, 1)

            def turned(i, lane):
                pe.wait_ge(s_at, pair(i, lane) + 1)
                pe.transpose(ps[:, 6 + lane, 3 * P:4 * P], att[:, lane].rearrange("p u h d -> p (u h d)"),
                             ident).then_inc(s_ot, 1)

            def projected(i, lane):
                pe.wait_ge(s_otc, pair(i, lane) + 1)
                pe.matmul(ps[:, 6 + lane, 0:P], attT[:, lane], W("wproj"), start=True, stop=True).then_inc(s_pr, 1)
            pipelined(pe, 2 * turns, [(1, transposes), (0, product), (2, turned), (1, outputs), (0, values),
                                      (2, projected)])

        @block.vector
        def _(dve):
            dve.memset(v_diag[:], 0.0).then_inc(s_init, 1)
            dve.wait_ge(s_init, 1)
            for hp in range(2):
                ins = dve.memset(v_diag[hp * C:(hp + 1) * C, :, :, :, hp, HD:V1], 1.0)
            ins.then_inc(s_init, 1)
            dve.wait_ge(s_init, 2)
            bias_v = W("bias_v").rearrange("p (b n h d) -> p b n h d", b=B, n=HP, h=2)

            def softmax(i, lane):
                s3 = lambda k: ps[:, k, :].rearrange("p (h n) -> p h n", h=NH)
                for u in range(2):
                    dve.wait_ge(s_s, win(i, lane, u) + 1)
                    dve.sem_inc(s_opu, 1)
                    k = 2 * lane + u
                    dve.tensor_reduce(row_max[:, k], s3(k), AX.X, ALU.max).then_inc(s_mx, 1)
                for u in range(2):
                    dve.wait_ge(s_mx, win(i, lane, u) + 1)
                    k = 2 * lane + u
                    wide = row_max[:, k].rearrange("p (h n) -> p h n", n=1).broadcast_to([P, NH, C])
                    dve.tensor_tensor(scores[:, k].rearrange("p (h n) -> p h n", h=NH), s3(k), wide,
                                      ALU.subtract).then_inc(s_sub, 1)

            def values(i, lane):
                dve.wait_ge(s_v, pair(i, lane) + 1)
                dve.sem_inc(s_vu, 1)
                for u in range(2):
                    for hp in range(2):
                        rows = slice(hp * C, (hp + 1) * C)
                        src = ps[rows, 4 + lane, u * P:(u + 1) * P].rearrange("p (b n h d) -> p b n h d", b=B, n=HP, h=2)
                        ins = dve.tensor_tensor(
                            v_diag[rows, 2 * lane + u, :, :, hp, 0:HD].rearrange("p n b d -> p b n d"),
                            src[:, :, :, hp], bias_v[rows, :, :, hp], ALU.add)
                ins.then_inc(s_vd, 1)

            def normalise(i, lane):
                dve.wait_ge(s_pv, pair(i, lane) + 1)
                out = ps[:, 6 + lane, 0:2 * HP * 4 * V1].rearrange("p (n b h e) -> p n b h e", n=2 * HP, b=B, h=2)
                for b in range(B):
                    rows = slice(b * C, (b + 1) * C)
                    ins = dve.reciprocal(row_inv[rows, lane].rearrange("p u (n h) -> p (u n) h", h=2),
                                         out[rows, :, b, :, HD])
                ins.then_inc(s_iv, 1)
                dve.wait_ge(s_iv, pair(i, lane) + 1)
                for b in range(B):
                    rows = slice(b * C, (b + 1) * C)
                    inv = row_inv[rows, lane].rearrange("p u (n h e) -> p (u n) h e", h=2, e=1)
                    ins = dve.tensor_tensor(att[rows, lane].rearrange("p u (n h) d -> p (u n) h d", h=2),
                                            out[rows, :, b, :, 0:HD], inv.broadcast_to([C, 2 * HP, 2, HD]), ALU.mult)
                ins.then_inc(s_at, 1)

            def projected(i, lane):
                dve.wait_ge(s_pr, pair(i, lane) + 1)
                dst = proj[:, :, :, :].rearrange("p r w c -> p (r w c)").rearrange("p (i k n) -> p i k n", k=2, n=2 * C)
                dve.tensor_tensor(dst[:, i, lane], ps[:, 6 + lane, 0:P], W("bias_proj"), ALU.add).then_inc(s_prc, 1)
            pipelined(dve, 2 * turns, [(0, softmax), (1, normalise), (0, values), (2, projected)])

        @block.scalar
        def _(act):
            act.activation(warm[:], ident[:, 0:1], ACT.Exp)

            def twice(i, lane):
                for u in range(2):
                    k = 2 * lane + u
                    if u == 0:
                        act.wait_ge(s_vu, pair(i, lane) + 1)
                    act.activation(x_twice[:, k], window(xT, i, lane, u).broadcast_to([P, 2, C]),
                                   ACT.Copy).then_inc(s_xt, 1)

            def exponentials(i, lane):
                for u in range(2):
                    k = 2 * lane + u
                    act.wait_ge(s_sub, win(i, lane, u) + 1)
                    act.activation(probs[:, k], scores[:, k], ACT.Exp, scale=SCALE).then_inc(s_e, 1)

            def probabilities(i, lane):
                for u in range(2):
                    k = 2 * lane + u
                    act.wait_ge(s_pt, win(i, lane, u) + 1)
                    act.activation(probsT[:, k], ps[:, k, :], ACT.Copy).then_inc(s_ptc, 1)

            def turned(i, lane):
                act.wait_ge(s_ot, pair(i, lane) + 1)
                act.activation(attT[:, lane], ps[:, 6 + lane, 3 * P:4 * P], ACT.Copy).then_inc(s_otc, 1)
            pipelined(act, 2 * turns, [(1, probabilities), (0, twice), (2, turned), (0, exponentials)])

        @block.sync
        def _(sp):
            load_more(sp)
            with sp.Fori(0, NROW) as r:
                sp.wait_ge(s_prc, (r + 1) * (WIN // 2) + 2)
                for b in range(B):
                    dst = h_img[b].rearrange("(r y w x) c -> r y x w c", r=NROW, y=WIN, w=WIN)
                    for y in range(WIN):
                        p0 = b * C + y * WIN
                        sp.dma_start(dst[r, y], proj[p0:p0 + WIN, r]).then_inc(s_out, 16)
            sp.wait_ge(s_out, 16 * B * WIN * NROW)



def text_field(nc, ctx, ps, bytes_rep, positions_rep, wt, cols, hh):
    TT = S_TXT // P
    TILES = B * TT
    E = C + 4
    TWO_PI = 6.283185
    K1, K2, K3 = 7, 5, 3
    sb = lambda n, s, d=F32: ctx.enter_context(nc.sbuf_tensor(n, s, d))
    sem = lambda n: ctx.enter_context(nc.semaphore(n))
    W = lambda n: cols.view(wt, n)
    byte = sb("byte", [C, B, S_TXT], I32)
    pos = sb("pos", [P, B, S_TXT])
    onehot = sb("onehot", [C, B, S_TXT + K1 - 1])
    conv1 = sb("conv1", [P, B, S_TXT + K2 - 1])
    conv2 = sb("conv2", [C, B, S_TXT + K3 - 1])
    ctxw = sb("context", [P, TILES])
    gath = sb("gathered", [P, TILES, E])
    amp_scale = sb("amp_scale", [P, TILES])
    center = sb("center", [P, TILES])
    phase = sb("phase", [P, TILES])
    inv_width = sb("inv_width", [P, NS, TILES])
    sw2 = sb("scale_weight_squared", [P, NS])
    z = sb("z", [P, 2, NS, S_TXT])
    assert TILES * C == S_TXT
    amps = z[:, 0].rearrange("p s (t c) -> p s t c", c=C)
    turns = sb("turns", [P, 2, NS, S_TXT])
    env = sb("envelope", [P, TT, B, NS, S_TXT])
    wave = sb("wave", [P, TT, B, NS, S_TXT])
    packet = turns

    s_in = sem("text_loaded")
    s_cl = sem("text_cleared")
    s_oh = sem("onehot_ready")
    s_c1 = sem("conv1_ready")
    s_g1 = sem("gelu1_ready")
    s_c2 = sem("conv2_ready")
    s_g2 = sem("gelu2_ready")
    s_c3 = sem("conv3_ready")
    s_ga = sem("gather_ready")
    s_gc = sem("gathered_copied")
    s_sg = sem("sigmoids_ready")
    s_sc = sem("text_scalars")
    s_z = sem("z_ready")
    s_a = sem("turns_shifted")
    s_d = sem("turns_ready")
    s_r = sem("wave_arg_ready")
    s_sq = sem("z_squared")
    s_ex = sem("envelope_ready")
    s_si = sem("sine_ready")
    s_pk = sem("packet_ready")
    s_pm = sem("packet_summed")
    s_h = sem("text_h_ready")
    tile = lambda st, b: b * TT + st

    with nc.Block() as block:
        @block.sync
        def _(sp):
            sp.dma_start(byte[:, :, :], bytes_rep).then_inc(s_in, 16)
            sp.dma_start(pos[:, :, :], positions_rep).then_inc(s_in, 16)

        @block.vector
        def _(dve):
            step = Steps(dve, s_sc)
            dve.memset(onehot[:], 0.0).then_inc(s_cl, 1)
            dve.memset(conv1[:], 0.0).then_inc(s_cl, 1)
            dve.memset(conv2[:], 0.0).then_inc(s_cl, 1)
            dve.wait_ge(s_in, 32)
            dve.wait_ge(s_cl, 3)
            dve.tensor_scalar(onehot[:, :, K1 // 2:K1 // 2 + S_TXT], byte[:], W("iota"), None,
                              ALU.is_equal).then_inc(s_oh, 1)
            for half in range(2):
                dve.wait_ge(s_ga, half + 1)
                n = TILES // 2
                dve.tensor_copy(gath[:, half * n:(half + 1) * n], ps[:, 2 + half, 0:n * E].rearrange(
                    "p (t e) -> p t e", e=E)).then_inc(s_gc, 1)
            dve.wait_ge(s_gc, 2)
            lp = lambda k: gath[:, :, C + k]
            step.tick(dve.scalar_tensor_tensor(center[:], lp(0), 0.05, W("byte_pos"), ALU.mult, ALU.add))
            step.tick(dve.tensor_scalar(phase[:], lp(3), 0.5, 0.25, ALU.mult, ALU.add))
            step.tick(dve.tensor_tensor(sw2[:], W("scale_weights"), W("scale_weights"), ALU.mult))
            step.tick(dve.scalar_tensor_tensor(inv_width[:, 0], lp(1), -1.0, lp(1), ALU.mult, ALU.max))
            step.hold()
            for s in reversed(range(NS)):
                step.tick(dve.tensor_scalar(inv_width[:, s], inv_width[:, 0], W("widths")[:, s:s + 1], 1e-5,
                                            ALU.mult, ALU.add))
            step.hold()
            step.tick(dve.reciprocal(inv_width[:], inv_width[:]))
            step.hold()
            for st in range(TT):
                for b in range(B):
                    t, n = tile(st, b), B * st + b
                    if n >= 2:
                        dve.wait_ge(s_sq, n - 1)
                        dve.wait_ge(s_r, n - 1)
                    for s in range(NS):
                        ins = dve.tensor_scalar(z[:, b, s], pos[:, b], center[:, t:t + 1], inv_width[:, s, t:t + 1],
                                                ALU.subtract, ALU.mult)
                    ins.then_inc(s_z, 1)
                    dve.wait_ge(s_z, n + 1)
                    dve.tensor_scalar(turns[:, b], z[:, b], phase[:, t:t + 1], None, ALU.add).then_inc(s_a, 1)
                    dve.wait_ge(s_a, n + 1)
                    dve.tensor_scalar(wave[:, st, b], turns[:, b], ROUND, ROUND, ALU.add,
                                      ALU.subtract).then_inc(s_d, 1)
                    dve.wait_ge(s_d, n + 1)
                    dve.tensor_tensor(wave[:, st, b], turns[:, b], wave[:, st, b], ALU.subtract).then_inc(s_r, 1)
            dve.wait_ge(s_sg, 2)
            step.tick(dve.tensor_tensor(amp_scale[:], amp_scale[:], ctxw[:], ALU.mult))
            step.hold()
            wide = amp_scale[:].rearrange("p (t c) -> p t c", c=1).broadcast_to([P, TILES, C])
            step.tick(dve.tensor_tensor(gath[:, :, 0:C], gath[:, :, 0:C], wide, ALU.mult))
            step.hold()
            dve.wait_ge(s_sq, TILES)
            dve.wait_ge(s_d, TILES)
            for s in range(NS):
                step.tick(dve.tensor_scalar(amps[:, s], gath[:, :, 0:C], sw2[:, s:s + 1], None, ALU.mult))
            for st in range(TT):
                for b in range(B):
                    n = B * st + b
                    dve.wait_ge(s_si, n + 1)
                    dve.wait_ge(s_ex, n + 1)
                    if n == 0:
                        dve.wait_ge(s_r, TILES)
                    if n >= 2:
                        dve.wait_ge(s_pm, n - 1)
                    dve.tensor_tensor(packet[:, b], env[:, st, b], wave[:, st, b], ALU.mult).then_inc(s_pk, 1)
            for b in range(B):
                dve.wait_ge(s_pm, TILES - 1 + b)
                for p in range(TT):
                    ins = dve.tensor_copy(hh[:, NT_IMG + p, b, :], ps[:, b * TT + p, 0:C])
            ins.then_inc(s_h, 1)

        @block.tensor
        def _(pe):
            pe.wait_ge(s_oh, 1)
            w1 = W("conv1").rearrange("i (k o) -> i k o", k=K1)
            for b in range(B):
                for k in range(K1):
                    ins = pe.matmul(ps[:, b, :], w1[:, k], onehot[:, b, k:k + S_TXT], start=k == 0, stop=k == K1 - 1)
                ins.then_inc(s_c1, 1)
            for t in range(TILES):
                b, st = divmod(t, TT)
                ins = pe.matmul(ps[:, 2 + b, st * E:(st + 1) * E], onehot[:, b, K1 // 2 + st * P:K1 // 2 + (st + 1) * P],
                                W("embed"), start=True, stop=True)
                if st == TT - 1:
                    ins.then_inc(s_ga, 1)
            w2 = W("conv2").rearrange("i (k o) -> i k o", k=K2)
            for b in range(B):
                pe.wait_ge(s_g1, b + 1)
                for k in range(K2):
                    ins = pe.matmul(ps[0:C, 4 + b, :], w2[:, k], conv1[:, b, k:k + S_TXT], start=k == 0, stop=k == K2 - 1)
                ins.then_inc(s_c2, 1)
            pe.wait_ge(s_g2, B)
            for t in range(TILES):
                b, st = divmod(t, TT)
                for k in range(K3):
                    ins = pe.matmul(ps[:, 6, t:t + 1], conv2[:, b, k + st * P:k + (st + 1) * P], W("conv3")[:, k:k + 1],
                                    start=k == 0, stop=k == K3 - 1)
            ins.then_inc(s_c3, 1)
            for st in range(TT):
                for b in range(B):
                    pe.wait_ge(s_pk, B * st + b + 1)
                    if st == 0 and b == 0:
                        pe.wait_ge(s_sg, 2)
                    for p in range(TT):
                        for s in range(NS):
                            ins = pe.matmul(ps[:, b * TT + p, 0:C], packet[:, b, s, p * P:(p + 1) * P],
                                            amps[:, s, tile(st, b)], start=st == 0 and s == 0,
                                            stop=st == TT - 1 and s == NS - 1)
                    ins.then_inc(s_pm, 1)

        @block.scalar
        def _(act):
            act.wait_ge(s_cl, 3)
            for b in range(B):
                act.wait_ge(s_c1, b + 1)
                act.activation(conv1[:, b, K2 // 2:K2 // 2 + S_TXT], ps[:, b, :], ACT.Gelu,
                               bias=W("bias1")).then_inc(s_g1, 1)
            for b in range(B):
                act.wait_ge(s_c2, b + 1)
                act.activation(conv2[:, b, K3 // 2:K3 // 2 + S_TXT], ps[0:C, 4 + b, :], ACT.Gelu,
                               bias=W("bias2")).then_inc(s_g2, 1)
            act.wait_ge(s_gc, 2)
            act.wait_ge(s_c3, 1)
            act.activation(ctxw[:], ps[:, 6, 0:TILES], ACT.Sigmoid, bias=W("bias3")).then_inc(s_sg, 1)
            act.activation(amp_scale[:], gath[:, :, C + 2], ACT.Sigmoid).then_inc(s_sg, 1)
            for st in range(TT):
                for b in range(B):
                    n = B * st + b
                    act.wait_ge(s_z, n + 1)
                    act.activation(env[:, st, b], z[:, b], ACT.Square).then_inc(s_sq, 1)
                    act.wait_ge(s_sq, n + 1)
                    act.activation(env[:, st, b], env[:, st, b], ACT.Exp, scale=-0.5).then_inc(s_ex, 1)
            for st in range(TT):
                for b in range(B):
                    act.wait_ge(s_r, B * st + b + 1)
                    act.activation(wave[:, st, b], wave[:, st, b], ACT.Sin, scale=TWO_PI).then_inc(s_si, 1)


def text_columns(i):
    c = Columns()
    rep = lambda a: np.tile(np.asarray(a).reshape(1, -1), (P, 1))
    c.add("conv1", (0, C), i["L0_txt_w1"].transpose(1, 2, 0).reshape(C, -1))
    c.add("conv2", (0, P), i["L0_txt_w2"].transpose(1, 2, 0).reshape(P, -1))
    c.add("conv3", (0, C), i["L0_txt_w3"][0])
    c.add("embed", (0, C), np.concatenate([i["L0_txt_emb"], i["L0_txt_locality_shapes"]], 1))
    c.add("bias1", (0, P), i["L0_txt_b1"][:, None])
    c.add("bias2", (0, C), i["L0_txt_b2"][:, None])
    c.add("bias3", (0, P), rep(i["L0_txt_b3"]))
    c.add("widths", (0, P), rep(i["L0_txt_multiscale_widths"]))
    c.add("scale_weights", (0, P), rep(i["L0_txt_scale_weights"]))
    c.add("iota", (0, C), np.arange(C, dtype=np.float32)[:, None])
    at = np.linspace(0.0, 1.0, S_TXT, dtype=np.float32).reshape(-1, P).T
    c.add("byte_pos", (0, P), np.tile(at, (1, B)))
    return c



class Norm:

    PARTS = 3
    EPS = 1e-5

    def __init__(self, nc, ctx, name):
        sb = lambda n, s: ctx.enter_context(nc.sbuf_tensor(f"{name}_{n}", s, F32))
        self.nc = nc
        self.names = iter(range(100))
        self.mean = sb("mean", [P, NT, B])
        self.centred = sb("centred", [P, NT, B, C])
        self.rstd = sb("rstd", [P, NT, B])
        sem = lambda n: ctx.enter_context(nc.semaphore(f"{name}_{n}"))
        self.s_dve, self.s_c, self.s_sq, self.s_var, self.s_sd = map(sem, ("dve", "centred", "squared", "var", "dev"))

    def wide(self, a, part):
        n = NT // self.PARTS * B
        v = a[:, :, :].rearrange("p t b -> p (t b)")[:, part * n:(part + 1) * n]
        return v.rearrange("p (n c) -> p n c", c=1).broadcast_to([P, n, C])

    def rows(self, a, part):
        n = NT // self.PARTS * B
        return a[:, :, :, :].rearrange("p t b c -> p (t b) c")[:, part * n:(part + 1) * n]

    def run(self, src, turn):
        PT, n = self.PARTS, NT // self.PARTS * B
        small = lambda a, k: a[:, :, :].rearrange("p t b -> p (t b)")[:, k * n:(k + 1) * n]
        with self.nc.sbuf_tensor(f"norm_square_{next(self.names)}", [P, NT, B, C], F32) as square, \
                self.nc.Block() as block:
            @block.vector
            def _(dve):
                step = Steps(dve, self.s_dve)
                step.enter(turn, 4 * PT)
                for k in range(PT):
                    step.tick(dve.tensor_reduce(small(self.mean, k), self.rows(src, k), AX.X, ALU.add))
                step.hold()
                for k in range(PT):
                    step.tick(dve.tensor_scalar(small(self.mean, k), small(self.mean, k), 1.0 / C, None, ALU.mult))
                step.hold()
                for k in range(PT):
                    dve.tensor_tensor(self.rows(self.centred, k), self.rows(src, k), self.wide(self.mean, k),
                                      ALU.subtract).then_inc(self.s_c, 1)
                for k in range(PT):
                    dve.wait_ge(self.s_sq, PT * turn + k + 1)
                    step.tick(dve.tensor_reduce(small(self.rstd, k), self.rows(square, k), AX.X, ALU.add))
                step.hold()
                for k in range(PT):
                    dve.tensor_scalar(small(self.rstd, k), small(self.rstd, k), 1.0 / C, self.EPS, ALU.mult,
                                      ALU.add).then_inc(self.s_var, 1)
                for k in range(PT):
                    dve.wait_ge(self.s_sd, PT * turn + k + 1)
                    step.tick(dve.reciprocal(small(self.rstd, k), small(self.rstd, k)))
                step.leave(1)

            @block.scalar
            def _(act):
                for k in range(PT):
                    act.wait_ge(self.s_c, PT * turn + k + 1)
                    act.activation(self.rows(square, k), self.rows(self.centred, k), ACT.Square).then_inc(self.s_sq, 1)
                for k in range(PT):
                    act.wait_ge(self.s_var, PT * turn + k + 1)
                    act.activation(small(self.rstd, k), small(self.rstd, k), ACT.Sqrt).then_inc(self.s_sd, 1)



class Layer:

    HP = NH // 2
    V1 = HD + 1
    VP = 2 * HD + 1
    ITERS = 6
    U = 3

    def __init__(self, nc, ctx, ps, hh, weights, cols):
        self.nc, self.ctx, self.ps, self.hh = nc, ctx, ps, hh
        self.W = lambda n: cols.view(weights, n)
        self.y = self.sb("y", [P, NT, B, C])
        self.sems = {}

    def sb(self, n, s, ctx=None):
        return (ctx or self.ctx).enter_context(self.nc.sbuf_tensor(n, s, F32))

    def sem(self, name):
        if name not in self.sems:
            self.sems[name] = self.ctx.enter_context(self.nc.semaphore(name))
        return self.sems[name]


def chunk_of(t, i, u):
    return t[:, :, :, :].rearrange("p (i u t) b c -> p i u t b c", u=Layer.U, t=TPC)[:, i, u]


def cols_of(t, i, u):
    return t[:, :].rearrange("p (i u n) -> p i u n", u=Layer.U, n=CHUNK)[:, i, u]


def normed(eng, norm, out, i, u):
    r = norm.rstd[:, :, :].rearrange("p (i u t) (b c) -> p i u t b c", u=Layer.U, t=TPC, c=1)[:, i, u]
    return eng.tensor_tensor(out, chunk_of(norm.centred, i, u), r.broadcast_to([P, TPC, B, C]), ALU.mult)


def first_norm(nc, ctx, norm, y, turn):
    s_y = ctx.enter_context(nc.semaphore("y_ready"))
    with nc.Block() as block:
        @block.vector
        def _(dve):
            with dve.Fori(0, NCH // Layer.U) as i:
                for u in range(Layer.U):
                    normed(dve, norm, chunk_of(y, i, u), i, u).then_inc(s_y, 1)
            dve.wait_ge(s_y, NCH)


def project_values(L, turn, norm, xnT, V, V_padded):
    nc, ps, W, U = L.nc, L.ps, L.W, L.U
    sem = L.sem
    s_n, s_nu, s_t, s_xT, s_xu, s_v, s_vc = (sem("norm1_" + n) for n in (
        "ready", "used", "transposed", "xT_ready", "xT_copied", "values", "values_copied"))
    at = lambda i, u: NCH * turn + U * i + u
    credit = lambda i, u: (NCH + U) * turn + U * i + u + 1
    with ExitStack() as stage:
        xn = L.sb("xn", [P, U, TPC, B, C], stage)
        xs = L.sb("xs", [P, U, CHUNK], stage)
        with nc.Block() as block:
            @block.vector
            def _(dve):
                for pad in (0, NT + 1):
                    dve.memset(V_padded[:, pad], 0.0)
                dve.memset(V[:, :, :, :, 2 * HD:], 1.0)
                with dve.Fori(0, NCH // U) as i:
                    for u in range(U):
                        dve.wait_ge(s_nu, credit(i, u))
                        normed(dve, norm, xn[:, u], i, u).then_inc(s_n, 1)
                    for u in range(U):
                        dve.wait_ge(s_v, at(i, u) + 1)
                        out = V[:, :, :, :, 0:2 * HD].rearrange("p (i u t) b n e -> p i u (t b n) e", u=U, t=TPC)[:, i, u]
                        dve.tensor_copy(out, ps[:, U + u, :].rearrange("p (n e) -> p n e", e=2 * HD)).then_inc(s_vc, 1)

            @block.tensor
            def _(pe):
                pe.sem_inc(s_nu, U)
                with pe.Fori(0, NCH // U) as i:
                    for u in range(U):
                        pe.wait_ge(s_n, at(i, u) + 1)
                        for t in range(TPC):
                            ins = pe.transpose(ps[:, u, t * P:(t + 1) * P],
                                               xn[:, u, t].rearrange("p b c -> p (b c)"), W("ident"))
                        ins.then_inc(s_t, 1)
                    for u in range(U):
                        pe.wait_ge(s_t, at(i, u) + 1)
                        pe.sem_inc(s_nu, 1)
                        pe.wait_ge(s_xT, at(i, u) + 1)
                        for t in range(TPC):
                            ins = pe.matmul(ps[:, U + u, t * P:(t + 1) * P], xs[:, u, t * P:(t + 1) * P], W("wv"),
                                            start=True, stop=True)
                        ins.then_inc(s_v, 1)
                    pe.wait_ge(s_vc, at(i, 0) + U)

            @block.scalar
            def _(act):
                with act.Fori(0, NCH // U) as i:
                    for u in range(U):
                        act.wait_ge(s_t, at(i, u) + 1)
                        act.wait_ge(s_xu, (NCH + U) * turn + U * i + u + 1)
                        act.activation(xs[:, u], ps[:, u, :], ACT.Identity, bias=W("ln1_b"),
                                       scale=W("ln1_g")).then_inc(s_xT, 1)

            @block.gpsimd
            def _(pool):
                pool.sem_inc(s_xu, U)
                with pool.Fori(0, NCH // U) as i:
                    for u in range(U):
                        pool.wait_ge(s_xT, at(i, u) + 1)
                        pool.wait_ge(s_v, at(i, u) + 1)
                        pool.tensor_copy(cols_of(xnT, i, u), xs[:, u]).then_inc(s_xu, 1)


def landmarks(L, turn, xnT, ql_diag, kl_diag, X_diag, XT_diag, Z, ZT, ZT_diag):
    nc, ps, W, sem = L.nc, L.ps, L.W, L.sem
    G = B * NH
    SCALE = float(HD) ** -0.5
    STEPS, BEFORE_EXP = 23, 9
    s_s, s_pr, s_b, s_at, s_e, s_tr, s_mx, s_ar, s_m2 = (sem("lm_" + n) for n in (
        "dve", "projected", "diag", "scores", "exp", "transposed", "max", "all_max", "inputs"))
    with ExitStack() as stage:
        xl = L.sb("xl", [P, M], stage)
        ql = L.sb("ql", [P, B, M], stage)
        kl = L.sb("kl", [P, M], stage)
        kd = L.sb("kl_unscaled", [P, B, NH, M], stage)
        X = L.sb("X", [P, NH, M], stage)
        mx = L.sb("lm_max", [P, NH], stage)
        sm = L.sb("lm_sum", [P, 2, NH], stage)
        am = L.sb("lm_peak", [P, 2], stage)
        ar = L.sb("lm_peak_all", [P, 2], stage)
        inv = L.sb("lm_inv", [P, 1], stage)
        rows = lambda b: slice(b * M, (b + 1) * M)
        with nc.Block() as block:
            @block.vector
            def _(dve):
                st = Steps(dve, s_s)
                st.enter(turn, STEPS)
                st.tick(dve.tensor_reduce(xl[:], xnT[:, :].rearrange("p (m l) -> p m l", l=GROUP), AX.X, ALU.add))
                st.hold()
                dve.tensor_scalar(xl[:], xl[:], 1.0 / GROUP, None, ALU.mult).then_inc(s_m2, 1)
                dve.wait_ge(s_pr, turn + 1)
                for b in range(B):
                    st.tick(dve.tensor_scalar(ql[:, b], ps[:, 0, 0:M], SCALE, None, ALU.mult))
                st.tick(dve.tensor_copy(kl[:], ps[:, 1, 0:M]))
                st.hold()
                units = W("unit_of").rearrange("p (g n) -> p g n", n=1).broadcast_to([P, G, M])
                over = lambda a: a.rearrange("p (g m) -> p g m", g=1).broadcast_to([P, G, M])
                every = lambda a: a.rearrange("p b h m -> p (b h) m")
                st.tick(dve.tensor_tensor(every(kd[:]), over(kl[:]), units, ALU.mult))
                st.hold()
                dve.tensor_scalar(kl_diag[:], kd[:], SCALE, None, ALU.mult).then_inc(s_b, 1)
                dve.wait_ge(s_b, turn + 1)
                dve.wait_ge(s_at, turn + 1)
                wide = lambda a: a.rearrange("p (g n) -> p g n", n=1).broadcast_to([a.shape[0], NH, M])
                S = lambda b: ps[rows(b), 2 + b, :].rearrange("p (g n) -> p g n", n=M)
                for b in range(B):
                    st.tick(dve.tensor_reduce(mx[rows(b)], S(b), AX.X, ALU.max))
                st.hold()
                for b in range(B):
                    st.tick(dve.tensor_tensor(X[rows(b)], S(b), wide(mx[rows(b)]), ALU.subtract))
                assert st.n == BEFORE_EXP
                st.tick(dve.tensor_tensor(every(ql_diag[:]), over(ql[:, 0]), units, ALU.mult))
                dve.wait_ge(s_e, turn + 1)
                st.tick(dve.tensor_reduce(sm[:, 0], X[:], AX.X, ALU.add))
                st.hold()
                st.tick(dve.reciprocal(sm[:, 1], sm[:, 0]))
                st.hold()
                st.tick(dve.tensor_tensor(X[:], X[:], wide(sm[:, 1]), ALU.mult))
                st.hold()
                both_x = X[:].rearrange("p h (n m) -> p h n m", n=1).broadcast_to([P, NH, B, M])
                batches = W("batch_of").rearrange("p (h b m) -> p h b m", h=1, m=1).broadcast_to([P, NH, B, M])
                dve.tensor_tensor(X_diag[:], both_x, batches, ALU.mult).then_inc(s_mx, 1)
                st.tick(dve.tensor_reduce(sm[:, 0], X[:], AX.X, ALU.add, apply_absolute_value=True))
                dve.wait_ge(s_tr, turn + 1)
                for k in range(2):
                    st.tick(dve.tensor_copy(XT_diag[:, 4 * k:4 * k + 4], ps[:, 4 + k, :].rearrange(
                        "p (h b m) -> p h b m", b=B, m=M)))
                st.hold()
                st.tick(dve.tensor_reduce(sm[:, 1], XT_diag[:].rearrange("p h b m -> p h (b m)"), AX.X, ALU.add,
                                          apply_absolute_value=True))
                st.hold()
                dve.tensor_reduce(am[:], sm[:], AX.X, ALU.max).then_inc(s_mx, 1)
                dve.wait_ge(s_ar, turn + 1)
                st.tick(dve.tensor_tensor(inv[:], ar[:, 0:1], ar[:, 1:2], ALU.mult))
                st.hold()
                st.tick(dve.reciprocal(inv[:], inv[:]))
                st.hold()
                for b in range(B):
                    st.tick(dve.tensor_scalar(Z[rows(b)], XT_diag[rows(b), :, b], inv[rows(b)], None, ALU.mult))
                st.tick(dve.tensor_scalar(ZT[:], X[:], inv[:], None, ALU.mult))
                dve.wait_ge(s_mx, 2 * turn + 2)
                st.tick(dve.tensor_scalar(ZT_diag[:], X_diag[:], inv[:], None, ALU.mult))
                st.leave(1)

            @block.gpsimd
            def _(pool):
                wait_alone(pool, s_mx, 2 * turn + 2, L.sem("waits_passed"))
                pool.partition_all_reduce(ar[:], am[:], P, bass.bass_isa.ReduceOp.max).then_inc(s_ar, 1)

            @block.scalar
            def _(act):
                act.wait_ge(s_s, turn * STEPS + BEFORE_EXP)
                act.activation(X[:], X[:], ACT.Exp).then_inc(s_e, 1)

            @block.tensor
            def _(pe):
                pe.wait_ge(s_m2, turn + 1)
                pe.matmul(ps[:, 0, 0:M], W("wq"), xl[:], start=True, stop=True)
                pe.matmul(ps[:, 1, 0:M], W("wk"), xl[:], start=True, stop=True).then_inc(s_pr, 1)
                wait_alone(pe, s_b, turn + 1, L.sem("waits_passed"))
                for b in range(B):
                    ins = pe.matmul(ps[:, 2 + b, :], ql[:].rearrange("p b m -> p (b m)"),
                                    kd[:, b].rearrange("p h m -> p (h m)"), start=True, stop=True)
                ins.then_inc(s_at, 1)
                wait_alone(pe, s_mx, 2 * turn + 1, L.sem("waits_passed"))
                for h in range(NH):
                    ins = pe.transpose(ps[:, 4 + h // 4, h % 4 * P:(h % 4 + 1) * P],
                                       X_diag[:, h].rearrange("p b m -> p (b m)"), W("ident"))
                ins.then_inc(s_tr, 1)


def with_inverse(eng, emit):
    for s in range(4):
        emit(0, None, s, None)
    with eng.Fori(0, Layer.ITERS) as i:
        for s in range(4):
            emit(i + 1, i, s, i)
    for c in range(Layer.ITERS + 1, NCH):
        for s in range(4):
            emit(c, c - 1, s, None)
    for s in range(2):
        emit(None, NCH - 1, s, None)


def landmark_values(L, turn, xnT, V, ql_diag, O, XT_diag, Z, ZT, ZT_diag):
    nc, ps, W, sem = L.nc, L.ps, L.W, L.sem
    HP, VP, ITERS = L.HP, L.VP, L.ITERS
    s_kp, s_kc, s_s, s_cm, s_nm, s_e, s_al, s_t, s_tc, s_td, s_pv, s_o, s_i = (sem("lv_" + n) for n in (
        "k_projected", "k_copied", "scores", "chunk_max", "new_max", "exp", "alpha", "transposed", "copied_act",
        "copied_dve", "pv", "summed", "init"))
    s_p = sem("pinv_product")
    s_c = sem("pinv_terms")
    s_z = sem("pinv_copied")
    s_td2 = sem("pinv_terms_diag")
    s_zd = sem("pinv_diag")
    UPC = 2 * B
    SUM_BANK = (4, 5)
    INV_BANK, KEY_BANK = 6, 7
    with ExitStack() as stage:
        kT = L.sb("lv_kT", [P, CHUNK], stage)
        pr = L.sb("lv_probs", [P, 2, 2, CHUNK], stage)
        prT = L.sb("lv_probsT", [P, 2, 2, TPC, P], stage)
        cm = L.sb("lv_chunk_max", [P, B, HP], stage)
        mx = L.sb("lv_max", [P, B, HP], stage)
        neg = L.sb("lv_neg_max", [P, B, HP], stage)
        dl = L.sb("lv_delta", [P, B, HP], stage)
        al = L.sb("lv_alpha", [P, B, HP], stage)
        A_diag = L.sb("XZ", [P, NH, B, M], stage)
        T = L.sb("pinv_T", [P, 2, NH, M], stage)
        T_diag = L.sb("pinv_T_diag", [P, NH, B, M], stage)
        eye = W("eye").rearrange("p (h m) -> p h m", h=1).broadcast_to([P, NH, M])
        u_of = lambda c, s: UPC * (NCH * turn + c) + s
        c_before = lambda c: NCH * turn + c
        p_of = lambda i: 5 * (ITERS * turn + i)
        c_of = lambda i: 3 * (ITERS * turn + i)
        z_of = lambda i: 2 * (ITERS * turn + i) + 1
        d_of = lambda i: ITERS * turn + i
        rows = lambda b: slice(b * M, (b + 1) * M)
        bank = ps[:, INV_BANK, :].rearrange("p (h m) -> p h m", m=M)

        def lagged(fn, now, before, s, lag):
            c, k = (now, s - lag) if s >= lag else (before, s - lag + UPC)
            if c is not None:
                fn(c, k)
        first = lambda c, s: isinstance(c, int) and c == 0 and s < 2
        more_after = lambda c: c is not None and not (isinstance(c, int) and c == NCH - 1)

        with nc.Block() as block:
            @block.tensor
            def _(pe):
                def keys(c):
                    chunk = xnT[:, :].rearrange("p (c n) -> p c n", n=CHUNK)[:, c]
                    pe.matmul(ps[:, KEY_BANK, :], W("wk"), chunk, start=True, stop=True).then_inc(s_kp, 1)

                def scores(c, s):
                    b, hf = divmod(s, 2)
                    if s == 0:
                        pe.wait_ge(s_kc, c_before(c) + 1)
                    if not first(c, s):
                        pe.wait_ge(s_tc, u_of(c, s) - 1)
                        pe.wait_ge(s_td, u_of(c, s) - 1)
                    for k in range(2):
                        p = 2 * hf + k
                        pe.matmul(ps[:, 2 * hf + k, :], ql_diag[:, b, 2 * p:2 * p + 2].rearrange("p h m -> p (h m)"),
                                  kT[:], start=True, stop=True).then_inc(s_s, 1)

                def transposes(c, s):
                    hf = s % 2
                    for k in range(2):
                        pe.wait_ge(s_e, 2 * u_of(c, s) + k + 1)
                        for t in range(TPC):
                            ins = pe.transpose(ps[:, 2 * hf + k, t * P:(t + 1) * P],
                                               pr[:, hf, k, t * P:(t + 1) * P], W("ident"))
                        ins.then_inc(s_t, 1)

                def values(c, s):
                    b, hf = divmod(s, 2)
                    pe.wait_ge(s_tc, u_of(c, s) + 1)
                    pe.wait_ge(s_td, u_of(c, s) + 1)
                    if not first(c, s):
                        pe.wait_ge(s_o, u_of(c, s) - 1)
                    for k in range(2):
                        for t in range(TPC):
                            vals = V[:, :, b, 2 * hf + k, :].rearrange("p (c t) e -> p c t e", t=TPC)[:, c, t]
                            ins = pe.matmul(ps[:, SUM_BANK[hf], k * VP:(k + 1) * VP], prT[:, hf, k, t], vals,
                                            start=t == 0, stop=t == TPC - 1)
                    ins.then_inc(s_pv, 1)

                def product(stationary, moving):
                    for h in range(NH):
                        ins = pe.matmul(ps[:, INV_BANK, h * M:(h + 1) * M], stationary[:, h].rearrange("p b m -> p (b m)"),
                                        moving[:, h], start=True, stop=True)
                    ins.then_inc(s_p, 1)

                def step(now, before, s, i):
                    lagged(scores, now, before, s, 0)
                    if i is not None and s == 3:
                        wait_alone(pe, s_c, c_of(i) + 3, sem("waits_passed"))
                        wait_alone(pe, s_zd, d_of(i) + 1, sem("waits_passed"))
                        product(ZT_diag, T[:, 0])
                    if s == 3 and more_after(now):
                        keys(now + 1)
                    lagged(transposes, now, before, s, 1)
                    lagged(values, now, before, s, 2)
                    if i is None:
                        return
                    if s == 0:
                        wait_alone(pe, s_z, z_of(i), sem("waits_passed"))
                        product(XT_diag, Z)
                    elif s < 3:
                        wait_alone(pe, s_c, c_of(i) + s, sem("waits_passed"))
                        product(A_diag, T[:, s - 1])
                    else:
                        wait_alone(pe, s_z, z_of(i) + 1, sem("waits_passed"))
                        wait_alone(pe, s_td2, d_of(i) + 1, sem("waits_passed"))
                        product(T_diag, ZT)
                keys(0)
                with_inverse(pe, step)

            @block.vector
            def _(dve):
                def maxima(c, s):
                    b, hf = divmod(s, 2)
                    for k in range(2):
                        dve.wait_ge(s_s, 2 * u_of(c, s) + k + 1)
                        p = 2 * hf + k
                        dve.tensor_reduce(cm[:, b, p:p + 1], ps[:, p, :], AX.X, ALU.max).then_inc(s_cm, 1)

                def running(c, s):
                    b, hf = divmod(s, 2)
                    r = slice(2 * hf, 2 * hf + 2)
                    dve.wait_ge(s_cm, 2 * u_of(c, s) + 2)
                    dve.tensor_tensor(cm[:, b, r], cm[:, b, r], mx[:, b, r], ALU.max).then_inc(s_nm, 1)
                    dve.wait_ge(s_nm, 3 * u_of(c, s) + 1)
                    dve.tensor_scalar(neg[:, b, r], cm[:, b, r], -1.0, None, ALU.mult)
                    dve.tensor_tensor(dl[:, b, r], mx[:, b, r], cm[:, b, r], ALU.subtract).then_inc(s_nm, 1)
                    dve.wait_ge(s_nm, 3 * u_of(c, s) + 2)
                    dve.tensor_copy(mx[:, b, r], cm[:, b, r]).then_inc(s_nm, 1)

                def copied(c, s):
                    hf = s % 2
                    dve.wait_ge(s_t, 2 * u_of(c, s) + 2)
                    dve.tensor_copy(prT[:, hf, 1], ps[:, 2 * hf + 1, :].rearrange("p (t n) -> p t n", n=P)).then_inc(s_td, 1)

                def sums(c, s):
                    b, hf = divmod(s, 2)
                    dve.wait_ge(s_al, u_of(c, s) + 1)
                    dve.wait_ge(s_pv, u_of(c, s) + 1)
                    if not first(c, s):
                        dve.wait_ge(s_o, u_of(c, s) - 1)
                    for k in range(2):
                        p = 2 * hf + k
                        ins = dve.scalar_tensor_tensor(O[:, b, p], O[:, b, p], al[:, b, p:p + 1],
                                                       ps[:, SUM_BANK[hf], k * VP:(k + 1) * VP], ALU.mult, ALU.add)
                    ins.then_inc(s_o, 1)

                def step(now, before, s, i):
                    lagged(maxima, now, before, s, 0)
                    lagged(copied, now, before, s, 1)
                    lagged(running, now, before, s, 0)
                    lagged(sums, now, before, s, 2)
                    if i is not None and s < 3:
                        dve.wait_ge(s_p, p_of(i) + s + 1)
                        if s == 0:
                            for b in range(B):
                                dve.tensor_copy(A_diag[rows(b), :, b], bank[rows(b)])
                        dve.scalar_tensor_tensor(T[:, s % 2], eye, (7.0, 15.0, 13.0)[s], bank, ALU.mult,
                                                 ALU.subtract).then_inc(s_c, 1)
                dve.memset(mx[:], -1e30)
                dve.memset(A_diag[:], 0.0)
                dve.memset(O[:], 0.0).then_inc(s_i, 1)
                wait_alone(dve, s_i, turn + 1, sem("waits_passed"))
                with_inverse(dve, step)

            @block.scalar
            def _(act):
                def keys(c):
                    act.wait_ge(s_kp, c_before(c) + 1)
                    act.activation(kT[:], ps[:, KEY_BANK, :], ACT.Copy).then_inc(s_kc, 1)

                def copied(c, s):
                    hf = s % 2
                    act.wait_ge(s_t, 2 * u_of(c, s) + 1)
                    act.activation(prT[:, hf, 0], ps[:, 2 * hf, :].rearrange("p (t n) -> p t n", n=P),
                                   ACT.Copy).then_inc(s_tc, 1)

                def exponentials(c, s):
                    b, hf = divmod(s, 2)
                    act.wait_ge(s_nm, 3 * u_of(c, s) + 2)
                    for k in range(2):
                        p = 2 * hf + k
                        act.activation(pr[:, hf, k], ps[:, p, :], ACT.Exp, bias=neg[:, b, p:p + 1]).then_inc(s_e, 1)
                    act.activation(al[:, b, 2 * hf:2 * hf + 2], dl[:, b, 2 * hf:2 * hf + 2], ACT.Exp).then_inc(s_al, 1)

                def scaled(out, count):
                    act.wait_ge(s_p, count)
                    act.activation(out[:], bank, ACT.Copy, scale=0.25).then_inc(s_z, 1)

                def step(now, before, s, i):
                    if i is not None and s == 3:
                        scaled(Z, p_of(i) + 4)
                    if s == 3 and more_after(now):
                        keys(now + 1)
                    lagged(copied, now, before, s, 1)
                    lagged(exponentials, now, before, s, 0)
                    if i is not None and s == 3:
                        scaled(ZT, p_of(i) + 5)
                keys(0)
                with_inverse(act, step)

            @block.gpsimd
            def _(pool):
                batches = W("batch_of").rearrange("p (h b m) -> p h b m", h=1, m=1).broadcast_to([P, NH, B, M])
                twice = lambda a: a.rearrange("p h (n m) -> p h n m", n=1).broadcast_to([P, NH, B, M])
                with pool.Fori(0, ITERS) as i:
                    wait_alone(pool, s_c, c_of(i) + 3, sem("waits_passed"))
                    pool.tensor_tensor(T_diag[:], twice(T[:, 0]), batches, ALU.mult).then_inc(s_td2, 1)
                    wait_alone(pool, s_z, z_of(i) + 2, sem("waits_passed"))
                    pool.tensor_tensor(ZT_diag[:], twice(ZT[:]), batches, ALU.mult).then_inc(s_zd, 1)


def landmark_weights(L, turn, O, ZT_diag, w_diag):
    nc, ps, W, sem = L.nc, L.ps, L.W, L.sem
    HP, V1, G = L.HP, L.V1, B * L.HP
    s_i, s_o, s_p, s_d = (sem("lw_" + n) for n in ("init", "o_ready", "product", "diag"))
    with ExitStack() as stage:
        inv = L.sb("lw_inv", [P, G], stage)
        On = L.sb("lw_o", [P, G, HD], stage)
        O0 = L.sb("lw_o0", [P, HP, 2, HD], stage)
        with nc.Block() as block:
            @block.vector
            def _(dve):
                st = Steps(dve, s_i)
                st.enter(turn, 10)
                st.tick(dve.memset(w_diag[:], 0.0))
                O3 = O[:, :, :, :].rearrange("p b h e -> p (b h) e")
                st.tick(dve.reciprocal(inv[:], O3[:, :, 2 * HD]))
                st.hold()
                for q in range(2):
                    rows = slice(q * M, (q + 1) * M)
                    st.tick(dve.memset(w_diag[rows, :, :, q, HD:V1], 1.0))
                    wide = inv[rows].rearrange("p (g e) -> p g e", e=1).broadcast_to([M, G, HD])
                    st.tick(dve.tensor_tensor(On[rows], O3[rows, :, q * HD:(q + 1) * HD], wide, ALU.mult))
                st.hold()
                for q in range(2):
                    for b in range(B):
                        st.tick(dve.tensor_copy(O0[b * M:(b + 1) * M, :, q], On[q * M:(q + 1) * M, b * HP:(b + 1) * HP]))
                st.hold()
                st.leave(1)
                dve.wait_ge(s_p, turn + 1)
                for q in range(2):
                    for b in range(B):
                        ins = dve.tensor_copy(w_diag[q * M:(q + 1) * M, b, :, q, 0:HD], ps[b * M:(b + 1) * M, 0, 0:C].rearrange(
                            "p (h q d) -> p h q d", q=2, d=HD)[:, :, q])
                ins.then_inc(s_d, 1)

            @block.tensor
            def _(pe):
                wait_alone(pe, s_i, 10 * turn + 10, L.sem("waits_passed"))
                for h in range(NH):
                    ins = pe.matmul(ps[:, 0, h * HD:(h + 1) * HD], ZT_diag[:, h].rearrange("p b m -> p (b m)"),
                                    O0[:, h // 2, h % 2], start=True, stop=True)
                ins.then_inc(s_p, 1)


def value_convolution(L, turn, V, res):
    nc, ps, W, sem = L.nc, L.ps, L.W, L.sem
    s_c, s_cc = sem("conv_product"), sem("conv_copied")
    NU = NH * B
    near = W("band").rearrange("p (h n) -> p h n", h=NH)
    before = W("band_before").rearrange("p (h n) -> p h n", h=NH)
    after = W("band_after").rearrange("p (h n) -> p h n", h=NH)
    with nc.Block() as block:
        @block.tensor
        def _(pe):
            for n in range(NU):
                h, b = divmod(n, B)
                p, q = divmod(h, 2)
                vals = V[:, :, b, p, q * HD:(q + 1) * HD]
                if n >= 8:
                    pe.wait_ge(s_cc, NU * turn + n - 7)
                out = ps[:, n % 8, 0:NT * HD].rearrange("p (t d) -> p t d", d=HD)
                pe.matmul(out, near[:, h], vals[:, 1:NT + 1], start=True, stop=False)
                pe.matmul(out, before[:, h], vals[:, 0:NT], start=False, stop=False)
                pe.matmul(out, after[:, h], vals[:, 2:NT + 2], start=False, stop=True).then_inc(s_c, 1)

        def copy(eng, fn, parity):
            for n in range(NU):
                h, b = divmod(n, B)
                eng.wait_ge(s_c, NU * turn + n + 1)
                fn(res[:, :, b, h * HD:(h + 1) * HD], ps[:, n % 8, 0:NT * HD].rearrange(
                    "p (t d) -> p t d", d=HD)).then_inc(s_cc, 1)

        @block.vector
        def _(dve):
            copy(dve, dve.tensor_copy, 0)


def attend(L, turn, xnT, kl_diag, w_diag, res, y):
    nc, ps, W, sem = L.nc, L.ps, L.W, L.sem
    HP, V1 = L.HP, L.V1
    s_qp, s_qc, s_s, s_mx, s_sub, s_e, s_t, s_tc, s_pv, s_iv, s_a, s_ar, s_ot, s_otc, s_pr, s_y, s_b = (
        sem("at_" + n) for n in ("q_projected", "q_copied", "scores", "max", "sub", "exp", "transposed", "copied",
                                 "pv", "inverse", "normalised", "with_res", "outT", "outT_copied", "projected", "y",
                                 "bias_added"))
    with ExitStack() as stage:
        qT = L.sb("at_qT", [P, 2, P], stage)
        sc = L.sb("at_scores", [P, 4, NH * M], stage)
        prT = L.sb("at_probsT", [P, 4, HP, P], stage)
        mx = L.sb("at_max", [P, 4, NH], stage)
        inv = L.sb("at_inv", [P, 2, B * NH], stage)
        o = L.sb("at_out", [P, 2, B, NH, HD], stage)
        oT = L.sb("at_outT", [P, 2, P], stage)
        m = lambda i, lane: NT * turn + 2 * i + lane
        n = lambda i, lane, b: B * (NT * turn + 2 * i + lane) + b
        tile = lambda a, i, lane: a[:, :, :, :].rearrange("p (i k) b e -> p i k b e", k=2)[:, i, lane]
        with nc.Block() as block:
            @block.tensor
            def _(pe):
                def queries(i, lane):
                    wait_alone(pe, s_y, m(i, lane) + 4 * turn + 1, sem("waits_passed"))
                    toks = xnT[:, :].rearrange("p (i k n) -> p i k n", k=2, n=P)[:, i, lane]
                    pe.matmul(ps[:, 6 + lane, 0:P], W("wq"), toks, start=True, stop=True).then_inc(s_qp, 1)

                def product(i, lane):
                    pe.wait_ge(s_qc, m(i, lane) + 1)
                    for b in range(B):
                        pe.matmul(ps[:, 2 * lane + b, :], qT[:, lane], kl_diag[:, b].rearrange("p h m -> p (h m)"),
                                  start=True, stop=True).then_inc(s_s, 1)

                def transposes(i, lane):
                    for b in range(B):
                        k = 2 * lane + b
                        pe.wait_ge(s_e, n(i, lane, b) + 1)
                        for p in range(HP):
                            ins = pe.transpose(ps[:, k, p * P:(p + 1) * P], sc[:, k, p * P:(p + 1) * P], W("ident"))
                        ins.then_inc(s_t, 1)

                def outputs(i, lane):
                    for b in range(B):
                        pe.wait_ge(s_tc, n(i, lane, b) + 1)
                        for p in range(HP):
                            at = (b * HP + p) * 2 * V1
                            ins = pe.matmul(ps[:, 4 + lane, at:at + 2 * V1], prT[:, 2 * lane + b, p],
                                            w_diag[:, b, p].rearrange("p q e -> p (q e)"), start=True, stop=True)
                    ins.then_inc(s_pv, 1)

                def turned(i, lane):
                    pe.wait_ge(s_ar, m(i, lane) + 1)
                    pe.transpose(ps[:, 6 + lane, 2 * P:3 * P], o[:, lane].rearrange("p b h d -> p (b h d)"),
                                 W("ident")).then_inc(s_ot, 1)

                def projected(i, lane):
                    pe.wait_ge(s_otc, m(i, lane) + 1)
                    pe.matmul(ps[:, 6 + lane, 3 * P:4 * P], oT[:, lane], W("w_out"), start=True,
                              stop=True).then_inc(s_pr, 1)
                pe.sem_inc(s_y, 4)
                pipelined(pe, NT, [(2, transposes), (1, product), (3, turned), (2, outputs), (0, queries),
                                   (3, projected)])

            @block.vector
            def _(dve):
                def softmax(i, lane):
                    s3 = lambda b: ps[:, 2 * lane + b, :].rearrange("p (h m) -> p h m", h=NH)
                    for b in range(B):
                        dve.wait_ge(s_s, n(i, lane, b) + 1)
                        dve.tensor_reduce(mx[:, 2 * lane + b], s3(b), AX.X, ALU.max).then_inc(s_mx, 1)
                    for b in range(B):
                        dve.wait_ge(s_mx, n(i, lane, b) + 1)
                        wide = mx[:, 2 * lane + b].rearrange("p (h m) -> p h m", m=1).broadcast_to([P, NH, M])
                        dve.tensor_tensor(sc[:, 2 * lane + b].rearrange("p (h m) -> p h m", h=NH), s3(b), wide,
                                          ALU.subtract).then_inc(s_sub, 1)

                def normalise(i, lane):
                    pv = ps[:, 4 + lane, 0:B * NH * V1].rearrange("p (g e) -> p g e", e=V1)
                    dve.wait_ge(s_pv, m(i, lane) + 1)
                    dve.reciprocal(inv[:, lane], pv[:, :, HD]).then_inc(s_iv, 1)
                    dve.wait_ge(s_iv, m(i, lane) + 1)
                    wide = inv[:, lane].rearrange("p (g e) -> p g e", e=1).broadcast_to([P, B * NH, HD])
                    dve.tensor_tensor(o[:, lane].rearrange("p b h d -> p (b h) d"), pv[:, :, 0:HD], wide,
                                      ALU.mult).then_inc(s_a, 1)
                    dve.wait_ge(s_a, m(i, lane) + 1)
                    both_b = o[:, lane].rearrange("p b h d -> p b (h d)")
                    dve.tensor_tensor(both_b, both_b, tile(res, i, lane), ALU.add).then_inc(s_ar, 1)

                def projected(i, lane):
                    dve.wait_ge(s_pr, m(i, lane) + 1)
                    dve.tensor_tensor(tile(y, i, lane), tile(y, i, lane), ps[:, 6 + lane, 3 * P:4 * P].rearrange(
                        "p (b e) -> p b e", b=B), ALU.add).then_inc(s_y, 1)
                wait_alone(dve, s_b, NCH * turn + NCH, L.sem("waits_passed"))
                pipelined(dve, NT, [(1, softmax), (2, normalise), (3, projected)])

            @block.gpsimd
            def _(pool):
                wide = W("b_out").rearrange("p (t b c) -> p t b c", t=1, b=1).broadcast_to([P, TPC, B, C])
                with pool.Fori(0, NCH) as c:
                    rows = y[:, :, :, :].rearrange("p (c t) b e -> p c t b e", t=TPC)[:, c]
                    pool.tensor_tensor(rows, rows, wide, ALU.add).then_inc(s_b, 1)

            @block.scalar
            def _(act):
                def queries(i, lane):
                    act.wait_ge(s_qp, m(i, lane) + 1)
                    act.activation(qT[:, lane], ps[:, 6 + lane, 0:P], ACT.Copy).then_inc(s_qc, 1)

                def exponentials(i, lane):
                    for b in range(B):
                        k = 2 * lane + b
                        act.wait_ge(s_sub, n(i, lane, b) + 1)
                        act.activation(sc[:, k], sc[:, k], ACT.Exp).then_inc(s_e, 1)

                def probabilities(i, lane):
                    for b in range(B):
                        k = 2 * lane + b
                        act.wait_ge(s_t, n(i, lane, b) + 1)
                        act.activation(prT[:, k], ps[:, k, :].rearrange("p (h n) -> p h n", n=P),
                                       ACT.Copy).then_inc(s_tc, 1)

                def turned(i, lane):
                    act.wait_ge(s_ot, m(i, lane) + 1)
                    act.activation(oT[:, lane], ps[:, 6 + lane, 2 * P:3 * P], ACT.Copy).then_inc(s_otc, 1)
                pipelined(act, NT, [(2, probabilities), (3, turned), (1, exponentials), (0, queries)])


def feed_forward(L, turn, norm, y):
    nc, ps, W, sem, U = L.nc, L.ps, L.W, L.sem, L.U
    s_n, s_t, s_x, s_h, s_g, s_o, s_b, s_y = (sem("ff_" + n) for n in (
        "ready", "transposed", "xT_ready", "hidden", "gelu", "out", "bias_added", "y"))
    at = lambda i, u: NCH * turn + U * i + u
    with ExitStack() as stage:
        xn = L.sb("ff_xn", [P, U, TPC, B, C], stage)
        xs = L.sb("ff_xs", [P, U, CHUNK], stage)
        hd = L.sb("ff_hidden", [P, U, B, CHUNK], stage)
        with nc.Block() as block:
            @block.gpsimd
            def _(pool):
                wide = W("b2").rearrange("p (t b c) -> p t b c", t=1, b=1).broadcast_to([P, TPC, B, C])
                with pool.Fori(0, NCH // U) as i:
                    for u in range(U):
                        pool.tensor_tensor(chunk_of(y, i, u), chunk_of(y, i, u), wide, ALU.add).then_inc(s_b, 1)

            @block.vector
            def _(dve):
                with dve.Fori(0, NCH // U) as i:
                    for u in range(U):
                        normed(dve, norm, xn[:, u], i, u).then_inc(s_n, 1)
                    for u in range(U):
                        dve.wait_ge(s_o, at(i, u) + 1)
                        dve.wait_ge(s_b, at(i, u) + 1)
                        dve.tensor_tensor(chunk_of(y, i, u), chunk_of(y, i, u), ps[:, 6 + u % 2, :].rearrange(
                            "p (t b c) -> p t b c", t=TPC, b=B), ALU.add).then_inc(s_y, 1)

            @block.tensor
            def _(pe):
                with pe.Fori(0, NCH // U) as i:
                    for u in range(U):
                        pe.wait_ge(s_n, at(i, u) + 1)
                        for t in range(TPC):
                            ins = pe.transpose(ps[:, u, t * P:(t + 1) * P],
                                               xn[:, u, t].rearrange("p b c -> p (b c)"), W("ident"))
                        ins.then_inc(s_t, 1)
                    for u in range(U):
                        pe.wait_ge(s_x, at(i, u) + 1)
                        for b in range(B):
                            k = B * u + b
                            bank = (3, 4, 5)[k % 3]
                            if k >= 3:
                                pe.wait_ge(s_g, B * at(i, 0) + k - 2)
                            pe.matmul(ps[:, bank, :], W(f"w1_{b}"), xs[:, u], start=True, stop=True).then_inc(s_h, 1)
                    for u in range(U):
                        pe.wait_ge(s_g, B * at(i, u) + B)
                        if u == 2:
                            pe.wait_ge(s_y, at(i, 0) + 1)
                        for t in range(TPC):
                            for b in range(B):
                                ins = pe.matmul(ps[:, 6 + u % 2, (t * B + b) * C:(t * B + b + 1) * C],
                                                hd[:, u, b, t * P:(t + 1) * P], W("w2"), start=True, stop=True)
                        ins.then_inc(s_o, 1)
                    pe.wait_ge(s_y, at(i, 0) + U)

            @block.scalar
            def _(act):
                with act.Fori(0, NCH // U) as i:
                    for u in range(U):
                        act.wait_ge(s_t, at(i, u) + 1)
                        act.activation(xs[:, u], ps[:, u, :], ACT.Identity, bias=W("ln2_b"),
                                       scale=W("ln2_g")).then_inc(s_x, 1)
                    for u in range(U):
                        for b in range(B):
                            k = B * u + b
                            act.wait_ge(s_h, B * at(i, 0) + k + 1)
                            act.activation(hd[:, u, b], ps[:, (3, 4, 5)[k % 3], :], ACT.Gelu,
                                           bias=W("b1")).then_inc(s_g, 1)


def attention_layer(L, turn, norm):
    y, HP = L.y, L.HP
    with ExitStack() as stage:
        norm.run(y, 1 + 2 * turn)
        xnT = L.sb("xnT", [P, N_TOK], stage)
        V_padded = L.sb("V", [P, NT + 2, B, HP, L.VP], stage)
        V = V_padded[:, 1:NT + 1]
        w_diag = L.sb("w_diag", [P, B, HP, 2, L.V1], stage)
        kl_diag = L.sb("kl_diag", [P, B, NH, M], stage)
        project_values(L, turn, norm, xnT, V, V_padded)
        with ExitStack() as inner:
            X_diag, XT_diag, ZT_diag = (L.sb(n, [P, NH, B, M], inner) for n in ("X_diag", "XT_diag", "ZT_diag"))
            Z, ZT = (L.sb(n, [P, NH, M], inner) for n in ("Z", "ZT"))
            ql_diag = L.sb("ql_diag", [P, B, NH, M], inner)
            O = L.sb("O", [P, B, HP, L.VP], inner)
            landmarks(L, turn, xnT, ql_diag, kl_diag, X_diag, XT_diag, Z, ZT, ZT_diag)
            landmark_values(L, turn, xnT, V, ql_diag, O, XT_diag, Z, ZT, ZT_diag)
            landmark_weights(L, turn, O, ZT_diag, w_diag)
        res = L.sb("res", [P, NT, B, C], stage)
        value_convolution(L, turn, V_padded, res)
        attend(L, turn, xnT, kl_diag, w_diag, res, y)
    norm.run(y, 2 + 2 * turn)
    feed_forward(L, turn, norm, y)



NE = 16
HID = 128
TOP = 2


class Experts:

    X_SCALE = 2.0 ** 10
    W_PEAK = 2.0 ** 10
    QUARTERS = 4

    def __init__(self, nc, ctx):
        self.nc = nc
        sb = lambda n, s, d=F16: ctx.enter_context(nc.sbuf_tensor("moe_" + n, s, d))
        self.w_a = sb("w_part1", [P, NE, 2 * HID])
        self.w_b = sb("w_part2", [P, NE, 2 * HID])
        self.down = sb("down", [P, NE, C], F32)
        self.unscale = sb("unscale", [P, 1], F32)
        self.s_load, self.s_pk, self.s_all, self.s_inv, self.s_w, self.s_a, self.s_b = (
            ctx.enter_context(nc.semaphore("moe_" + n)) for n in (
                "weights_loaded", "peak", "peak_of_all", "scale", "w_scaled", "w_part1", "w_part2"))

    def place(self, ctx):
        sb = lambda n, s: ctx.enter_context(self.nc.sbuf_tensor("moe_" + n, s, F32))
        self.raw = sb("raw", [P, NE, 2 * HID])
        self.scaled = sb("scaled", [P, NE, 2 * HID])
        self.peak = sb("peak", [P, 1])
        self.all = sb("peak_of_all", [P, 1])
        self.inv = sb("scale", [P, 1])

    def load(self, sp, w1, w2, w3):
        for half in range(2):
            for k, w in enumerate((w1, w2)):
                sp.dma_start(self.raw[half * C:(half + 1) * C, :, k * HID:(k + 1) * HID],
                             w.rearrange("e c h -> c e h")).then_inc(self.s_load, 16)
        sp.dma_start(self.down[:], w3.rearrange("e h c -> h e c")).then_inc(self.s_load, 16)

    def split(self, block):
        n = NE // self.QUARTERS
        part = lambda t, q: t[:, q * n:(q + 1) * n, :]

        @block.vector
        def _(dve):
            dve.wait_ge(self.s_load, 16 * 5)
            dve.tensor_reduce(self.peak[:], self.raw[:].rearrange("p e h -> p (e h)"), AX.X, ALU.max,
                              apply_absolute_value=True).then_inc(self.s_pk, 1)
            dve.wait_ge(self.s_all, 1)
            dve.tensor_scalar(self.inv[:], self.all[:], 1e-30, None, ALU.max).then_inc(self.s_inv, 1)
            dve.wait_ge(self.s_inv, 1)
            dve.tensor_scalar(self.unscale[:], self.inv[:], 1.0 / (self.X_SCALE * self.W_PEAK), None,
                              ALU.mult).then_inc(self.s_inv, 1)
            dve.wait_ge(self.s_inv, 2)
            dve.reciprocal(self.inv[:], self.inv[:]).then_inc(self.s_inv, 1)
            dve.wait_ge(self.s_inv, 3)
            for q in range(self.QUARTERS):
                dve.tensor_scalar(part(self.scaled, q), part(self.raw, q), self.inv[:], self.W_PEAK, ALU.mult,
                                  ALU.mult).then_inc(self.s_w, 1)
            for q in range(self.QUARTERS):
                dve.wait_ge(self.s_a, q + 1)
                dve.wait_ge(self.s_w, q + 1)
                dve.tensor_tensor(part(self.w_b, q), part(self.scaled, q), part(self.w_a, q),
                                  ALU.subtract).then_inc(self.s_b, 1)
            dve.wait_ge(self.s_b, self.QUARTERS)

        @block.gpsimd
        def _(pool):
            pool.wait_ge(self.s_pk, 1)
            pool.partition_all_reduce(self.all[:], self.peak[:], P, bass.bass_isa.ReduceOp.max).then_inc(self.s_all, 1)

        @block.scalar
        def _(act):
            for q in range(self.QUARTERS):
                act.wait_ge(self.s_w, q + 1)
                act.activation(part(self.w_a, q), part(self.scaled, q), ACT.Copy).then_inc(self.s_a, 1)


def route(nc, ctx, ps, norm, x12, gate, W):
    sem = lambda n: ctx.enter_context(nc.semaphore("route_" + n))
    s_n, s_t, s_x, s_1, s_2, s_l, s_lg = map(sem, (
        "ready", "transposed", "xT_ready", "part1", "part2", "logits", "logits_copied"))
    s_d, s_e = sem("dve"), sem("exp")
    with ExitStack() as stage:
        sb = lambda n, s, d=F32: stage.enter_context(nc.sbuf_tensor("rt_" + n, s, d))
        xn = sb("xn", [P, B, TPC, 2, C])
        xs = sb("xs", [P, B, CHUNK])
        x1 = sb("x_part1", [P, B, CHUNK], F16)
        prob = sb("prob", [P, NT * B, NE])
        rest = sb("rest", [P, NT * B, NE])
        cand = sb("cand", [P, NT * B, NE])
        small = sb("small", [P, 6, NT * B])
        g = gate[:, :, :, :].rearrange("p t b e -> p (t b) e")
        u_of = lambda c, b: B * c + b
        later = lambda c: not (isinstance(c, int) and c == 0)
        cols = lambda t, c, b, rows: t[rows, b].rearrange("p (c n) -> p c n", n=CHUNK)[:, c]
        lower, upper = slice(0, C), slice(C, P)
        with nc.Block() as block:
            @block.vector
            def _(dve):
                def normalise(c, b):
                    if later(c):
                        dve.wait_ge(s_t, u_of(c, b) - 1)
                    r = norm.rstd[:, :, :].rearrange("p (c t) (b n) -> p c t b n", t=TPC, n=1)[:, c, :, b]
                    x = norm.centred[:, :, :, :].rearrange("p (c t) b n -> p c t b n", t=TPC)[:, c, :, b]
                    for n in range(2):
                        ins = dve.tensor_tensor(xn[:, b, :, n], x, r.broadcast_to([P, TPC, C]), ALU.mult)
                    ins.then_inc(s_n, 1)

                def part2(c, b):
                    dve.wait_ge(s_x, u_of(c, b) + 1)
                    dve.wait_ge(s_1, u_of(c, b) + 1)
                    dve.scalar_tensor_tensor(cols(x12, c, b, upper), xs[upper, b], Experts.X_SCALE, x1[upper, b],
                                             ALU.mult, ALU.subtract).then_inc(s_2, 1)

                def logits(c, b):
                    dve.wait_ge(s_l, u_of(c, b) + 1)
                    out = prob[:, :, :].rearrange("p (c t b) e -> p c t b e", t=TPC, b=B)[:, c, :, b]
                    bias = W("gate_b").rearrange("p (t e) -> p t e", t=1).broadcast_to([P, TPC, NE])
                    dve.tensor_tensor(out, ps[:, 2 + b, 0:TPC * NE].rearrange("p (t e) -> p t e", t=TPC), bias,
                                      ALU.add).then_inc(s_lg, 1)
                pipelined(dve, B * NCH, [(0, normalise), (1, part2), (2, logits)])
                dve.wait_ge(s_lg, B * NCH)
                st = Steps(dve, s_d)

                def do(ins):
                    st.tick(ins)
                    st.hold()
                wide = lambda k: small[:, k].rearrange("p (n e) -> p n e", e=1).broadcast_to([P, NT * B, NE])
                iota = W("expert_iota").rearrange("p (n e) -> p n e", n=1).broadcast_to([P, NT * B, NE])
                do(dve.tensor_reduce(small[:, 0], prob[:], AX.X, ALU.max))
                do(dve.tensor_tensor(prob[:], prob[:], wide(0), ALU.subtract))
                dve.wait_ge(s_e, 1)
                do(dve.tensor_reduce(small[:, 0], prob[:], AX.X, ALU.add))
                do(dve.reciprocal(small[:, 0], small[:, 0]))
                do(dve.tensor_tensor(prob[:], prob[:], wide(0), ALU.mult))
                for k, src in enumerate((prob, rest)):
                    do(dve.tensor_reduce(small[:, 1 + k], src[:], AX.X, ALU.max))
                    do(dve.tensor_tensor(cand[:], src[:], wide(1 + k), ALU.is_equal))
                    do(dve.scalar_tensor_tensor(cand[:], cand[:], -64.0, iota, ALU.mult, ALU.add))
                    do(dve.tensor_reduce(small[:, 3], cand[:], AX.X, ALU.min))
                    do(dve.tensor_tensor(cand[:], cand[:], wide(3), ALU.is_equal))
                    if k == 0:
                        do(dve.scalar_tensor_tensor(rest[:], cand[:], -2.0, prob[:], ALU.mult, ALU.add))
                        do(dve.tensor_tensor(g, cand[:], wide(1), ALU.mult))
                    else:
                        do(dve.tensor_tensor(cand[:], cand[:], wide(2), ALU.mult))
                do(dve.tensor_tensor(small[:, 4], small[:, 1], small[:, 2], ALU.add))
                do(dve.reciprocal(small[:, 4], small[:, 4]))
                do(dve.tensor_tensor(g, g, cand[:], ALU.add))
                do(dve.tensor_tensor(g, g, wide(4), ALU.mult))

            @block.tensor
            def _(pe):
                def transposes(c, b):
                    pe.wait_ge(s_n, u_of(c, b) + 1)
                    if later(c):
                        pe.wait_ge(s_1, u_of(c, b) - 1)
                    for t in range(TPC):
                        ins = pe.transpose(ps[:, b, t * P:(t + 1) * P], xn[:, b, t].rearrange("p n c -> p (n c)"),
                                           W("ident"))
                    ins.then_inc(s_t, 1)

                def logits(c, b):
                    pe.wait_ge(s_x, u_of(c, b) + 1)
                    if later(c):
                        pe.wait_ge(s_lg, u_of(c, b) - 1)
                    for t in range(TPC):
                        ins = pe.matmul(ps[:, 2 + b, t * NE:(t + 1) * NE], xs[:, b, t * P:(t + 1) * P], W("gate_w"),
                                        start=True, stop=True)
                    ins.then_inc(s_l, 1)
                pipelined(pe, B * NCH, [(0, transposes), (1, logits)])

            @block.scalar
            def _(act):
                def part1(c, b):
                    act.wait_ge(s_t, u_of(c, b) + 1)
                    if later(c):
                        act.wait_ge(s_l, u_of(c, b) - 1)
                        act.wait_ge(s_2, u_of(c, b) - 1)
                    act.activation(xs[:, b], ps[:, b, :], ACT.Copy).then_inc(s_x, 1)
                    act.activation(cols(x12, c, b, lower), ps[lower, b, :], ACT.Copy, scale=Experts.X_SCALE)
                    act.activation(x1[upper, b], ps[upper, b, :], ACT.Copy, scale=Experts.X_SCALE).then_inc(s_1, 1)
                pipelined(act, B * NCH, [(0, part1)])
                act.wait_ge(s_d, 2)
                act.activation(prob[:], prob[:], ACT.Exp).then_inc(s_e, 1)


def experts(nc, ctx, ps, E, x12, gate, hh):
    sem = lambda n: ctx.enter_context(nc.semaphore("moe_" + n))
    s_h1, s_h2, s_sl, s_hd, s_z, s_gu, s_acc = map(sem, (
        "h1", "h2", "silu", "hidden", "out", "out_used", "summed"))
    sb = lambda n, s: ctx.enter_context(nc.sbuf_tensor("moe_" + n, s, F32))
    silu = sb("silu", [P, B, CHUNK])
    hid = sb("hidden", [P, B, CHUNK])
    gated = sb("gated", [P, B, TPC, C])
    unused = sb("unused", [P, 1])
    unit = lambda e, c, b: B * NCH * e + B * c + b

    def in_order(eng, ahead, behind):
        ahead(0, 0, 0)
        with eng.Fori(0, NE - 1) as e:
            with eng.Fori(0, NCH - 1) as c:
                ahead(e, c, 1)
                behind(e, c, 0)
                ahead(e, c + 1, 0)
                behind(e, c, 1)
            ahead(e, NCH - 1, 1)
            behind(e, NCH - 1, 0)
            ahead(e + 1, 0, 0)
            behind(e, NCH - 1, 1)
        e = NE - 1
        with eng.Fori(0, NCH - 1) as c:
            ahead(e, c, 1)
            behind(e, c, 0)
            ahead(e, c + 1, 0)
            behind(e, c, 1)
        ahead(e, NCH - 1, 1)
        behind(e, NCH - 1, 0)
        behind(e, NCH - 1, 1)

    with nc.Block() as block:
        @block.tensor
        def _(pe):
            def hidden(e, c, b):
                cols = lambda t: t[:, b].rearrange("p (c n) -> p c n", n=CHUNK)[:, c]
                for k, done in enumerate((s_h1, s_h2)):
                    w = lambda t: t[:, e, k * HID:(k + 1) * HID]
                    out = ps[:, 2 * k + b, :]
                    pe.matmul(out, w(E.w_a), cols(x12), start=True, stop=False)
                    pe.matmul(out, w(E.w_b), cols(x12), start=False, stop=True).then_inc(done, 1)

            def output(e, c, b):
                pe.wait_ge(s_hd, unit(e, c, b) + 1)
                pe.wait_ge(s_gu, unit(e, c, b) + 1)
                for t in range(TPC):
                    ins = pe.matmul(ps[:, 4 + b, t * C:(t + 1) * C], hid[:, b, t * P:(t + 1) * P], E.down[:, e],
                                    start=True, stop=True)
                ins.then_inc(s_z, 1)
            in_order(pe, hidden, output)

        @block.scalar
        def _(act):
            act.activation(unused[:], E.down[:, 0, 0:1], ACT.Silu)
            with act.Fori(0, NE) as e:
                with act.Fori(0, NCH) as c:
                    for b in range(B):
                        act.wait_ge(s_h1, unit(e, c, b) + 1)
                        act.activation(silu[:, b], ps[:, b, :], ACT.Silu, scale=E.unscale[:]).then_inc(s_sl, 1)

        @block.vector
        def _(dve):
            dve.sem_inc(s_gu, 2)

            def multiply(e, c, b):
                dve.wait_ge(s_h2, unit(e, c, b) + 1)
                dve.wait_ge(s_sl, unit(e, c, b) + 1)
                dve.scalar_tensor_tensor(hid[:, b], ps[:, 2 + b, :], E.unscale[:], silu[:, b], ALU.mult,
                                         ALU.mult).then_inc(s_hd, 1)

            def weigh(e, c, b):
                dve.wait_ge(s_z, unit(e, c, b) + 1)
                dve.wait_ge(s_acc, unit(e, c, b) + 1)
                gt = gate[:, :, :, :].rearrange("p (c t) b (e n) -> p e c b t n", t=TPC, n=1)[:, e, c, b]
                dve.tensor_tensor(gated[:, b], ps[:, 4 + b, 0:TPC * C].rearrange("p (t n) -> p t n", n=C),
                                  gt.broadcast_to([P, TPC, C]), ALU.mult).then_inc(s_gu, 1)
            in_order(dve, multiply, weigh)

        @block.gpsimd
        def _(pool):
            pool.sem_inc(s_acc, 2)
            with pool.Fori(0, NE) as e:
                with pool.Fori(0, NCH) as c:
                    for b in range(B):
                        pool.wait_ge(s_gu, unit(e, c, b) + 3)
                        pool.wait_ge(s_acc, unit(e, c, b) + 2)
                        rows = hh[:, :, :, :].rearrange("p (c t) b n -> p c b t n", t=TPC)[:, c, b]
                        pool.tensor_tensor(rows, rows, gated[:, b], ALU.add).then_inc(s_acc, 1)
            pool.wait_ge(s_acc, unit(NE, 0, 0) + 2)


def moe_columns(i):
    c = Columns()
    c.add("ident", (0, P), np.eye(P, dtype=np.float32))
    c.add("gate_w", (0, P), np.concatenate([i["L0_ffn_gate_w"], np.zeros_like(i["L0_ffn_gate_w"])]))
    c.add("gate_b", (0, P), np.tile(i["L0_ffn_gate_b"], (P, 1)))
    c.add("expert_iota", (0, P), np.tile(np.arange(NE, dtype=np.float32), (P, 1)))
    return c


def layer_columns(i, l):
    c = Columns()
    zero = np.zeros((C, C), np.float32)
    w = i["L0_attn_w_qkv"][l]
    rep = lambda a: np.tile(np.asarray(a).reshape(1, -1), (P, 1))
    twice = lambda a: np.tile(np.asarray(a).reshape(-1, 1), (B, 1))
    c.add("ident", (0, P), np.eye(P, dtype=np.float32))
    c.add("unit_of", (0, P), np.repeat(np.eye(B * NH, dtype=np.float32), HD, 0))
    c.add("batch_of", (0, P), np.repeat(np.eye(B, dtype=np.float32), C, 0))
    c.add("eye", (0, P), np.tile(np.eye(M, dtype=np.float32), (B, 1)))
    for b in range(B):
        one = lambda a: np.concatenate([a if k == b else np.zeros_like(a) for k in range(B)], 0)
        c.add(f"w1_{b}", (0, P), one(i["L0_attn_w1"][l]))
    c.add("wq", (0, P), both(w[:, 0:C]))
    c.add("wk", (0, P), both(w[:, C:2 * C]))
    c.add("wv", (0, P), both(w[:, 2 * C:]))
    c.add("w_out", (0, P), both(i["L0_attn_w_out"][l]))
    c.add("w2", (0, P), i["L0_attn_w2"][l])
    for n in ("ln1_g", "ln1_b", "ln2_g", "ln2_b"):
        c.add(n, (0, P), twice(i["L0_attn_" + n][l]))
    c.add("b1", (0, P), i["L0_attn_b1"][l][:, None])
    c.add("b_out", (0, P), rep(i["L0_attn_b_out"][l]))
    c.add("b2", (0, P), rep(i["L0_attn_b2"][l]))
    taps = i["L0_attn_res_w"][l][:, 0, :, 0]
    K = taps.shape[1]
    pad = K // 2
    line = np.zeros((NH, 3 * P), np.float32)
    line[:, P + P // 2 - pad:P + P // 2 - pad + K] = taps
    j, o = np.meshgrid(np.arange(P), np.arange(P), indexing="ij")
    banded = lambda shift: line[:, np.clip(j + shift - o + P + P // 2, 0, 3 * P - 1)]
    near, before, after = (banded(s).transpose(1, 0, 2) for s in (0, -P, P))
    for name, m in (("band", near), ("band_before", before), ("band_after", after)):
        c.add(name, (0, P), m.reshape(P, -1))
    return c


def build(nc, x, bytes_rep, positions_rep, w_img, w_txt, w_att, w_moe, w1, w2, w3, h_img, out, cols):
    with ExitStack() as ctx:
        ps = ctx.enter_context(nc.psum_tensor("ps", [P, 8, 512], F32))
        hh = ctx.enter_context(nc.sbuf_tensor("hh", [P, NT, B, C], F32))
        sem = lambda n: ctx.enter_context(nc.semaphore(n))
        s_w = sem("weights_loaded")
        s_h = sem("h_loaded")

        def load(stage, name, src, n):
            tile = stage.enter_context(nc.sbuf_tensor(name, list(src.shape), F32))
            with nc.Block() as block:
                @block.sync
                def _(sp):
                    sp.dma_start(tile[:], src).then_inc(s_w, 16)
                    sp.wait_ge(s_w, 16 * n)
            return tile

        with ExitStack() as stage:
            wt = load(stage, "weights_txt", w_txt, 1)
            text_field(nc, stage, ps, bytes_rep, positions_rep, wt, cols["txt"], hh)
        E = Experts(nc, ctx)
        with ExitStack() as raw:
            E.place(raw)
            with ExitStack() as stage:
                wa = load(stage, "weights_img", w_img, 2)
                image_attention(nc, stage, ps, x, wa, cols["img"], h_img, lambda sp: E.load(sp, w1, w2, w3))
            with nc.Block() as block:
                @block.sync
                def _(sp):
                    for b in range(B):
                        sp.dma_start(hh[:, 0:NT_IMG, b, :], h_img[b].rearrange("(t p) c -> p t c", p=P)).then_inc(s_h, 16)
                    sp.wait_ge(s_h, 16 * B)
                E.split(block)
        norm = Norm(nc, ctx, "norm")
        norm.run(hh, 0)
        s_l = sem("layer_weights_loaded")
        with ExitStack() as stage:
            weights = stage.enter_context(nc.sbuf_tensor("weights_att", [P, cols["att"].width], F32))
            L = Layer(nc, stage, ps, hh, weights, cols["att"])
            first_norm(nc, stage, norm, L.y, 0)
            with nc.Block() as block:
                @block.gpsimd
                def _(pool):
                    for name in ("pinv_copied", "pinv_diag"):
                        pool.sem_inc(L.sem(name), 1)
            with nc.Fori(0, 2) as turn:
                with nc.Block() as block:
                    @block.sync
                    def _(sp):
                        sp.dma_start(weights[:], w_att[turn]).then_inc(s_l, 16)
                        wait_alone(sp, s_l, 16 * turn + 16, L.sem("waits_passed"))
                attention_layer(L, turn, norm)
            s_r = sem("residual_added")
            with nc.Block() as block:
                @block.vector
                def _(dve):
                    dve.tensor_tensor(hh[:], hh[:], L.y[:], ALU.add).then_inc(s_r, 1)
                    dve.wait_ge(s_r, 1)
        norm.run(hh, 5)
        with ExitStack() as stage:
            wm = load(stage, "weights_moe", w_moe, 3)
            x12 = stage.enter_context(nc.sbuf_tensor("x_parts", [P, B, N_TOK], F16))
            gate = stage.enter_context(nc.sbuf_tensor("gate", [P, NT, B, NE], F32))
            route(nc, stage, ps, norm, x12, gate, lambda n: cols["moe"].view(wm, n))
            experts(nc, stage, ps, E, x12, gate, hh)
        s_o = sem("out_stored")
        with nc.Block() as block:
            @block.sync
            def _(sp):
                for b in range(B):
                    sp.dma_start(out[b].rearrange("(t p) c -> p t c", p=P), hh[:, :, b, :]).then_inc(s_o, 16)
                sp.wait_ge(s_o, 16 * B)


def both(a):
    z = np.zeros_like(a)
    return np.block([[a, z], [z, a]])


def image_columns(i):
    c = Columns()
    w, bias = i["L0_tok_qkv_w"], i["L0_tok_qkv_b"]
    pair = np.arange(C) ^ 1
    wq, wk, wv = w[0:C], w[C:2 * C], w[2 * C:3 * C]
    bq, bk, bv = bias[0:C], bias[C:2 * C], bias[2 * C:3 * C]
    all_rows = (0, P)
    c.add("ident", all_rows, np.eye(P, dtype=np.float32))
    for name, m in (("wq", wq), ("wq_pair", wq[pair]), ("wk", wk), ("wk_pair", wk[pair]), ("wv", wv)):
        c.add(name, all_rows, both(m.T))
    c.add("bias", all_rows, np.stack([np.tile(m, B) for m in (bq, bq[pair], bk, bk[pair])], 1))
    c.add("bias_v", all_rows, np.tile(bv, (P, B)))
    c.add("wproj", all_rows, both(i["L0_tok_proj_w"].T))
    c.add("bias_proj", all_rows, np.tile(i["L0_tok_proj_b"], (P, 2)))
    half = HD // 2
    freq = (1.0 / 10000.0 ** (np.arange(0, half, 2, dtype=np.float32) / np.float32(half))).astype(np.float32)
    d = np.arange(C) % HD
    y, xx = np.divmod(np.arange(WIN * WIN), WIN)
    pos = np.where((d < half)[:, None], y[None], xx[None]).astype(np.float32)
    ang = pos * freq[(d % half) // 2][:, None]
    sign = np.where(d % 2 == 0, -1.0, 1.0).astype(np.float32)[:, None]
    c.add("cos", all_rows, np.tile(np.cos(ang), (B, 1)))
    c.add("sin", all_rows, np.tile(np.sin(ang) * sign, (B, 1)))
    c.add("batch_of", all_rows, np.repeat(np.eye(B, dtype=np.float32), C, 0))
    c.add("head_of", all_rows, np.tile(np.repeat(np.eye(NH, dtype=np.float32), HD, 0), (B, 1)))
    return c


def kernel(**inputs):
    import concourse.bacc as bacc
    from concourse.bass_utils import run_bass_kernel_spmd

    i = {k: np.asarray(v) for k, v in inputs.items()}
    layers = [layer_columns(i, l) for l in range(i["L0_attn_ln1_g"].shape[0])]
    cols = {"img": image_columns(i), "txt": text_columns(i), "att": layers[0], "moe": moe_columns(i)}
    arrays = {
        "x": i["x"],
        "bytes_rep": np.broadcast_to(i["x_txt"], (C, B, S_TXT)),
        "positions_rep": np.broadcast_to(i["fside_BS_continuous_positions"], (P, B, S_TXT)),
        "w_img": cols["img"].array(), "w_txt": cols["txt"].array(),
        "w_att": np.stack([c.array() for c in layers]), "w_moe": cols["moe"].array(),
        "w1": i["L0_ffn_w1"], "w2": i["L0_ffn_w2"], "w3": i["L0_ffn_w3"],
    }
    arrays = {n: np.ascontiguousarray(a) for n, a in arrays.items()}
    nc = bacc.Bacc("TRN2", target_bir_lowering=False, num_devices=1)
    args = {n: nc.dram_tensor(n, a.shape, mybir.dt.from_np(a.dtype), kind="ExternalInput").ap()
            for n, a in arrays.items()}
    h_img = nc.dram_tensor("h_img", (B, IMG * IMG, C), F32, kind="Internal").ap()
    out = nc.dram_tensor("out_0_dram", (B, N_TOK, C), F32, kind="ExternalOutput").ap()
    build(nc, **args, h_img=h_img, out=out, cols=cols)
    r = run_bass_kernel_spmd(nc, [arrays], core_ids=[0])
    return r.results[0]["out_0_dram"]
```

```python
from contextlib import ExitStack

import numpy as np

import concourse.bass as bass
from concourse import mybir

F32 = mybir.dt.float32
F16 = mybir.dt.float16
I32 = mybir.dt.int32
ALU = mybir.AluOpType
ACT = mybir.ActivationFunctionType
AX = mybir.AxisListType

P = 128
B = 2
C = 64
NH = 8
HD = C // NH
IMG = 64
WIN = 8
NT_IMG = IMG * IMG // P
S_TXT = 512
NT = NT_IMG + S_TXT // P
N_TOK = NT * P
M = 64
GROUP = N_TOK // M
CHUNK = 512
NCH = N_TOK // CHUNK
TPC = CHUNK // P
NS = 4
ROUND = 1.5 * 2.0 ** 23


def pipelined(eng, n, stages):
    deepest = max(lag for lag, _ in stages)
    turns = deepest // 2 + 1

    def peeled(h):
        for lag, emit in stages:
            if 0 <= h - lag < n:
                emit(*divmod(h - lag, 2))
    for h in range(2 * turns):
        peeled(h)
    with eng.Fori(0, n // 2 - turns) as i:
        for lane in range(2):
            for lag, emit in stages:
                back, k = divmod(lane - lag, 2)
                emit(i + turns + back, k)
    for h in range(n, n + deepest):
        peeled(h)


class Columns:

    def __init__(self):
        self.at, self.width, self.parts = {}, 0, []

    def add(self, name, rows, array):
        array = np.asarray(array)
        self.at[name] = (rows, self.width, array.shape[1])
        self.parts.append((rows, self.width, array))
        self.width += array.shape[1]

    def array(self):
        out = np.zeros((P, self.width), np.float32)
        for (r0, r1), at, a in self.parts:
            out[r0:r1, at:at + a.shape[1]] = a
        return out

    def view(self, tile, name):
        (r0, r1), at, w = self.at[name]
        return tile[r0:r1, at:at + w]


def wait_alone(eng, sem, value, passed):
    eng.wait_ge(sem, value)
    eng.sem_inc(passed, 1)


class Steps:

    def __init__(self, eng, sem):
        self.eng, self.sem, self.base, self.n = eng, sem, 0, 0

    def tick(self, ins):
        ins.then_inc(self.sem, 1)
        self.n += 1

    def hold(self):
        self.eng.wait_ge(self.sem, self.base + self.n)

    def enter(self, i, per):
        self.outer, self.per = (self.base, self.n), per
        self.base, self.n = self.base + self.n + i * per, 0

    def leave(self, turns):
        assert self.n == self.per, (self.n, self.per)
        base, n = self.outer
        self.base, self.n = base, n + turns * self.per



def image_attention(nc, ctx, sem, ps, x, wa, cols, h_img, hh, s_h, weights_loaded, load_more, finish):
    NROW = IMG // WIN
    NW = NROW * WIN
    SCALE = float(HD) ** -0.5
    HP = NH // 2
    sb = lambda n, s: ctx.enter_context(nc.sbuf_tensor(n, s, F32))
    x_in = sb("x_in", [P, 2, TPC, B, C])
    xT = sb("xT", [P, NROW, CHUNK])
    qT = sb("qT", [P, NROW, CHUNK])
    kT = sb("kT", [P, NROW, CHUNK])
    rope_a = sb("rope_a", [P, 2, 2, CHUNK])
    rope_b = sb("rope_b", [P, 2, 2, CHUNK])
    W = lambda n: cols.view(wa, n)
    ident = W("ident")
    over_windows = lambda n: W(n).rearrange("p (w n) -> p w n", w=1).broadcast_to([P, WIN, WIN * WIN])

    s_x = [sem("x_loaded_0"), sem("x_loaded_1")]
    s_tr = sem("x_transposed")
    s_xT = sem("xT_ready")
    s_qk = sem("qk_projected")
    s_ra = sem("rope_terms_ready")
    s_rd = sem("rope_done")

    with nc.Block() as block:
        @block.sync
        def _(sp):
            def fetch(i, u):
                if later(i):
                    sp.wait_ge(s_tr, 2 * i + u - 1)
                for b in range(B):
                    rows = x[b].rearrange("(i u t y) x c -> i u (y x) t c", u=2, t=TPC, y=2)
                    sp.dma_start(x_in[:, u, :, b, :], rows[i, u]).then_inc(s_x[u], 16)
            pipelined(sp, NROW, [(0, fetch)])
            load_more(sp)

        @block.tensor
        def _(pe):
            weights_loaded(pe)

            def transposes(i, u):
                pe.wait_ge(s_x[u], 32 * i + 32)
                if later(i):
                    pe.wait_ge(s_xT, 2 * i + u - 1)
                for t in range(TPC):
                    ins = pe.transpose(ps[:, (0, 5)[u], t * P:(t + 1) * P],
                                       x_in[:, u, t].rearrange("p b c -> p (b c)"), ident)
                ins.then_inc(s_tr, 1)

            def projections(i, u):
                pe.wait_ge(s_xT, 2 * i + u + 1)
                chunk = xT[:, :, :].rearrange("p (i u) n -> p i u n", u=2)[:, i, u]
                for n, name in enumerate(("wq", "wq_pair", "wk", "wk_pair")):
                    if later(i) or u:
                        pe.wait_ge(s_ra, 4 * (2 * i + u) - 3 + n)
                    pe.matmul(ps[:, 1 + n, :], W(name), chunk, start=True, stop=True).then_inc(s_qk, 1)
            pipelined(pe, NROW, [(0, transposes), (1, projections)])

        @block.scalar
        def _(act):
            def turned(i, u):
                act.wait_ge(s_tr, 2 * i + u + 1)
                out = xT[:, :, :].rearrange("p (i u) (w y x) -> p i u y w x", u=2, y=WIN, x=WIN)[:, i, u]
                for y in range(WIN):
                    ins = act.activation(out[:, y], ps[:, (0, 5)[u], y * IMG:(y + 1) * IMG].rearrange(
                        "p (w x) -> p w x", x=WIN), ACT.Copy)
                ins.then_inc(s_xT, 1)
            pipelined(act, NROW, [(0, turned)])

        @block.vector
        def _(dve):
            def rotated(i, u):
                if later(i):
                    dve.wait_ge(s_rd, 2 * i + u - 1)
                for n in range(4):
                    dve.wait_ge(s_qk, 4 * (2 * i + u) + n + 1)
                    out = (rope_a, rope_b)[n % 2][:, u, n // 2, :].rearrange("p (w n) -> p w n", w=WIN)
                    dve.scalar_tensor_tensor(
                        out=out, in0=ps[:, 1 + n, :].rearrange("p (w n) -> p w n", w=WIN),
                        scalar=W("bias")[:, n:n + 1], in1=over_windows(("cos", "sin")[n % 2]),
                        op0=ALU.add, op1=ALU.mult).then_inc(s_ra, 1)
            pipelined(dve, NROW, [(0, rotated)])

        @block.gpsimd
        def _(pool):
            def sums(i, u):
                pool.wait_ge(s_ra, 4 * (2 * i + u) + 4)
                for n, dst in enumerate((qT, kT)):
                    out = dst[:, :, :].rearrange("p (i u) n -> p i u n", u=2)[:, i, u]
                    ins = pool.tensor_tensor(out, rope_a[:, u, n], rope_b[:, u, n], ALU.add)
                ins.then_inc(s_rd, 1)
            pipelined(pool, NROW, [(0, sums)])

    q_diag = sb("q_diag", [P, 4, B, C])
    k_diag = sb("k_diag", [P, 4, NH, C])
    x_twice = sb("x_twice", [P, 4, 2, C])
    scores = sb("scores", [P, 4, NH * C])
    probs = sb("probs", [P, 4, NH * C])
    probsT = sb("probsT", [P, 4, NH * C])
    V1 = HD + 1
    v_diag = sb("v_diag", [P, 4, HP, B, 2, V1])
    row_max = sb("row_max", [P, 4, NH])
    row_inv = sb("row_inv", [P, 2, 2, NH])
    att = sb("att", [P, 2, 2, NH, HD])
    attT = sb("attT", [P, 2, P])
    proj = sb("proj", [P, NROW, WIN, C])
    warm = sb("warm_exp", [P, 1])
    s_op = sem("window_operands")
    s_xt = sem("window_x_twice")
    s_opu = sem("window_operands_used")
    s_vu = sem("window_x_twice_used")
    s_s = sem("window_scores")
    s_v = sem("window_values")
    s_vd = sem("window_v_diag")
    s_mx = sem("window_max")
    s_sub = sem("window_sub")
    s_e = sem("window_exp")
    s_pt = sem("window_probsT")
    s_ptc = sem("window_probsT_copied")
    s_pv = sem("window_pv")
    s_iv = sem("window_inverse")
    s_at = sem("window_att")
    s_ot = sem("window_attT")
    s_otc = sem("window_attT_copied")
    s_pr = sem("window_projected")
    s_prc = sem("window_projected_copied")
    s_init = sem("window_init")
    s_passed = sem("image_waits_passed")
    s_out = [sem("h_img_stored_0"), sem("h_img_stored_1")]
    turns = NW // 4
    pair = lambda i, lane: 2 * i + lane
    win = lambda i, lane, u: 4 * i + 2 * lane + u

    def window(t, i, lane, u):
        v = t[:, :, :].rearrange("p r (w n) -> p (r w) n", n=C).rearrange("p (i k) n -> p i k n", k=4)
        return v[:, i, 2 * lane + u].rearrange("p (a n) -> p a n", a=1)

    with nc.Block() as block:
        @block.gpsimd
        def _(pool):
            batches = W("batch_of").rearrange("p (b n) -> p b n", n=1).broadcast_to([P, B, C])
            heads = W("head_of").rearrange("p (h n) -> p h n", n=1).broadcast_to([P, NH, C])
            with pool.Fori(0, turns) as i:
                for lane in range(2):
                    for u in range(2):
                        k = 2 * lane + u
                        pool.wait_ge(s_opu, win(i, lane, u) + 1)
                        pool.tensor_tensor(q_diag[:, k], window(qT, i, lane, u).broadcast_to([P, B, C]), batches,
                                           ALU.mult)
                        pool.tensor_tensor(k_diag[:, k], window(kT, i, lane, u).broadcast_to([P, NH, C]), heads,
                                           ALU.mult).then_inc(s_op, 1)
            finish["gpsimd"](pool)

        @block.tensor
        def _(pe):
            pe.sem_inc(s_opu, 4)
            pe.sem_inc(s_vu, 2)
            pe.sem_inc(s_prc, 2)
            pe.wait_ge(s_init, 2)

            def product(i, lane):
                for u in range(2):
                    k = 2 * lane + u
                    pe.wait_ge(s_op, win(i, lane, u) + 1)
                    pe.matmul(ps[:, k, :], q_diag[:, k].rearrange("p b n -> p (b n)"),
                              k_diag[:, k].rearrange("p h n -> p (h n)"), start=True, stop=True).then_inc(s_s, 1)

            def values(i, lane):
                pe.wait_ge(s_xt, win(i, lane, 0) + 2)
                for u in range(2):
                    ins = pe.matmul(ps[:, 4 + lane, u * P:(u + 1) * P],
                                    x_twice[:, 2 * lane + u].rearrange("p a n -> p (a n)"), W("wv"),
                                    start=True, stop=True)
                ins.then_inc(s_v, 1)

            def transposes(i, lane):
                for u in range(2):
                    k = 2 * lane + u
                    pe.wait_ge(s_e, win(i, lane, u) + 1)
                    for n in range(HP):
                        ins = pe.transpose(ps[:, k, n * P:(n + 1) * P], probs[:, k, n * P:(n + 1) * P], ident)
                    ins.then_inc(s_pt, 1)

            def outputs(i, lane):
                pe.wait_ge(s_vd, pair(i, lane) + 1)
                pe.wait_ge(s_prc, pair(i, lane) + 1)
                for u in range(2):
                    k = 2 * lane + u
                    pe.wait_ge(s_ptc, win(i, lane, u) + 1)
                    for n in range(HP):
                        ins = pe.matmul(ps[:, 6 + lane, (u * HP + n) * 4 * V1:(u * HP + n + 1) * 4 * V1],
                                        probsT[:, k, n * P:(n + 1) * P],
                                        v_diag[:, k, n].rearrange("p b h e -> p (b h e)"), start=True, stop=True)
                ins.then_inc(s_pv, 1)

            def turned(i, lane):
                pe.wait_ge(s_at, pair(i, lane) + 1)
                pe.transpose(ps[:, 6 + lane, 3 * P:4 * P], att[:, lane].rearrange("p u h d -> p (u h d)"),
                             ident).then_inc(s_ot, 1)

            def projected(i, lane):
                pe.wait_ge(s_otc, pair(i, lane) + 1)
                pe.matmul(ps[:, 6 + lane, 0:P], attT[:, lane], W("wproj"), start=True, stop=True).then_inc(s_pr, 1)
            pipelined(pe, 2 * turns, [(1, transposes), (0, product), (2, turned), (1, outputs), (0, values),
                                      (2, projected)])

        @block.vector
        def _(dve):
            dve.memset(v_diag[:], 0.0).then_inc(s_init, 1)
            dve.wait_ge(s_init, 1)
            for hp in range(2):
                ins = dve.memset(v_diag[hp * C:(hp + 1) * C, :, :, :, hp, HD:V1], 1.0)
            ins.then_inc(s_init, 1)
            dve.wait_ge(s_init, 2)
            bias_v = W("bias_v").rearrange("p (b n h d) -> p b n h d", b=B, n=HP, h=2)

            def softmax(i, lane):
                s3 = lambda k: ps[:, k, :].rearrange("p (h n) -> p h n", h=NH)
                for u in range(2):
                    dve.wait_ge(s_s, win(i, lane, u) + 1)
                    dve.sem_inc(s_opu, 1)
                    k = 2 * lane + u
                    dve.tensor_reduce(row_max[:, k], s3(k), AX.X, ALU.max).then_inc(s_mx, 1)
                for u in range(2):
                    dve.wait_ge(s_mx, win(i, lane, u) + 1)
                    k = 2 * lane + u
                    wide = row_max[:, k].rearrange("p (h n) -> p h n", n=1).broadcast_to([P, NH, C])
                    dve.tensor_tensor(scores[:, k].rearrange("p (h n) -> p h n", h=NH), s3(k), wide,
                                      ALU.subtract).then_inc(s_sub, 1)

            def values(i, lane):
                dve.wait_ge(s_v, pair(i, lane) + 1)
                dve.sem_inc(s_vu, 1)
                for u in range(2):
                    for hp in range(2):
                        rows = slice(hp * C, (hp + 1) * C)
                        src = ps[rows, 4 + lane, u * P:(u + 1) * P].rearrange("p (b n h d) -> p b n h d", b=B, n=HP, h=2)
                        ins = dve.tensor_tensor(
                            v_diag[rows, 2 * lane + u, :, :, hp, 0:HD].rearrange("p n b d -> p b n d"),
                            src[:, :, :, hp], bias_v[rows, :, :, hp], ALU.add)
                ins.then_inc(s_vd, 1)

            def normalise(i, lane):
                dve.wait_ge(s_pv, pair(i, lane) + 1)
                out = ps[:, 6 + lane, 0:2 * HP * 4 * V1].rearrange("p (n b h e) -> p n b h e", n=2 * HP, b=B, h=2)
                for b in range(B):
                    rows = slice(b * C, (b + 1) * C)
                    ins = dve.reciprocal(row_inv[rows, lane].rearrange("p u (n h) -> p (u n) h", h=2),
                                         out[rows, :, b, :, HD])
                ins.then_inc(s_iv, 1)
                dve.wait_ge(s_iv, pair(i, lane) + 1)
                for b in range(B):
                    rows = slice(b * C, (b + 1) * C)
                    inv = row_inv[rows, lane].rearrange("p u (n h e) -> p (u n) h e", h=2, e=1)
                    ins = dve.tensor_tensor(att[rows, lane].rearrange("p u (n h) d -> p (u n) h d", h=2),
                                            out[rows, :, b, :, 0:HD], inv.broadcast_to([C, 2 * HP, 2, HD]), ALU.mult)
                ins.then_inc(s_at, 1)

            def projected(i, lane):
                dve.wait_ge(s_pr, pair(i, lane) + 1)
                dst = proj[:, :, :, :].rearrange("p r w c -> p (r w c)").rearrange("p (i k n) -> p i k n", k=2, n=2 * C)
                dve.tensor_tensor(dst[:, i, lane], ps[:, 6 + lane, 0:P], W("bias_proj"), ALU.add).then_inc(s_prc, 1)
            pipelined(dve, 2 * turns, [(0, softmax), (1, normalise), (0, values), (2, projected)])
            finish["vector"](dve)

        @block.scalar
        def _(act):
            act.activation(warm[:], ident[:, 0:1], ACT.Exp)

            def twice(i, lane):
                for u in range(2):
                    k = 2 * lane + u
                    if u == 0:
                        act.wait_ge(s_vu, pair(i, lane) + 1)
                    act.activation(x_twice[:, k], window(xT, i, lane, u).broadcast_to([P, 2, C]),
                                   ACT.Copy).then_inc(s_xt, 1)

            def exponentials(i, lane):
                for u in range(2):
                    k = 2 * lane + u
                    act.wait_ge(s_sub, win(i, lane, u) + 1)
                    act.activation(probs[:, k], scores[:, k], ACT.Exp, scale=SCALE).then_inc(s_e, 1)

            def probabilities(i, lane):
                for u in range(2):
                    k = 2 * lane + u
                    act.wait_ge(s_pt, win(i, lane, u) + 1)
                    act.activation(probsT[:, k], ps[:, k, :], ACT.Copy).then_inc(s_ptc, 1)

            def turned(i, lane):
                act.wait_ge(s_ot, pair(i, lane) + 1)
                act.activation(attT[:, lane], ps[:, 6 + lane, 3 * P:4 * P], ACT.Copy).then_inc(s_otc, 1)
            pipelined(act, 2 * turns, [(1, probabilities), (0, twice), (2, turned), (0, exponentials)])
            finish["scalar"](act)

        @block.sync
        def _(sp):
            def store(i, k):
                wait_alone(sp, s_prc, (2 * i + k + 1) * (WIN // 2) + 2, s_passed)
                src = proj[:, :, :, :].rearrange("p (i k) w c -> p i k w c", k=2)
                for b in range(B):
                    dst = h_img[b].rearrange("(i k y w x) c -> i k y x w c", k=2, y=WIN, w=WIN, x=WIN)
                    for y in range(WIN):
                        p0 = b * C + y * WIN
                        sp.dma_start(dst[i, k, y], src[p0:p0 + WIN, i, k]).then_inc(s_out[k], 16)

            def reload(i, k):
                wait_alone(sp, s_out[k], 16 * B * WIN * i + 16 * B * WIN, s_passed)
                for b in range(B):
                    rows = hh[:, 0:NT_IMG, b, :].rearrange("p (i k t) c -> p i k t c", k=2, t=TPC)[:, i, k]
                    src = h_img[b].rearrange("(i k t p) c -> p i k t c", p=P, k=2, t=TPC)[:, i, k]
                    sp.dma_start(rows, src).then_inc(s_h, 16)
            pipelined(sp, NROW, [(0, store), (1, reload)])
            sp.wait_ge(s_h, 16 * B * NROW)



def text_field(nc, ctx, sem, ps, bytes_rep, positions_rep, wt, cols, hh):
    TT = S_TXT // P
    TILES = B * TT
    E = C + 4
    TWO_PI = 6.283185
    K1, K2, K3 = 7, 5, 3
    sb = lambda n, s, d=F32: ctx.enter_context(nc.sbuf_tensor(n, s, d))
    W = lambda n: cols.view(wt, n)
    byte = sb("byte", [P, B, S_TXT], I32)
    pos = sb("pos", [P, B, S_TXT])
    PAIRS = (K1 + 1) // 2
    onehot = sb("onehot", [P, B, S_TXT + K1])
    conv1 = sb("conv1", [P, B, S_TXT + K2 - 1])
    conv2 = sb("conv2", [C, B, S_TXT + K3 - 1])
    ctxw = sb("context", [P, TILES])
    gath = sb("gathered", [P, TILES, E])
    amp_scale = sb("amp_scale", [P, TILES])
    center = sb("center", [P, TILES])
    phase = sb("phase", [P, TILES])
    inv_width = sb("inv_width", [P, NS, TILES])
    sw2 = sb("scale_weight_squared", [P, NS])
    z = sb("z", [P, 2, NS, S_TXT])
    amps = sb("amps", [P, NS, TILES, C])
    turns = sb("turns", [P, NS, S_TXT])
    env = sb("envelope", [P, TT, B, NS, S_TXT])
    wave = sb("wave", [P, TT, B, NS, S_TXT])
    packet = env
    field = z[0:C, 0]

    s_in = sem("text_loaded")
    s_cl = sem("text_cleared")
    s_oh = sem("onehot_ready")
    s_c1 = sem("conv1_ready")
    s_g1 = sem("gelu1_ready")
    s_c2 = sem("conv2_ready")
    s_g2 = sem("gelu2_ready")
    s_c3 = sem("conv3_ready")
    s_ga = sem("gather_ready")
    s_gc = sem("gathered_copied")
    s_sg = sem("sigmoids_ready")
    s_sc = sem("text_scalars")
    s_z = sem("z_ready")
    s_a = sem("turns_shifted")
    s_d = sem("turns_ready")
    s_r = sem("wave_arg_ready")
    s_sq = sem("z_squared")
    s_ex = sem("envelope_ready")
    s_si = sem("sine_ready")
    s_am = sem("amplitudes_ready")
    s_pk = sem("packet_ready")
    s_pm = sem("packet_summed")
    s_f = sem("field_copied")
    s_fa = sem("field_copied_act")
    s_ft = sem("field_transposed")
    tile = lambda st, b: b * TT + st

    with nc.Block() as block:
        @block.sync
        def _(sp):
            sp.dma_start(byte[:, :, :], bytes_rep).then_inc(s_in, 16)
            sp.dma_start(pos[:, :, :], positions_rep).then_inc(s_in, 16)

        @block.vector
        def _(dve):
            step = Steps(dve, s_sc)
            dve.memset(onehot[:], 0.0).then_inc(s_cl, 1)
            dve.memset(conv1[:], 0.0).then_inc(s_cl, 1)
            dve.memset(conv2[:], 0.0).then_inc(s_cl, 1)
            dve.wait_ge(s_in, 32)
            dve.wait_ge(s_cl, 3)
            for half in range(2):
                rows, at = slice(half * C, (half + 1) * C), K1 // 2 - half
                dve.tensor_scalar(onehot[rows, :, at:at + S_TXT], byte[rows], W("iota")[rows], None,
                                  ALU.is_equal).then_inc(s_oh, 1)
            for half in range(2):
                dve.wait_ge(s_ga, half + 1)
                n = TILES // 2
                dve.tensor_copy(gath[:, half * n:(half + 1) * n], ps[:, 2 + half, 0:n * E].rearrange(
                    "p (t e) -> p t e", e=E)).then_inc(s_gc, 1)
            dve.wait_ge(s_gc, 2)
            lp = lambda k: gath[:, :, C + k]
            step.tick(dve.scalar_tensor_tensor(center[:], lp(0), 0.05, W("byte_pos"), ALU.mult, ALU.add))
            step.tick(dve.tensor_scalar(phase[:], lp(3), 0.5, 0.25, ALU.mult, ALU.add))
            step.tick(dve.tensor_tensor(sw2[:], W("scale_weights"), W("scale_weights"), ALU.mult))
            step.tick(dve.scalar_tensor_tensor(inv_width[:, 0], lp(1), -1.0, lp(1), ALU.mult, ALU.max))
            step.hold()
            for s in reversed(range(NS)):
                step.tick(dve.tensor_scalar(inv_width[:, s], inv_width[:, 0], W("widths")[:, s:s + 1], 1e-5,
                                            ALU.mult, ALU.add))
            step.hold()
            step.tick(dve.reciprocal(inv_width[:], inv_width[:]))
            step.hold()

            def arguments(n):
                st, b = divmod(n, B)
                t = tile(st, b)
                if n >= 2:
                    dve.wait_ge(s_sq, n - 1)
                if n >= 1:
                    dve.wait_ge(s_r, n)
                for s in range(NS):
                    ins = dve.tensor_scalar(z[:, b, s], pos[:, b], center[:, t:t + 1], inv_width[:, s, t:t + 1],
                                            ALU.subtract, ALU.mult)
                ins.then_inc(s_z, 1)
                dve.wait_ge(s_z, n + 1)
                dve.tensor_scalar(turns[:], z[:, b], phase[:, t:t + 1], None, ALU.add).then_inc(s_a, 1)
                dve.wait_ge(s_a, n + 1)
                dve.tensor_scalar(wave[:, st, b], turns[:], ROUND, ROUND, ALU.add,
                                  ALU.subtract).then_inc(s_d, 1)
                dve.wait_ge(s_d, n + 1)
                dve.tensor_tensor(wave[:, st, b], turns[:], wave[:, st, b], ALU.subtract).then_inc(s_r, 1)

            def amplitudes():
                dve.wait_ge(s_sg, 2)
                step.tick(dve.tensor_tensor(amp_scale[:], amp_scale[:], ctxw[:], ALU.mult))
                step.hold()
                wide = amp_scale[:].rearrange("p (t c) -> p t c", c=1).broadcast_to([P, TILES, C])
                step.tick(dve.tensor_tensor(gath[:, :, 0:C], gath[:, :, 0:C], wide, ALU.mult))
                step.hold()
                for s in range(NS):
                    ins = dve.tensor_scalar(amps[:, s], gath[:, :, 0:C], sw2[:, s:s + 1], None, ALU.mult)
                ins.then_inc(s_am, 1)

            def packets(n):
                st, b = divmod(n, B)
                dve.wait_ge(s_si, n + 1)
                dve.wait_ge(s_ex, n + 1)
                dve.tensor_tensor(packet[:, st, b], env[:, st, b], wave[:, st, b], ALU.mult).then_inc(s_pk, 1)
            for n in range(5):
                arguments(n)
            amplitudes()
            for n in range(5, TILES):
                arguments(n)
                packets(n - 5)
            for n in range(TILES - 5, TILES):
                packets(n)
            dve.wait_ge(s_pm, TILES)
            dve.tensor_copy(field[:, 0], ps[0:C, 0, :]).then_inc(s_f, 1)
            for b in range(B):
                dve.wait_ge(s_ft, b + 1)
                dve.tensor_copy(hh[:, NT_IMG:NT, b, :], ps[:, 2 + b, 0:TT * C].rearrange("p (t c) -> p t c", c=C))

        @block.tensor
        def _(pe):
            pe.wait_ge(s_oh, 2)
            for t in range(TILES):
                b, st = divmod(t, TT)
                ins = pe.matmul(ps[:, 2 + b, st * E:(st + 1) * E],
                                onehot[0:C, b, K1 // 2 + st * P:K1 // 2 + (st + 1) * P], W("embed"), start=True, stop=True)
                if st == TT - 1:
                    ins.then_inc(s_ga, 1)
            w1 = W("conv1").rearrange("i (k o) -> i k o", k=PAIRS)
            for b in range(B):
                for k in range(PAIRS):
                    ins = pe.matmul(ps[:, b, :], w1[:, k], onehot[:, b, 2 * k:2 * k + S_TXT], start=k == 0,
                                    stop=k == PAIRS - 1)
                ins.then_inc(s_c1, 1)
            w2 = W("conv2").rearrange("i (k o) -> i k o", k=K2)
            for b in range(B):
                pe.wait_ge(s_g1, b + 1)
                for k in range(K2):
                    ins = pe.matmul(ps[0:C, 4 + b, :], w2[:, k], conv1[:, b, k:k + S_TXT], start=k == 0, stop=k == K2 - 1)
                ins.then_inc(s_c2, 1)
            pe.wait_ge(s_g2, B)
            for t in range(TILES):
                b, st = divmod(t, TT)
                for k in range(K3):
                    ins = pe.matmul(ps[:, 6, t:t + 1], conv2[:, b, k + st * P:k + (st + 1) * P], W("conv3")[:, k:k + 1],
                                    start=k == 0, stop=k == K3 - 1)
            ins.then_inc(s_c3, 1)
            pe.wait_ge(s_am, 1)
            for st in range(TT):
                for b in range(B):
                    pe.wait_ge(s_pk, B * st + b + 1)
                    for s in range(NS):
                        ins = pe.matmul(ps[0:C, b, :], amps[:, s, tile(st, b)], packet[:, st, b, s],
                                        start=st == 0 and s == 0, stop=st == TT - 1 and s == NS - 1)
                    ins.then_inc(s_pm, 1)
            for b in range(B):
                pe.wait_ge((s_f, s_fa)[b], 1)
                for p in range(TT):
                    ins = pe.transpose(ps[:, 2 + b, p * C:(p + 1) * C], field[:, b, p * P:(p + 1) * P], W("ident"))
                ins.then_inc(s_ft, 1)

        @block.scalar
        def _(act):
            def square(n):
                act.wait_ge(s_z, n + 1)
                act.activation(env[:, n // B, n % B], z[:, n % B], ACT.Square).then_inc(s_sq, 1)

            def envelope(n):
                act.wait_ge(s_sq, n + 1)
                act.activation(env[:, n // B, n % B], env[:, n // B, n % B], ACT.Exp, scale=-0.5).then_inc(s_ex, 1)

            def sine(n):
                act.wait_ge(s_r, n + 1)
                act.activation(wave[:, n // B, n % B], wave[:, n // B, n % B], ACT.Sin, scale=TWO_PI).then_inc(s_si, 1)
            act.wait_ge(s_cl, 3)
            for b in range(B):
                act.wait_ge(s_c1, b + 1)
                act.activation(conv1[:, b, K2 // 2:K2 // 2 + S_TXT], ps[:, b, :], ACT.Gelu,
                               bias=W("bias1")).then_inc(s_g1, 1)
            square(0)
            for b in range(B):
                act.wait_ge(s_c2, b + 1)
                act.activation(conv2[:, b, K3 // 2:K3 // 2 + S_TXT], ps[0:C, 4 + b, :], ACT.Gelu,
                               bias=W("bias2")).then_inc(s_g2, 1)
            square(1)
            act.wait_ge(s_gc, 2)
            act.wait_ge(s_c3, 1)
            act.activation(ctxw[:], ps[:, 6, 0:TILES], ACT.Sigmoid, bias=W("bias3")).then_inc(s_sg, 1)
            act.activation(amp_scale[:], gath[:, :, C + 2], ACT.Sigmoid).then_inc(s_sg, 1)
            for group in ((2, 3), (4, 5, 6, 7)):
                for n in group:
                    square(n)
                    for k in {2: (0,), 3: (1, 2, 3)}.get(n, (n,)):
                        envelope(k)
                for n in range(4) if group[0] == 2 else group:
                    sine(n)
            act.wait_ge(s_pm, TILES)
            act.activation(field[:, 1], ps[0:C, 1, :], ACT.Copy).then_inc(s_fa, 1)


def text_columns(i):
    c = Columns()
    rep = lambda a: np.tile(np.asarray(a).reshape(1, -1), (P, 1))
    w1 = i["L0_txt_w1"].transpose(2, 1, 0)
    w1 = np.concatenate([w1, np.zeros_like(w1[:1])]).reshape(-1, 2 * C, w1.shape[2])
    c.add("conv1", (0, P), w1.transpose(1, 0, 2).reshape(P, -1))
    c.add("ident", (0, C), np.eye(C, dtype=np.float32))
    c.add("conv2", (0, P), i["L0_txt_w2"].transpose(1, 2, 0).reshape(P, -1))
    c.add("conv3", (0, C), i["L0_txt_w3"][0])
    c.add("embed", (0, C), np.concatenate([i["L0_txt_emb"], i["L0_txt_locality_shapes"]], 1))
    c.add("bias1", (0, P), i["L0_txt_b1"][:, None])
    c.add("bias2", (0, C), i["L0_txt_b2"][:, None])
    c.add("bias3", (0, P), rep(i["L0_txt_b3"]))
    c.add("widths", (0, P), rep(i["L0_txt_multiscale_widths"]))
    c.add("scale_weights", (0, P), rep(i["L0_txt_scale_weights"]))
    c.add("iota", (0, P), np.tile(np.arange(C, dtype=np.float32), 2)[:, None])
    at = np.linspace(0.0, 1.0, S_TXT, dtype=np.float32).reshape(-1, P).T
    c.add("byte_pos", (0, P), np.tile(at, (1, B)))
    return c



class Norm:

    PARTS = 3
    EPS = 1e-5

    def __init__(self, nc, ctx, name):
        sb = lambda n, s: ctx.enter_context(nc.sbuf_tensor(f"{name}_{n}", s, F32))
        self.nc = nc
        self.names = iter(range(100))
        self.mean = sb("mean", [P, NT, B])
        self.centred = sb("centred", [P, NT, B, C])
        self.rstd = sb("rstd", [P, NT, B])
        sem = lambda n: ctx.enter_context(nc.semaphore(f"{name}_{n}"))
        self.s_dve, self.s_c, self.s_sq, self.s_var, self.s_sd = map(sem, ("dve", "centred", "squared", "var", "dev"))

    def wide(self, a, part):
        n = NT // self.PARTS * B
        v = a[:, :, :].rearrange("p t b -> p (t b)")[:, part * n:(part + 1) * n]
        return v.rearrange("p (n c) -> p n c", c=1).broadcast_to([P, n, C])

    def rows(self, a, part):
        n = NT // self.PARTS * B
        return a[:, :, :, :].rearrange("p t b c -> p (t b) c")[:, part * n:(part + 1) * n]

    def finish(self, runs, finishes):
        PT = self.PARTS
        flat = self.rstd[:, :, :].rearrange("p t b -> p (t b)")
        with self.nc.Block() as block:
            @block.vector
            def _(dve):
                dve.tensor_scalar(flat, flat, 1.0 / C, self.EPS, ALU.mult, ALU.add).then_inc(self.s_var, 1)
                dve.wait_ge(self.s_sd, PT * runs + finishes + 1)
                dve.reciprocal(flat, flat).then_inc(self.s_dve, 1)

            @block.scalar
            def _(act):
                act.wait_ge(self.s_var, PT * runs + finishes + 1)
                act.activation(flat, flat, ACT.Sqrt).then_inc(self.s_sd, 1)

    def run(self, src, turn):
        PT, n = self.PARTS, NT // self.PARTS * B
        small = lambda a, k: a[:, :, :].rearrange("p t b -> p (t b)")[:, k * n:(k + 1) * n]
        with self.nc.sbuf_tensor(f"norm_square_{next(self.names)}", [P, NT, B, C], F32) as square, \
                self.nc.Block() as block:
            @block.vector
            def _(dve):
                step = Steps(dve, self.s_dve)
                step.base = 4 * PT * turn
                for k in range(PT):
                    step.tick(dve.tensor_reduce(small(self.mean, k), self.rows(src, k), AX.X, ALU.add))
                step.hold()
                for k in range(PT):
                    step.tick(dve.tensor_scalar(small(self.mean, k), small(self.mean, k), 1.0 / C, None, ALU.mult))
                step.hold()
                for k in range(PT):
                    dve.tensor_tensor(self.rows(self.centred, k), self.rows(src, k), self.wide(self.mean, k),
                                      ALU.subtract).then_inc(self.s_c, 1)
                for k in range(PT):
                    dve.wait_ge(self.s_sq, PT * turn + k + 1)
                    step.tick(dve.tensor_reduce(small(self.rstd, k), self.rows(square, k), AX.X, ALU.add))
                step.hold()
                for k in range(PT):
                    dve.tensor_scalar(small(self.rstd, k), small(self.rstd, k), 1.0 / C, self.EPS, ALU.mult,
                                      ALU.add).then_inc(self.s_var, 1)
                for k in range(PT):
                    dve.wait_ge(self.s_sd, PT * turn + k + 1)
                    step.tick(dve.reciprocal(small(self.rstd, k), small(self.rstd, k)))

            @block.scalar
            def _(act):
                for k in range(PT):
                    act.wait_ge(self.s_c, PT * turn + k + 1)
                    act.activation(self.rows(square, k), self.rows(self.centred, k), ACT.Square).then_inc(self.s_sq, 1)
                for k in range(PT):
                    act.wait_ge(self.s_var, PT * turn + k + 1)
                    act.activation(small(self.rstd, k), small(self.rstd, k), ACT.Sqrt).then_inc(self.s_sd, 1)



class Layer:

    QK_PEAK = 2.0 ** 14

    HP = NH // 2
    V1 = HD + 1
    VP = 2 * HD + 1
    ITERS = 6
    U = 3

    def __init__(self, nc, ctx, ps, hh, y, att, ff):
        self.nc, self.ctx, self.ps, self.hh = nc, ctx, ps, hh
        self.W = lambda n: att[1].view(att[0], n)
        self.W_ff = lambda n: ff[1].view(ff[0], n)
        self.y = y
        self.scale = self.sb("qk_scale", [P, 2])
        self.unscale = self.sb("qk_unscale", [P, 1])
        self.last = self.sb("is_last", [P, 1])
        self.sems = {}

    def sb(self, n, s, ctx=None, dtype=F32):
        return (ctx or self.ctx).enter_context(self.nc.sbuf_tensor(n, s, dtype))

    def norm_sems(self):
        return (self.sem("norm_" + n) for n in ("sum", "part_centred", "part_squared", "squares_summed"))

    def sem(self, name):
        if name not in self.sems:
            self.sems[name] = self.ctx.enter_context(self.nc.semaphore(name))
        return self.sems[name]


def chunk_of(t, i, u):
    return t[:, :, :, :].rearrange("p (i u t) b c -> p i u t b c", u=Layer.U, t=TPC)[:, i, u]


def cols_of(t, i, u):
    return t[:, :].rearrange("p (i u n) -> p i u n", u=Layer.U, n=CHUNK)[:, i, u]


def normed(eng, norm, out, i, u):
    r = norm.rstd[:, :, :].rearrange("p (i u t) (b c) -> p i u t b c", u=Layer.U, t=TPC, c=1)[:, i, u]
    return eng.tensor_tensor(out, chunk_of(norm.centred, i, u), r.broadcast_to([P, TPC, B, C]), ALU.mult)


HALF = CHUNK // 2
TPH = HALF // P


def half_of(t, i, lane):
    return t[:, :, :, :].rearrange("p (i k t) b c -> p i k t b c", k=2, t=TPH)[:, i, lane]


def half_normed(eng, norm, out, i, lane):
    r = norm.rstd[:, :, :].rearrange("p (i k t) (b c) -> p i k t b c", k=2, t=TPH, c=1)[:, i, lane]
    return eng.tensor_tensor(out, half_of(norm.centred, i, lane), r.broadcast_to([P, TPH, B, C]), ALU.mult)


def later(i):
    return not (isinstance(i, int) and i == 0)


def first_norm(nc, ctx, norm, y, turn):
    s_y = ctx.enter_context(nc.semaphore("y_ready"))
    with nc.Block() as block:
        @block.vector
        def _(dve):
            with dve.Fori(0, NCH // Layer.U) as i:
                for u in range(Layer.U):
                    normed(dve, norm, chunk_of(y, i, u), i, u).then_inc(s_y, 1)
            dve.wait_ge(s_y, NCH)


def project_values(L, turn, norm, xnT, V, V_padded):
    nc, ps, W = L.nc, L.ps, L.W
    sem = L.sem
    s_n, s_t, s_xT = (sem("normed_" + n) for n in ("ready", "transposed", "xT_ready"))
    s_xu, s_v, s_vc = (sem("norm1_" + n) for n in ("xT_copied", "values", "values_copied"))
    s_most, s_all = sem("scale_most"), sem("lm_all_max")
    NU = 2 * NCH
    at_n = lambda i, lane: 2 * NU * turn + 2 * i + lane
    at = lambda i, lane: NU * turn + 2 * i + lane
    with ExitStack() as stage:
        most = L.sb("scale_most_of", [P, 4], stage)
        bound = L.sb("scale_bound", [P, 2], stage)
        xn = L.sb("xn", [P, 2, TPH, B, C], stage)
        xs = L.sb("xs", [P, 2, HALF], stage)
        with nc.Block() as block:
            @block.vector
            def _(dve):
                def normalise(i, lane):
                    if later(i):
                        dve.wait_ge(s_t, at_n(i, lane) - 1)
                    half_normed(dve, norm, xn[:, lane], i, lane).then_inc(s_n, 1)

                def values(i, lane):
                    dve.wait_ge(s_v, at(i, lane) + 1)
                    out = V[:, :, :, :, 0:2 * HD].rearrange("p (i k t) b n e -> p i k (t b n) e", k=2, t=TPH)[:, i, lane]
                    dve.tensor_copy(out, ps[:, 2 + lane, 0:HALF].rearrange("p (n e) -> p n e", e=2 * HD)).then_inc(s_vc, 1)
                st = Steps(dve, sem("scale_dve"))
                st.enter(turn, 10)
                for k, w in enumerate(("wq", "wk")):
                    st.tick(dve.tensor_reduce(most[:, k:k + 1], W(w), AX.X, ALU.max, apply_absolute_value=True))
                for k, w in enumerate(("ln1_g", "ln1_b")):
                    st.tick(dve.tensor_reduce(most[:, 2 + k:3 + k], W(w), AX.X, ALU.max, apply_absolute_value=True))
                st.hold()
                st.tick(dve.scalar_tensor_tensor(most[:, 2:3], most[:, 2:3], float(C) ** 0.5, most[:, 3:4], ALU.mult,
                                                 ALU.add))
                st.hold()
                dve.tensor_scalar(most[:, 0:2], most[:, 0:2], most[:, 2:3], float(C), ALU.mult,
                                  ALU.mult).then_inc(s_most, 1)
                for pad in (0, NT + 1):
                    dve.memset(V_padded[:, pad], 0.0)
                dve.memset(V[:, :, :, :, 2 * HD:], 1.0)
                dve.wait_ge(s_all, 2 * turn + 1)
                st.tick(dve.tensor_scalar(bound[:], bound[:], 1e-15, None, ALU.max))
                st.hold()
                st.tick(dve.reciprocal(L.scale[:], bound[:]))
                st.tick(dve.tensor_tensor(L.unscale[:], bound[:, 0:1], bound[:, 1:2], ALU.mult))
                st.hold()
                st.tick(dve.tensor_scalar(L.scale[:], L.scale[:], L.QK_PEAK, None, ALU.mult))
                st.tick(dve.tensor_scalar(L.unscale[:], L.unscale[:], L.QK_PEAK ** -2, None, ALU.mult))
                st.leave(1)
                pipelined(dve, NU, [(0, normalise), (3, values)])

            @block.tensor
            def _(pe):
                def transposes(i, lane):
                    pe.wait_ge(s_n, at_n(i, lane) + 1)
                    if later(i):
                        pe.wait_ge(s_xT, at_n(i, lane) - 1)
                    for t in range(TPH):
                        ins = pe.transpose(ps[:, lane, t * P:(t + 1) * P], xn[:, lane, t].rearrange("p b c -> p (b c)"),
                                           W("ident"))
                    ins.then_inc(s_t, 1)

                def values(i, lane):
                    pe.wait_ge(s_xT, at_n(i, lane) + 1)
                    if later(i):
                        pe.wait_ge(s_vc, at(i, lane) - 1)
                    for t in range(TPH):
                        ins = pe.matmul(ps[:, 2 + lane, t * P:(t + 1) * P], xs[:, lane, t * P:(t + 1) * P], W("wv"),
                                        start=True, stop=True)
                    ins.then_inc(s_v, 1)
                pipelined(pe, NU, [(1, transposes), (2, values)])

            @block.scalar
            def _(act):
                def turned(i, lane):
                    act.wait_ge(s_t, at_n(i, lane) + 1)
                    if later(i):
                        act.wait_ge(s_v, at(i, lane) - 1)
                        act.wait_ge(s_xu, at(i, lane) - 1)
                    act.activation(xs[:, lane], ps[:, lane, 0:HALF], ACT.Identity, bias=W("ln1_b"),
                                   scale=W("ln1_g")).then_inc(s_xT, 1)
                pipelined(act, NU, [(0, turned)])

            @block.gpsimd
            def _(pool):
                wait_alone(pool, s_most, turn + 1, sem("waits_passed"))
                pool.partition_all_reduce(bound[:], most[:, 0:2], P, bass.bass_isa.ReduceOp.max).then_inc(s_all, 1)

                def kept(i, lane):
                    wait_alone(pool, s_xT, at_n(i, lane) + 1, sem("waits_passed"))
                    out = xnT[:, :].rearrange("p (i k n) -> p i k n", k=2, n=HALF)[:, i, lane]
                    pool.tensor_copy(out, xs[:, lane]).then_inc(s_xu, 1)
                pipelined(pool, NU, [(0, kept)])


def value_convolution(L, turn, V, res, banks):
    ps, W, sem = L.ps, L.W, L.sem
    s_c, s_cc = sem("conv_product"), sem("conv_copied")
    NU = NH * B
    bands = [W(n).rearrange("p (h n) -> p h n", h=NH) for n in ("band", "band_before", "band_after")]
    out_of = lambda n: ps[:, banks[n % len(banks)], 0:NT * HD].rearrange("p (t d) -> p t d", d=HD)

    def product(pe, n):
        h, b = divmod(n, B)
        p, q = divmod(h, 2)
        vals = V[:, :, b, p, q * HD:(q + 1) * HD]
        if n >= len(banks):
            pe.wait_ge(s_cc, NU * turn + n - len(banks) + 1)
        for k, (band, first) in enumerate(zip(bands, (1, 0, 2))):
            ins = pe.matmul(out_of(n), band[:, h], vals[:, first:first + NT], start=k == 0, stop=k == 2)
        ins.then_inc(s_c, 1)

    def copy(act, n):
        h, b = divmod(n, B)
        act.wait_ge(s_c, NU * turn + n + 1)
        act.activation(res[:, :, b, h * HD:(h + 1) * HD], out_of(n), ACT.Copy).then_inc(s_cc, 1)
    return product, copy


def landmarks(L, turn, xnT, V_padded, res, q12, k12, X_diag, XT_diag, Z, ZT, ZT_diag):
    convolve, keep = value_convolution(L, turn, V_padded, res, (6, 7))
    nc, ps, W, sem = L.nc, L.ps, L.W, L.sem
    G = B * NH
    SCALE = float(HD) ** -0.5
    STEPS, BEFORE_EXP = 26, 13
    s_s, s_pr, s_b, s_at, s_e, s_tr, s_mx, s_ar, s_m2, s_wd, s_p1 = (sem("lm_" + n) for n in (
        "dve", "projected", "diag", "scores", "exp", "transposed", "max", "all_max", "inputs", "by_head", "part1"))
    with ExitStack() as stage:
        xl = L.sb("xl", [P, M], stage)
        ql = L.sb("ql", [P, B, M], stage)
        kl = L.sb("kl", [P, M], stage)
        kd = L.sb("kl_unscaled", [P, B, NH, M], stage)
        X = L.sb("X", [P, NH, M], stage)
        twice = L.sb("lm_qk_twice", [P, 2, B, M], stage)
        wide_qk = L.sb("lm_qk_by_head", [P, 2, B, NH, M], stage)
        mx = L.sb("lm_max", [P, NH], stage)
        sm = L.sb("lm_sum", [P, 2, NH], stage)
        am = L.sb("lm_peak", [P, 2], stage)
        ar = L.sb("lm_peak_all", [P, 2], stage)
        inv = L.sb("lm_inv", [P, 1], stage)
        rows = lambda b: slice(b * M, (b + 1) * M)
        with nc.Block() as block:
            @block.vector
            def _(dve):
                st = Steps(dve, s_s)
                st.enter(turn, STEPS)
                st.tick(dve.tensor_reduce(xl[:], xnT[:, :].rearrange("p (m l) -> p m l", l=GROUP), AX.X, ALU.add))
                st.hold()
                dve.tensor_scalar(xl[:], xl[:], 1.0 / GROUP, None, ALU.mult).then_inc(s_m2, 1)
                dve.wait_ge(s_pr, turn + 1)
                for b in range(B):
                    st.tick(dve.tensor_scalar(ql[:, b], ps[:, 0, 0:M], SCALE, None, ALU.mult))
                st.tick(dve.tensor_copy(kl[:], ps[:, 1, 0:M]))
                for b in range(B):
                    st.tick(dve.tensor_scalar(twice[:, 0, b], ps[:, 0, (1 + b) * M:(2 + b) * M], L.scale[:, 0:1], SCALE,
                                              ALU.mult, ALU.mult))
                    st.tick(dve.tensor_scalar(twice[:, 1, b], ps[:, 1, (1 + b) * M:(2 + b) * M], L.scale[:, 1:2], SCALE,
                                              ALU.mult, ALU.mult))
                st.hold()
                units = W("unit_of").rearrange("p (g n) -> p g n", n=1).broadcast_to([P, G, M])
                over = lambda a: a.rearrange("p (g m) -> p g m", g=1).broadcast_to([P, G, M])
                every = lambda a: a.rearrange("p b h m -> p (b h) m")
                st.tick(dve.tensor_tensor(every(kd[:]), over(kl[:]), units, ALU.mult))
                st.hold()
                dve.sem_inc(s_b, 1)
                dve.wait_ge(s_at, turn + 1)
                wide = lambda a: a.rearrange("p (g n) -> p g n", n=1).broadcast_to([a.shape[0], NH, M])
                S = lambda b: ps[rows(b), 2 + b, :].rearrange("p (g n) -> p g n", n=M)
                for b in range(B):
                    st.tick(dve.tensor_reduce(mx[rows(b)], S(b), AX.X, ALU.max))
                st.hold()
                for b in range(B):
                    st.tick(dve.tensor_tensor(X[rows(b)], S(b), wide(mx[rows(b)]), ALU.subtract))
                assert st.n == BEFORE_EXP
                dve.wait_ge(s_e, turn + 1)
                st.tick(dve.tensor_reduce(sm[:, 0], X[:], AX.X, ALU.add))
                st.hold()
                st.tick(dve.reciprocal(sm[:, 1], sm[:, 0]))
                st.hold()
                st.tick(dve.tensor_tensor(X[:], X[:], wide(sm[:, 1]), ALU.mult))
                st.hold()
                both_x = X[:].rearrange("p h (n m) -> p h n m", n=1).broadcast_to([P, NH, B, M])
                batches = W("batch_of").rearrange("p (h b m) -> p h b m", h=1, m=1).broadcast_to([P, NH, B, M])
                dve.tensor_tensor(X_diag[:], both_x, batches, ALU.mult).then_inc(s_mx, 1)
                st.tick(dve.tensor_reduce(sm[:, 0], X[:], AX.X, ALU.add, apply_absolute_value=True))
                dve.wait_ge(s_tr, turn + 1)
                for k in range(2):
                    st.tick(dve.tensor_copy(XT_diag[:, 4 * k:4 * k + 4], ps[:, 4 + k, :].rearrange(
                        "p (h b m) -> p h b m", b=B, m=M)))
                st.hold()
                st.tick(dve.tensor_reduce(sm[:, 1], XT_diag[:].rearrange("p h b m -> p h (b m)"), AX.X, ALU.add,
                                          apply_absolute_value=True))
                st.hold()
                dve.tensor_reduce(am[:], sm[:], AX.X, ALU.max).then_inc(s_mx, 1)
                dve.wait_ge(s_ar, 2 * turn + 2)
                st.tick(dve.tensor_tensor(inv[:], ar[:, 0:1], ar[:, 1:2], ALU.mult))
                st.hold()
                st.tick(dve.reciprocal(inv[:], inv[:]))
                st.hold()
                for b in range(B):
                    st.tick(dve.tensor_scalar(Z[rows(b)], XT_diag[rows(b), :, b], inv[rows(b)], None, ALU.mult))
                st.tick(dve.tensor_scalar(ZT[:], X[:], inv[:], None, ALU.mult))
                dve.wait_ge(s_mx, 2 * turn + 2)
                st.tick(dve.tensor_scalar(ZT_diag[:], X_diag[:], inv[:], None, ALU.mult))
                st.leave(1)

            @block.gpsimd
            def _(pool):
                wait_alone(pool, s_b, turn + 1, L.sem("waits_passed"))
                heads = W("head_of").rearrange("p (h n) -> p h n", n=1).broadcast_to([P, NH, M])
                for k in range(2):
                    for b in range(B):
                        ins = pool.tensor_tensor(wide_qk[:, k, b], twice[:, k, b].rearrange(
                            "p (h m) -> p h m", h=1).broadcast_to([P, NH, M]), heads, ALU.mult)
                    ins.then_inc(s_wd, 1)
                for k, parts in enumerate((q12, k12)):
                    wait_alone(pool, s_p1, 2 * turn + k + 1, L.sem("waits_passed"))
                    wait_alone(pool, s_wd, 2 * turn + k + 1, L.sem("waits_passed"))
                    pool.tensor_tensor(parts[:, 1], wide_qk[:, k], parts[:, 0], ALU.subtract)
                wait_alone(pool, s_mx, 2 * turn + 2, L.sem("waits_passed"))
                pool.partition_all_reduce(ar[:], am[:], P, bass.bass_isa.ReduceOp.max).then_inc(s_ar, 1)

            @block.scalar
            def _(act):
                for n in range(7):
                    keep(act, n)
                act.wait_ge(s_s, turn * STEPS + BEFORE_EXP)
                act.activation(X[:], X[:], ACT.Exp).then_inc(s_e, 1)
                for k, parts in enumerate((q12, k12)):
                    keep(act, 7 + k)
                    act.wait_ge(s_wd, 2 * turn + k + 1)
                    act.activation(parts[:, 0], wide_qk[:, k], ACT.Copy).then_inc(s_p1, 1)
                for n in range(9, NH * B):
                    keep(act, n)

            @block.tensor
            def _(pe):
                for n in range(3):
                    convolve(pe, n)
                pe.wait_ge(s_m2, turn + 1)
                pe.matmul(ps[:, 0, 0:M], W("wq"), xl[:], start=True, stop=True)
                for b in range(B):
                    pe.matmul(ps[:, 0, (1 + b) * M:(2 + b) * M], W(f"wq_twice{b}"), xl[:], start=True, stop=True)
                    pe.matmul(ps[:, 1, (1 + b) * M:(2 + b) * M], W(f"wk_twice{b}"), xl[:], start=True, stop=True)
                pe.matmul(ps[:, 1, 0:M], W("wk"), xl[:], start=True, stop=True).then_inc(s_pr, 1)
                for n in range(3, 5):
                    convolve(pe, n)
                wait_alone(pe, s_b, turn + 1, L.sem("waits_passed"))
                for b in range(B):
                    ins = pe.matmul(ps[:, 2 + b, :], ql[:].rearrange("p b m -> p (b m)"),
                                    kd[:, b].rearrange("p h m -> p (h m)"), start=True, stop=True)
                ins.then_inc(s_at, 1)
                for n in range(5, 10):
                    convolve(pe, n)
                wait_alone(pe, s_mx, 2 * turn + 1, L.sem("waits_passed"))
                for h in range(NH):
                    ins = pe.transpose(ps[:, 4 + h // 4, h % 4 * P:(h % 4 + 1) * P],
                                       X_diag[:, h].rearrange("p b m -> p (b m)"), W("ident"))
                ins.then_inc(s_tr, 1)
                for n in range(10, NH * B):
                    convolve(pe, n)


def with_inverse(eng, emit):
    for s in range(4):
        emit(0, None, s, None)
    with eng.Fori(0, Layer.ITERS) as i:
        for s in range(4):
            emit(i + 1, i, s, i)
    for c in range(Layer.ITERS + 1, NCH):
        for s in range(4):
            emit(c, c - 1, s, None)
    for s in range(2):
        emit(None, NCH - 1, s, None)


def landmark_values(L, turn, xnT, V, q12, O, XT_diag, Z, ZT, ZT_diag):
    nc, ps, W, sem = L.nc, L.ps, L.W, L.sem
    HP, VP, ITERS = L.HP, L.VP, L.ITERS
    s_kp, s_kc, s_s, s_cm, s_nm, s_e, s_al, s_t, s_tc, s_td, s_pv, s_o, s_i = (sem("lv_" + n) for n in (
        "k_projected", "k_part1", "scores", "chunk_max", "new_max", "exp", "alpha", "transposed", "copied_act",
        "copied_dve", "pv", "summed", "init"))
    s_p = sem("pinv_product")
    s_c = sem("pinv_terms")
    s_z = sem("pinv_copied")
    s_td2 = sem("pinv_terms_diag")
    s_zd = sem("pinv_diag")
    s_k2 = sem("lv_k_part2")
    UPC = 2 * B
    SUM_BANK = (4, 5)
    INV_BANK, KEY_BANK = 6, 7
    with ExitStack() as stage:
        kT = L.sb("lv_kT", [P, B, CHUNK], stage, F16)
        k1 = L.sb("lv_k_part1", [P, B, CHUNK], stage, F16)
        pr = L.sb("lv_probs", [P, 2, 2, CHUNK], stage)
        prT = L.sb("lv_probsT", [P, 2, 2, TPC, P], stage)
        cm = L.sb("lv_chunk_max", [P, B, HP], stage)
        mx = L.sb("lv_max", [P, B, HP], stage)
        neg = L.sb("lv_neg_max", [P, B, HP], stage)
        dl = L.sb("lv_delta", [P, B, HP], stage)
        al = L.sb("lv_alpha", [P, B, HP], stage)
        minus = L.sb("lv_minus_unscale", [P, 1], stage)
        A_diag = L.sb("XZ", [P, NH, B, M], stage)
        T = L.sb("pinv_T", [P, 2, NH, M], stage)
        T_diag = L.sb("pinv_T_diag", [P, NH, B, M], stage)
        eye = W("eye").rearrange("p (h m) -> p h m", h=1).broadcast_to([P, NH, M])
        u_of = lambda c, s: UPC * (NCH * turn + c) + s
        k_of = lambda c, b: B * (NCH * turn + c) + b
        lower, upper = slice(0, C), slice(C, P)
        p_of = lambda i: 5 * (ITERS * turn + i)
        c_of = lambda i: 3 * (ITERS * turn + i)
        z_of = lambda i: 2 * (ITERS * turn + i) + 1
        d_of = lambda i: ITERS * turn + i
        rows = lambda b: slice(b * M, (b + 1) * M)
        bank = ps[:, INV_BANK, :].rearrange("p (h m) -> p h m", m=M)

        def lagged(fn, now, before, s, lag):
            c, k = (now, s - lag) if s >= lag else (before, s - lag + UPC)
            if c is not None:
                fn(c, k)
        first = lambda c, s: isinstance(c, int) and c == 0 and s < 2
        more_after = lambda c: c is not None and not (isinstance(c, int) and c == NCH - 1)

        with nc.Block() as block:
            @block.tensor
            def _(pe):
                def keys(c, b):
                    if not (isinstance(c, int) and c == 0 and b == 0):
                        pe.wait_ge(s_k2, k_of(c, b))
                    chunk = xnT[:, :].rearrange("p (c n) -> p c n", n=CHUNK)[:, c]
                    pe.matmul(ps[:, KEY_BANK, :], W(f"wk_twice{b}"), chunk, start=True, stop=True).then_inc(s_kp, 1)

                def scores(c, s):
                    b, hf = divmod(s, 2)
                    if hf == 0:
                        pe.wait_ge(s_kc, k_of(c, b) + 1)
                        pe.wait_ge(s_k2, k_of(c, b) + 1)
                    if not first(c, s):
                        pe.wait_ge(s_tc, u_of(c, s) - 1)
                        pe.wait_ge(s_td, u_of(c, s) - 1)
                    for k in range(2):
                        p = 2 * hf + k
                        for part in range(2):
                            ins = pe.matmul(ps[:, 2 * hf + k, :],
                                            q12[:, part, b, 2 * p:2 * p + 2].rearrange("p h m -> p (h m)"), kT[:, b],
                                            start=part == 0, stop=part == 1)
                        ins.then_inc(s_s, 1)

                def transposes(c, s):
                    hf = s % 2
                    for k in range(2):
                        pe.wait_ge(s_e, 2 * u_of(c, s) + k + 1)
                        for t in range(TPC):
                            ins = pe.transpose(ps[:, 2 * hf + k, t * P:(t + 1) * P],
                                               pr[:, hf, k, t * P:(t + 1) * P], W("ident"))
                        ins.then_inc(s_t, 1)

                def values(c, s):
                    b, hf = divmod(s, 2)
                    pe.wait_ge(s_tc, u_of(c, s) + 1)
                    pe.wait_ge(s_td, u_of(c, s) + 1)
                    if not first(c, s):
                        pe.wait_ge(s_o, u_of(c, s) - 1)
                    for k in range(2):
                        for t in range(TPC):
                            vals = V[:, :, b, :, :].rearrange("p (c t) n e -> p c t (n e)", t=TPC)[:, c, t]
                            ins = pe.matmul(ps[:, SUM_BANK[hf], k * HP * VP:(k + 1) * HP * VP], prT[:, hf, k, t], vals,
                                            start=t == 0, stop=t == TPC - 1)
                    ins.then_inc(s_pv, 1)

                def product(stationary, moving):
                    for h in range(NH):
                        ins = pe.matmul(ps[:, INV_BANK, h * M:(h + 1) * M], stationary[:, h].rearrange("p b m -> p (b m)"),
                                        moving[:, h], start=True, stop=True)
                    ins.then_inc(s_p, 1)

                def step(now, before, s, i):
                    lagged(scores, now, before, s, 0)
                    if i is not None and s == 3:
                        wait_alone(pe, s_c, c_of(i) + 3, sem("waits_passed"))
                        wait_alone(pe, s_zd, d_of(i) + 1, sem("waits_passed"))
                        product(ZT_diag, T[:, 0])
                    if s == 1 and now is not None:
                        keys(now, 1)
                    if s == 3 and more_after(now):
                        keys(now + 1, 0)
                    lagged(transposes, now, before, s, 1)
                    lagged(values, now, before, s, 2)
                    if i is None:
                        return
                    if s == 0:
                        wait_alone(pe, s_z, z_of(i), sem("waits_passed"))
                        product(XT_diag, Z)
                    elif s < 3:
                        wait_alone(pe, s_c, c_of(i) + s, sem("waits_passed"))
                        product(A_diag, T[:, s - 1])
                    else:
                        wait_alone(pe, s_z, z_of(i) + 1, sem("waits_passed"))
                        wait_alone(pe, s_td2, d_of(i) + 1, sem("waits_passed"))
                        product(T_diag, ZT)
                keys(0, 0)
                with_inverse(pe, step)

            @block.vector
            def _(dve):
                def maxima(c, s):
                    b, hf = divmod(s, 2)
                    for k in range(2):
                        dve.wait_ge(s_s, 2 * u_of(c, s) + k + 1)
                        p = 2 * hf + k
                        dve.tensor_reduce(cm[:, b, p:p + 1], ps[:, p, :], AX.X, ALU.max).then_inc(s_cm, 1)

                def running(c, s):
                    b, hf = divmod(s, 2)
                    r = slice(2 * hf, 2 * hf + 2)
                    dve.wait_ge(s_cm, 2 * u_of(c, s) + 2)
                    dve.tensor_tensor(cm[:, b, r], cm[:, b, r], mx[:, b, r], ALU.max).then_inc(s_nm, 1)
                    dve.wait_ge(s_nm, 3 * u_of(c, s) + 1)
                    dve.tensor_scalar(neg[:, b, r], cm[:, b, r], minus[:], None, ALU.mult)
                    dve.tensor_tensor(dl[:, b, r], mx[:, b, r], cm[:, b, r], ALU.subtract).then_inc(s_nm, 1)
                    dve.wait_ge(s_nm, 3 * u_of(c, s) + 2)
                    dve.tensor_copy(mx[:, b, r], cm[:, b, r]).then_inc(s_nm, 1)

                def copied(c, s):
                    hf = s % 2
                    dve.wait_ge(s_t, 2 * u_of(c, s) + 2)
                    dve.tensor_copy(prT[:, hf, 1], ps[:, 2 * hf + 1, :].rearrange("p (t n) -> p t n", n=P)).then_inc(s_td, 1)

                def sums(c, s):
                    b, hf = divmod(s, 2)
                    dve.wait_ge(s_al, u_of(c, s) + 1)
                    dve.wait_ge(s_pv, u_of(c, s) + 1)
                    if not first(c, s):
                        dve.wait_ge(s_o, u_of(c, s) - 1)
                    for k in range(2):
                        p = 2 * hf + k
                        ins = dve.scalar_tensor_tensor(O[:, b, p], O[:, b, p], al[:, b, p:p + 1],
                                                       ps[:, SUM_BANK[hf], (k * HP + p) * VP:(k * HP + p + 1) * VP], ALU.mult,
                                                       ALU.add)
                    ins.then_inc(s_o, 1)

                def keys(c, b):
                    dve.wait_ge(s_kc, k_of(c, b) + 1)
                    dve.scalar_tensor_tensor(kT[upper, b], ps[upper, KEY_BANK, :], L.scale[upper, 1:2], k1[upper, b],
                                             ALU.mult, ALU.subtract).then_inc(s_k2, 1)

                def step(now, before, s, i):
                    lagged(maxima, now, before, s, 0)
                    if s == 1 and now is not None:
                        keys(now, 1)
                    if s == 3 and more_after(now):
                        keys(now + 1, 0)
                    lagged(copied, now, before, s, 1)
                    lagged(running, now, before, s, 0)
                    lagged(sums, now, before, s, 2)
                    if i is not None and s < 3:
                        dve.wait_ge(s_p, p_of(i) + s + 1)
                        if s == 0:
                            for b in range(B):
                                dve.tensor_copy(A_diag[rows(b), :, b], bank[rows(b)])
                        dve.scalar_tensor_tensor(T[:, s % 2], eye, (7.0, 15.0, 13.0)[s], bank, ALU.mult,
                                                 ALU.subtract).then_inc(s_c, 1)
                dve.memset(mx[:], -1e30)
                dve.memset(A_diag[:], 0.0)
                dve.memset(O[:], 0.0).then_inc(s_i, 1)
                dve.tensor_scalar(minus[:], L.unscale[:], -1.0, None, ALU.mult).then_inc(s_i, 1)
                wait_alone(dve, s_i, 2 * turn + 2, sem("waits_passed"))
                keys(0, 0)
                with_inverse(dve, step)

            @block.scalar
            def _(act):
                def keys(c, b):
                    act.wait_ge(s_kp, k_of(c, b) + 1)
                    act.activation(k1[upper, b], ps[upper, KEY_BANK, :], ACT.Copy, scale=L.scale[upper, 1:2])
                    act.activation(kT[lower, b], ps[lower, KEY_BANK, :], ACT.Copy, scale=L.scale[lower, 1:2]).then_inc(s_kc, 1)

                def copied(c, s):
                    hf = s % 2
                    act.wait_ge(s_t, 2 * u_of(c, s) + 1)
                    act.activation(prT[:, hf, 0], ps[:, 2 * hf, :].rearrange("p (t n) -> p t n", n=P),
                                   ACT.Copy).then_inc(s_tc, 1)

                def exponentials(c, s):
                    b, hf = divmod(s, 2)
                    act.wait_ge(s_nm, 3 * u_of(c, s) + 2)
                    for k in range(2):
                        p = 2 * hf + k
                        act.activation(pr[:, hf, k], ps[:, p, :], ACT.Exp, bias=neg[:, b, p:p + 1],
                                       scale=L.unscale[:]).then_inc(s_e, 1)
                    act.activation(al[:, b, 2 * hf:2 * hf + 2], dl[:, b, 2 * hf:2 * hf + 2], ACT.Exp,
                                   scale=L.unscale[:]).then_inc(s_al, 1)

                def scaled(out, count):
                    act.wait_ge(s_p, count)
                    act.activation(out[:], bank, ACT.Copy, scale=0.25).then_inc(s_z, 1)

                def step(now, before, s, i):
                    if i is not None and s == 3:
                        scaled(Z, p_of(i) + 4)
                    if s == 1 and now is not None:
                        keys(now, 1)
                    if s == 3 and more_after(now):
                        keys(now + 1, 0)
                    lagged(copied, now, before, s, 1)
                    lagged(exponentials, now, before, s, 0)
                    if i is not None and s == 3:
                        scaled(ZT, p_of(i) + 5)
                keys(0, 0)
                with_inverse(act, step)

            @block.gpsimd
            def _(pool):
                batches = W("batch_of").rearrange("p (h b m) -> p h b m", h=1, m=1).broadcast_to([P, NH, B, M])
                twice = lambda a: a.rearrange("p h (n m) -> p h n m", n=1).broadcast_to([P, NH, B, M])
                with pool.Fori(0, ITERS) as i:
                    wait_alone(pool, s_c, c_of(i) + 3, sem("waits_passed"))
                    pool.tensor_tensor(T_diag[:], twice(T[:, 0]), batches, ALU.mult).then_inc(s_td2, 1)
                    wait_alone(pool, s_z, z_of(i) + 2, sem("waits_passed"))
                    pool.tensor_tensor(ZT_diag[:], twice(ZT[:]), batches, ALU.mult).then_inc(s_zd, 1)


def landmark_weights(L, turn, O, ZT_diag, w_diag):
    nc, ps, W, sem = L.nc, L.ps, L.W, L.sem
    HP, V1, G = L.HP, L.V1, B * L.HP
    s_i, s_p = (sem("lw_" + n) for n in ("init", "product"))
    with ExitStack() as stage:
        inv = L.sb("lw_inv", [P, G], stage)
        On = L.sb("lw_o", [P, G, HD], stage)
        O0 = L.sb("lw_o0", [P, HP, 2, HD], stage)
        with nc.Block() as block:
            @block.vector
            def _(dve):
                st = Steps(dve, s_i)
                st.enter(turn, 10)
                st.tick(dve.memset(w_diag[:], 0.0))
                O3 = O[:, :, :, :].rearrange("p b h e -> p (b h) e")
                st.tick(dve.reciprocal(inv[:], O3[:, :, 2 * HD]))
                st.hold()
                for q in range(2):
                    rows = slice(q * M, (q + 1) * M)
                    st.tick(dve.memset(w_diag[rows, :, :, q, HD:V1], 1.0))
                    wide = inv[rows].rearrange("p (g e) -> p g e", e=1).broadcast_to([M, G, HD])
                    st.tick(dve.tensor_tensor(On[rows], O3[rows, :, q * HD:(q + 1) * HD], wide, ALU.mult))
                st.hold()
                for q in range(2):
                    for b in range(B):
                        st.tick(dve.tensor_copy(O0[b * M:(b + 1) * M, :, q], On[q * M:(q + 1) * M, b * HP:(b + 1) * HP]))
                st.hold()
                st.leave(1)
                dve.wait_ge(s_p, turn + 1)
                for q in range(2):
                    for b in range(B):
                        dve.tensor_copy(w_diag[q * M:(q + 1) * M, b, :, q, 0:HD], ps[b * M:(b + 1) * M, 0, 0:C].rearrange(
                            "p (h q d) -> p h q d", q=2, d=HD)[:, :, q])

            @block.tensor
            def _(pe):
                wait_alone(pe, s_i, 10 * turn + 10, L.sem("waits_passed"))
                for h in range(NH):
                    ins = pe.matmul(ps[:, 0, h * HD:(h + 1) * HD], ZT_diag[:, h].rearrange("p b m -> p (b m)"),
                                    O0[:, h // 2, h % 2], start=True, stop=True)
                ins.then_inc(s_p, 1)


def attend(L, turn, xnT, k12, w_diag, res, y, norm):
    nc, ps, W, sem = L.nc, L.ps, L.W, L.sem
    HP, V1 = L.HP, L.V1
    s_qp, s_qc, s_s, s_mx, s_sub, s_e, s_t, s_tc, s_pv, s_iv, s_ar, s_ot, s_otc, s_pr, s_y, s_b = (
        sem("at_" + n) for n in ("q_projected", "q_copied", "scores", "max", "sub", "exp", "transposed", "copied",
                                 "pv", "inverse", "with_res", "outT", "outT_copied", "projected", "y",
                                 "bias_added"))
    s_q2 = sem("at_q_part2")
    s_sum, s_ce, s_sq, s_ss = L.norm_sems()
    with ExitStack() as stage:
        qT = L.sb("at_qT", [P, 2, B, P], stage, F16)
        q1 = L.sb("at_q_part1", [P, 2, B, P], stage, F16)
        sc = L.sb("at_scores", [P, 4, NH * M], stage)
        prT = L.sb("at_probsT", [P, 4, HP, P], stage)
        mx = L.sb("at_max", [P, 4, NH], stage)
        inv = L.sb("at_inv", [P, 2, B * NH], stage)
        o = L.sb("at_out", [P, 2, B, NH, HD], stage)
        oT = L.sb("at_outT", [P, 2, P], stage)
        square = L.sb("at_square", [P, 2, B, C], stage)
        small = lambda a, i, lane: a[:, :, :].rearrange("p (i k) b -> p i k b", k=2)[:, i, lane]
        m = lambda i, lane: NT * turn + 2 * i + lane
        mn = lambda i, lane: (NT + 2 * NCH) * turn + 2 * i + lane
        n = lambda i, lane, b: B * (NT * turn + 2 * i + lane) + b
        tile = lambda a, i, lane: a[:, :, :, :].rearrange("p (i k) b e -> p i k b e", k=2)[:, i, lane]
        with nc.Block() as block:
            @block.tensor
            def _(pe):
                def queries(i, lane):
                    wait_alone(pe, s_y, m(i, lane) + 5 * turn + 1, sem("waits_passed"))
                    toks = xnT[:, :].rearrange("p (i k n) -> p i k n", k=2, n=P)[:, i, lane]
                    for b in range(B):
                        ins = pe.matmul(ps[:, 7 - lane, b * P:(b + 1) * P], W(f"wq_twice{b}"), toks, start=True, stop=True)
                    ins.then_inc(s_qp, 1)

                def product(i, lane):
                    pe.wait_ge(s_qc, m(i, lane) + 1)
                    pe.wait_ge(s_q2, m(i, lane) + 1)
                    for b in range(B):
                        for part in range(2):
                            ins = pe.matmul(ps[:, 2 * lane + b, :], qT[:, lane, b], k12[:, part, b].rearrange(
                                "p h m -> p (h m)"), start=part == 0, stop=part == 1)
                        ins.then_inc(s_s, 1)

                def transposes(i, lane):
                    for b in range(B):
                        k = 2 * lane + b
                        pe.wait_ge(s_e, n(i, lane, b) + 1)
                        for p in range(HP):
                            ins = pe.transpose(ps[:, k, p * P:(p + 1) * P], sc[:, k, p * P:(p + 1) * P], W("ident"))
                        ins.then_inc(s_t, 1)

                def outputs(i, lane):
                    for b in range(B):
                        pe.wait_ge(s_tc, n(i, lane, b) + 1)
                        for p in range(HP):
                            at = (b * HP + p) * 2 * V1
                            ins = pe.matmul(ps[:, 4 + lane, at:at + 2 * V1], prT[:, 2 * lane + b, p],
                                            w_diag[:, b, p].rearrange("p q e -> p (q e)"), start=True, stop=True)
                    ins.then_inc(s_pv, 1)

                def turned(i, lane):
                    pe.wait_ge(s_ar, m(i, lane) + 1)
                    ahead = min(3, NT - 1 - 2 * i - lane) if isinstance(i, int) else 3
                    pe.wait_ge(s_q2, m(i, lane) + ahead + 1)
                    pe.transpose(ps[:, 6 + lane, 2 * P:3 * P], o[:, lane].rearrange("p b h d -> p (b h d)"),
                                 W("ident")).then_inc(s_ot, 1)

                def projected(i, lane):
                    pe.wait_ge(s_otc, m(i, lane) + 1)
                    pe.matmul(ps[:, 6 + lane, 3 * P:4 * P], oT[:, lane], W("w_out"), start=True,
                              stop=True).then_inc(s_pr, 1)
                pe.sem_inc(s_y, 5)
                pipelined(pe, NT, [(3, transposes), (2, product), (4, turned), (3, outputs), (0, queries),
                                   (4, projected)])

            @block.vector
            def _(dve):
                def softmax(i, lane):
                    s3 = lambda b: ps[:, 2 * lane + b, :].rearrange("p (h m) -> p h m", h=NH)
                    for b in range(B):
                        dve.wait_ge(s_s, n(i, lane, b) + 1)
                        dve.tensor_reduce(mx[:, 2 * lane + b], s3(b), AX.X, ALU.max).then_inc(s_mx, 1)
                    for b in range(B):
                        dve.wait_ge(s_mx, n(i, lane, b) + 1)
                        wide = mx[:, 2 * lane + b].rearrange("p (h m) -> p h m", m=1).broadcast_to([P, NH, M])
                        dve.tensor_tensor(sc[:, 2 * lane + b].rearrange("p (h m) -> p h m", h=NH), s3(b), wide,
                                          ALU.subtract).then_inc(s_sub, 1)

                def normalise(i, lane):
                    pv = ps[:, 4 + lane, 0:B * NH * V1].rearrange("p (g e) -> p g e", e=V1)
                    dve.wait_ge(s_pv, m(i, lane) + 1)
                    dve.reciprocal(inv[:, lane], pv[:, :, HD]).then_inc(s_iv, 1)
                    dve.wait_ge(s_iv, 2 * m(i, lane) + 1)
                    wide = inv[:, lane].rearrange("p (g e) -> p g e", e=1).broadcast_to([P, B * NH, HD])
                    dve.tensor_tensor(o[:, lane].rearrange("p b h d -> p (b h) d"), pv[:, :, 0:HD], wide,
                                      ALU.mult).then_inc(s_iv, 1)
                    dve.wait_ge(s_iv, 2 * m(i, lane) + 2)
                    both_b = o[:, lane].rearrange("p b h d -> p b (h d)")
                    dve.tensor_tensor(both_b, both_b, tile(res, i, lane), ALU.add).then_inc(s_ar, 1)

                def projected(i, lane):
                    dve.wait_ge(s_pr, m(i, lane) + 1)
                    dve.tensor_tensor(tile(y, i, lane), tile(y, i, lane), ps[:, 6 + lane, 3 * P:4 * P].rearrange(
                        "p (b e) -> p b e", b=B), ALU.add).then_inc(s_y, 1)

                def queries(i, lane):
                    dve.wait_ge(s_qc, m(i, lane) + 1)
                    upper = slice(C, P)
                    dve.scalar_tensor_tensor(qT[upper, lane], ps[upper, 7 - lane, 0:B * P].rearrange(
                        "p (b n) -> p b n", b=B), L.scale[upper, 0:1], q1[upper, lane], ALU.mult,
                        ALU.subtract).then_inc(s_q2, 1)

                def sums(i, lane):
                    dve.wait_ge(s_y, m(i, lane) + 5 * turn + 6)
                    dve.tensor_reduce(small(norm.mean, i, lane), tile(y, i, lane), AX.X, ALU.add).then_inc(s_sum, 1)

                def means(i, lane):
                    dve.wait_ge(s_sum, 2 * mn(i, lane) + 1)
                    mean = small(norm.mean, i, lane)
                    dve.tensor_scalar(mean, mean, 1.0 / C, None, ALU.mult).then_inc(s_sum, 1)

                def sums_of_squares(i, lane):
                    dve.wait_ge(s_sq, mn(i, lane) + 1)
                    dve.tensor_reduce(small(norm.rstd, i, lane), square[:, lane], AX.X, ALU.add).then_inc(s_ss, 1)
                wait_alone(dve, s_b, NCH * turn + NCH, L.sem("waits_passed"))
                pipelined(dve, NT, [(2, softmax), (3, normalise), (5, sums), (7, sums_of_squares), (5, means),
                                    (0, queries), (4, projected)])

            @block.gpsimd
            def _(pool):
                wide = W("b_out").rearrange("p (t b c) -> p t b c", t=1, b=1).broadcast_to([P, TPC, B, C])
                with pool.Fori(0, NCH) as c:
                    rows = y[:, :, :, :].rearrange("p (c t) b e -> p c t b e", t=TPC)[:, c]
                    pool.tensor_tensor(rows, rows, wide, ALU.add).then_inc(s_b, 1)

                def centre(i, lane):
                    pool.wait_ge(s_sum, 2 * mn(i, lane) + 2)
                    mean = small(norm.mean, i, lane).rearrange("p (b n) -> p b n", n=1).broadcast_to([P, B, C])
                    pool.tensor_tensor(tile(norm.centred, i, lane), tile(y, i, lane), mean, ALU.subtract).then_inc(s_ce, 1)
                pipelined(pool, NT, [(0, centre)])

            @block.scalar
            def _(act):
                def squares(i, lane):
                    act.wait_ge(s_ce, mn(i, lane) + 1)
                    if later(i):
                        act.wait_ge(s_ss, mn(i, lane) - 1)
                    act.activation(square[:, lane], tile(norm.centred, i, lane), ACT.Square).then_inc(s_sq, 1)

                def queries(i, lane):
                    act.wait_ge(s_qp, m(i, lane) + 1)
                    rows = lambda r: ps[r, 7 - lane, 0:B * P].rearrange("p (b n) -> p b n", b=B)
                    lower, upper = slice(0, C), slice(C, P)
                    act.activation(q1[upper, lane], rows(upper), ACT.Copy, scale=L.scale[upper, 0:1])
                    act.activation(qT[lower, lane], rows(lower), ACT.Copy, scale=L.scale[lower, 0:1]).then_inc(s_qc, 1)

                def exponentials(i, lane):
                    for b in range(B):
                        k = 2 * lane + b
                        act.wait_ge(s_sub, n(i, lane, b) + 1)
                        act.activation(sc[:, k], sc[:, k], ACT.Exp, scale=L.unscale[:]).then_inc(s_e, 1)

                def probabilities(i, lane):
                    for b in range(B):
                        k = 2 * lane + b
                        act.wait_ge(s_t, n(i, lane, b) + 1)
                        act.activation(prT[:, k], ps[:, k, :].rearrange("p (h n) -> p h n", n=P),
                                       ACT.Copy).then_inc(s_tc, 1)

                def turned(i, lane):
                    act.wait_ge(s_ot, m(i, lane) + 1)
                    act.activation(oT[:, lane], ps[:, 6 + lane, 2 * P:3 * P], ACT.Copy).then_inc(s_otc, 1)
                pipelined(act, NT, [(3, probabilities), (4, turned), (6, squares), (2, exponentials), (0, queries)])


def feed_forward(L, turn, norm, y, fetch):
    nc, ps, W, sem = L.nc, L.ps, L.W_ff, L.sem
    s_res = sem("ff_residual")
    s_sum, s_ce, s_sq, s_ss = L.norm_sems()
    s_n, s_t, s_x = (sem("normed_" + n) for n in ("ready", "transposed", "xT_ready"))
    s_h, s_g, s_o, s_b, s_y = (sem("ff_" + n) for n in ("hidden", "gelu", "out", "bias_added", "y"))
    NU = 2 * NCH
    at = lambda i, lane: NU * turn + 2 * i + lane
    mn = lambda i, lane: (NT + NU) * turn + NT + 2 * i + lane
    small = lambda a, i, lane: a[:, :, :].rearrange("p (i k t) b -> p i k t b", k=2, t=TPH)[:, i, lane]
    at_n = lambda i, lane: NU * (2 * turn + 1) + 2 * i + lane
    with ExitStack() as stage:
        xn = L.sb("ff_xn", [P, 2, TPH, B, C], stage)
        xs = L.sb("ff_xs", [P, 2, HALF], stage)
        hd = L.sb("ff_hidden", [P, 2, B, HALF], stage)
        unused = L.sb("ff_unused", [P, 1], stage)
        square = L.sb("ff_square", [P, 2, TPH, B, C], stage)
        with nc.Block() as block:
            @block.gpsimd
            def _(pool):
                wide = W("b2").rearrange("p (t b c) -> p t b c", t=1, b=1).broadcast_to([P, TPH, B, C])

                def bias(i, lane):
                    pool.tensor_tensor(half_of(y, i, lane), half_of(y, i, lane), wide, ALU.add).then_inc(s_b, 1)
                pipelined(pool, NU, [(0, bias)])

                def centre(i, lane):
                    pool.wait_ge(s_sum, 2 * mn(i, lane) + 2)
                    mean = small(norm.mean, i, lane).rearrange("p t (b n) -> p t b n", n=1).broadcast_to([P, TPH, B, C])
                    pool.tensor_tensor(half_of(norm.centred, i, lane), half_of(y, i, lane), mean,
                                       ALU.subtract).then_inc(s_ce, 1)
                pipelined(pool, NU, [(0, centre)])

            @block.vector
            def _(dve):
                def normalise(i, lane):
                    if later(i):
                        dve.wait_ge(s_t, at_n(i, lane) - 1)
                    half_normed(dve, norm, xn[:, lane], i, lane).then_inc(s_n, 1)

                def add(i, lane):
                    dve.wait_ge(s_o, at(i, lane) + 1)
                    dve.wait_ge(s_b, at(i, lane) + 1)
                    dve.tensor_tensor(half_of(y, i, lane), half_of(y, i, lane), ps[:, 4 + lane, 0:HALF].rearrange(
                        "p (t b c) -> p t b c", t=TPH, b=B), ALU.add).then_inc(s_y, 1)

                def residual(i, lane):
                    dve.wait_ge(s_y, at(i, lane) + 1)
                    dve.scalar_tensor_tensor(half_of(y, i, lane), half_of(L.hh, i, lane), L.last[:],
                                             half_of(y, i, lane), ALU.mult, ALU.add).then_inc(s_res, 1)

                def sums(i, lane):
                    dve.wait_ge(s_res, at(i, lane) + 1)
                    dve.tensor_reduce(small(norm.mean, i, lane), half_of(y, i, lane), AX.X, ALU.add).then_inc(s_sum, 1)

                def means(i, lane):
                    dve.wait_ge(s_sum, 2 * mn(i, lane) + 1)
                    mean = small(norm.mean, i, lane)
                    dve.tensor_scalar(mean, mean, 1.0 / C, None, ALU.mult).then_inc(s_sum, 1)

                def sums_of_squares(i, lane):
                    dve.wait_ge(s_sq, mn(i, lane) + 1)
                    dve.tensor_reduce(small(norm.rstd, i, lane), square[:, lane], AX.X, ALU.add).then_inc(s_ss, 1)
                pipelined(dve, NU, [(0, normalise), (4, add), (6, sums), (5, residual), (6, means),
                                    (8, sums_of_squares)])

            @block.tensor
            def _(pe):
                def transposes(i, lane):
                    pe.wait_ge(s_n, at_n(i, lane) + 1)
                    if later(i):
                        pe.wait_ge(s_x, at_n(i, lane) - 1)
                    for t in range(TPH):
                        ins = pe.transpose(ps[:, lane, t * P:(t + 1) * P], xn[:, lane, t].rearrange("p b c -> p (b c)"),
                                           W("ident"))
                    ins.then_inc(s_t, 1)

                def hidden(i, lane):
                    pe.wait_ge(s_x, at_n(i, lane) + 1)
                    if later(i):
                        pe.wait_ge(s_g, at(i, lane) - 1)
                    for b in range(B):
                        ins = pe.matmul(ps[:, 2 + lane, b * HALF:(b + 1) * HALF], W(f"w1_{b}"), xs[:, lane], start=True,
                                        stop=True)
                    ins.then_inc(s_h, 1)

                def output(i, lane):
                    pe.wait_ge(s_g, at(i, lane) + 1)
                    if later(i):
                        pe.wait_ge(s_y, at(i, lane) - 1)
                    for t in range(TPH):
                        for b in range(B):
                            ins = pe.matmul(ps[:, 4 + lane, (t * B + b) * C:(t * B + b + 1) * C],
                                            hd[:, lane, b, t * P:(t + 1) * P], W("w2"), start=True, stop=True)
                    ins.then_inc(s_o, 1)
                pipelined(pe, NU, [(2, hidden), (1, transposes), (3, output)])

            @block.scalar
            def _(act):
                def turned(i, lane):
                    act.wait_ge(s_t, at_n(i, lane) + 1)
                    if later(i):
                        act.wait_ge(s_h, at(i, lane) - 1)
                    act.activation(xs[:, lane], ps[:, lane, 0:HALF], ACT.Identity, bias=W("ln2_b"),
                                   scale=W("ln2_g")).then_inc(s_x, 1)

                def gelu(i, lane):
                    act.wait_ge(s_h, at(i, lane) + 1)
                    if later(i):
                        act.wait_ge(s_o, at(i, lane) - 1)
                    act.activation(hd[:, lane].rearrange("p b n -> p (b n)"), ps[:, 2 + lane, :], ACT.Gelu,
                                   bias=W("b1")).then_inc(s_g, 1)

                def squares(i, lane):
                    act.wait_ge(s_ce, mn(i, lane) + 1)
                    if later(i):
                        act.wait_ge(s_ss, mn(i, lane) - 1)
                    act.activation(square[:, lane], half_of(norm.centred, i, lane), ACT.Square).then_inc(s_sq, 1)
                act.activation(unused[:], W("b1"), ACT.Gelu)
                pipelined(act, NU, [(2, gelu), (1, turned), (7, squares)])

            @block.sync
            def _(sp):
                fetch(sp)


def attention_layer(L, turn, norm, fetch_ff, fetch_next, wait_for):
    with L.nc.Block() as block:
        @block.sync
        def _(sp):
            wait_for(sp, 0)
            fetch_ff(sp)
    y, HP = L.y, L.HP
    with ExitStack() as stage:
        xnT = L.sb("xnT", [P, N_TOK], stage)
        V_padded = L.sb("V", [P, NT + 2, B, HP, L.VP], stage)
        V = V_padded[:, 1:NT + 1]
        w_diag = L.sb("w_diag", [P, B, HP, 2, L.V1], stage)
        k12 = L.sb("k12", [P, 2, B, NH, M], stage, F16)
        project_values(L, turn, norm, xnT, V, V_padded)
        res = norm.centred
        with ExitStack() as inner:
            X_diag, XT_diag, ZT_diag = (L.sb(n, [P, NH, B, M], inner) for n in ("X_diag", "XT_diag", "ZT_diag"))
            Z, ZT = (L.sb(n, [P, NH, M], inner) for n in ("Z", "ZT"))
            q12 = L.sb("q12", [P, 2, B, NH, M], inner, F16)
            O = L.sb("O", [P, B, HP, L.VP], inner)
            landmarks(L, turn, xnT, V_padded, res, q12, k12, X_diag, XT_diag, Z, ZT, ZT_diag)
            landmark_values(L, turn, xnT, V, q12, O, XT_diag, Z, ZT, ZT_diag)
            landmark_weights(L, turn, O, ZT_diag, w_diag)
        attend(L, turn, xnT, k12, w_diag, res, y, norm)
    with L.nc.Block() as block:
        @block.sync
        def _(sp):
            wait_for(sp, 1)
    norm.finish(2, 2 * turn)
    feed_forward(L, turn, norm, y, fetch_next)
    with L.nc.Block() as block:
        @block.vector
        def _(dve):
            dve.memset(L.last[:], 1.0)
    norm.finish(2, 2 * turn + 1)



NE = 16
HID = 128
TOP = 2


class Experts:

    X_SCALE = 2.0 ** 10
    W_PEAK = 2.0 ** 10
    QUARTERS = 4

    def __init__(self, nc, ctx):
        self.nc = nc
        sb = lambda n, s, d=F16: ctx.enter_context(nc.sbuf_tensor("moe_" + n, s, d))
        self.w_a = sb("w_part1", [P, NE, 2 * HID])
        self.w_b = sb("w_part2", [P, NE, 2 * HID])
        self.down = sb("down", [P, NE, C], F32)
        self.unscale = sb("unscale", [P, 1], F32)
        self.s_load, self.s_dve, self.s_all, self.s_w, self.s_a, self.s_b = (
            ctx.enter_context(nc.semaphore("moe_" + n)) for n in (
                "weights_loaded", "dve", "peak_of_all", "scale", "w_part1", "w_part2"))

    def place(self, ctx):
        sb = lambda n, s: ctx.enter_context(self.nc.sbuf_tensor("moe_" + n, s, F32))
        self.raw = sb("raw", [P, NE, 2 * HID])
        self.peak = sb("peak", [P, 1])
        self.all = sb("peak_of_all", [P, 1])
        self.inv = sb("scale", [P, 1])

    def load(self, sp, w1, w2, w3):
        for half in range(2):
            for k, w in enumerate((w1, w2)):
                sp.dma_start(self.raw[half * C:(half + 1) * C, :, k * HID:(k + 1) * HID],
                             w.rearrange("e c h -> c e h")).then_inc(self.s_load, 16)
        sp.dma_start(self.down[:], w3.rearrange("e h c -> h e c")).then_inc(self.s_load, 16)

    def quarters(self, t):
        n = NE // self.QUARTERS
        return [t[:, q * n:(q + 1) * n, :] for q in range(self.QUARTERS)]

    def split_vector(self, dve):
        dve.wait_ge(self.s_load, 16 * 5)
        dve.tensor_reduce(self.peak[:], self.raw[:].rearrange("p e h -> p (e h)"), AX.X, ALU.max,
                          apply_absolute_value=True).then_inc(self.s_dve, 1)
        dve.wait_ge(self.s_all, 1)
        dve.tensor_scalar(self.inv[:], self.all[:], 1e-30, None, ALU.max).then_inc(self.s_dve, 1)
        dve.wait_ge(self.s_dve, 2)
        dve.tensor_scalar(self.unscale[:], self.inv[:], 1.0 / (self.X_SCALE * self.W_PEAK), None,
                          ALU.mult).then_inc(self.s_dve, 1)
        dve.wait_ge(self.s_dve, 3)
        dve.reciprocal(self.inv[:], self.inv[:]).then_inc(self.s_dve, 1)
        dve.wait_ge(self.s_dve, 4)
        dve.tensor_scalar(self.inv[:], self.inv[:], self.W_PEAK, None, ALU.mult).then_inc(self.s_w, 1)
        dve.wait_ge(self.s_w, 1)
        for q, (b, raw, a) in enumerate(zip(*map(self.quarters, (self.w_b, self.raw, self.w_a)))):
            dve.wait_ge(self.s_a, q + 1)
            dve.scalar_tensor_tensor(b, raw, self.inv[:], a, ALU.mult, ALU.subtract).then_inc(self.s_b, 1)
        dve.wait_ge(self.s_b, self.QUARTERS)

    def split_gpsimd(self, pool):
        pool.wait_ge(self.s_dve, 1)
        pool.partition_all_reduce(self.all[:], self.peak[:], P, bass.bass_isa.ReduceOp.max).then_inc(self.s_all, 1)

    def split_scalar(self, act):
        act.wait_ge(self.s_w, 1)
        for a, raw in zip(self.quarters(self.w_a), self.quarters(self.raw)):
            act.activation(a, raw, ACT.Copy, scale=self.inv[:]).then_inc(self.s_a, 1)


def route(nc, ctx, ps, norm, x12, gate, W):
    sem = lambda n: ctx.enter_context(nc.semaphore("route_" + n))
    s_n, s_t, s_x, s_2, s_l, s_lg = map(sem, ("ready", "transposed", "xT_ready", "part2", "logits", "logits_copied"))
    s_d, s_e = sem("dve"), sem("exp")
    with ExitStack() as stage:
        sb = lambda n, s, d=F32: stage.enter_context(nc.sbuf_tensor("rt_" + n, s, d))
        xn = sb("xn", [P, B, TPC, 2, C])
        xs = sb("xs", [P, B, CHUNK])
        x1 = sb("x_part1", [P, B, CHUNK], F16)
        prob = sb("prob", [P, NT * B, NE])
        rest = sb("rest", [P, NT * B, NE])
        cand = sb("cand", [P, NT * B, NE])
        small = sb("small", [P, 6, NT * B])
        g = gate[:, :, :, :].rearrange("p t b e -> p (t b) e")
        u_of = lambda c, b: B * c + b
        later = lambda c: not (isinstance(c, int) and c == 0)
        cols = lambda t, c, b, rows: t[rows, b].rearrange("p (c n) -> p c n", n=CHUNK)[:, c]
        lower, upper = slice(0, C), slice(C, P)
        with nc.Block() as block:
            @block.vector
            def _(dve):
                def normalise(c, b):
                    if later(c):
                        dve.wait_ge(s_t, u_of(c, b) - 1)
                    r = norm.rstd[:, :, :].rearrange("p (c t) (b n) -> p c t b n", t=TPC, n=1)[:, c, :, b]
                    x = norm.centred[:, :, :, :].rearrange("p (c t) b n -> p c t b n", t=TPC)[:, c, :, b]
                    for n in range(2):
                        ins = dve.tensor_tensor(xn[:, b, :, n], x, r.broadcast_to([P, TPC, C]), ALU.mult)
                    ins.then_inc(s_n, 1)

                def part2(c, b):
                    dve.wait_ge(s_x, 2 * u_of(c, b) + 2)
                    dve.scalar_tensor_tensor(cols(x12, c, b, upper), xs[upper, b], Experts.X_SCALE, x1[upper, b],
                                             ALU.mult, ALU.subtract).then_inc(s_2, 1)

                def logits(c, b):
                    dve.wait_ge(s_l, u_of(c, b) + 1)
                    out = prob[:, :, :].rearrange("p (c t b) e -> p c t b e", t=TPC, b=B)[:, c, :, b]
                    bias = W("gate_b").rearrange("p (t e) -> p t e", t=1).broadcast_to([P, TPC, NE])
                    dve.tensor_tensor(out, ps[:, 2 + b, 0:TPC * NE].rearrange("p (t e) -> p t e", t=TPC), bias,
                                      ALU.add).then_inc(s_lg, 1)
                pipelined(dve, B * NCH, [(0, normalise), (2, part2), (3, logits)])
                dve.wait_ge(s_lg, B * NCH)
                st = Steps(dve, s_d)

                def do(ins):
                    st.tick(ins)
                    st.hold()
                wide = lambda k: small[:, k].rearrange("p (n e) -> p n e", e=1).broadcast_to([P, NT * B, NE])
                iota = W("expert_iota").rearrange("p (n e) -> p n e", n=1).broadcast_to([P, NT * B, NE])
                do(dve.tensor_reduce(small[:, 0], prob[:], AX.X, ALU.max))
                do(dve.tensor_tensor(prob[:], prob[:], wide(0), ALU.subtract))
                dve.wait_ge(s_e, 1)
                do(dve.tensor_reduce(small[:, 0], prob[:], AX.X, ALU.add))
                do(dve.reciprocal(small[:, 0], small[:, 0]))
                do(dve.tensor_tensor(prob[:], prob[:], wide(0), ALU.mult))
                for k, src in enumerate((prob, rest)):
                    do(dve.tensor_reduce(small[:, 1 + k], src[:], AX.X, ALU.max))
                    do(dve.tensor_tensor(cand[:], src[:], wide(1 + k), ALU.is_equal))
                    do(dve.scalar_tensor_tensor(cand[:], cand[:], -64.0, iota, ALU.mult, ALU.add))
                    do(dve.tensor_reduce(small[:, 3], cand[:], AX.X, ALU.min))
                    do(dve.tensor_tensor(cand[:], cand[:], wide(3), ALU.is_equal))
                    if k == 0:
                        do(dve.scalar_tensor_tensor(rest[:], cand[:], -2.0, prob[:], ALU.mult, ALU.add))
                        do(dve.tensor_tensor(g, cand[:], wide(1), ALU.mult))
                    else:
                        do(dve.tensor_tensor(cand[:], cand[:], wide(2), ALU.mult))
                do(dve.tensor_tensor(small[:, 4], small[:, 1], small[:, 2], ALU.add))
                do(dve.reciprocal(small[:, 4], small[:, 4]))
                do(dve.tensor_tensor(g, g, cand[:], ALU.add))
                do(dve.tensor_tensor(g, g, wide(4), ALU.mult))

            @block.tensor
            def _(pe):
                def transposes(c, b):
                    pe.wait_ge(s_n, u_of(c, b) + 1)
                    if later(c):
                        pe.wait_ge(s_x, 2 * u_of(c, b) - 2)
                    for t in range(TPC):
                        ins = pe.transpose(ps[:, b, t * P:(t + 1) * P], xn[:, b, t].rearrange("p n c -> p (n c)"),
                                           W("ident"))
                    ins.then_inc(s_t, 1)

                def logits(c, b):
                    pe.wait_ge(s_x, 2 * u_of(c, b) + 1)
                    if later(c):
                        pe.wait_ge(s_lg, u_of(c, b) - 1)
                    for t in range(TPC):
                        ins = pe.matmul(ps[:, 2 + b, t * NE:(t + 1) * NE], xs[:, b, t * P:(t + 1) * P], W("gate_w"),
                                        start=True, stop=True)
                    ins.then_inc(s_l, 1)
                pipelined(pe, B * NCH, [(1, transposes), (2, logits)])

            @block.scalar
            def _(act):
                def part1(c, b):
                    act.wait_ge(s_t, u_of(c, b) + 1)
                    if later(c):
                        act.wait_ge(s_l, u_of(c, b) - 1)
                        act.wait_ge(s_2, u_of(c, b) - 1)
                    act.activation(xs[:, b], ps[:, b, :], ACT.Copy).then_inc(s_x, 1)
                    act.activation(cols(x12, c, b, lower), ps[lower, b, :], ACT.Copy, scale=Experts.X_SCALE)
                    act.activation(x1[upper, b], ps[upper, b, :], ACT.Copy, scale=Experts.X_SCALE).then_inc(s_x, 1)
                pipelined(act, B * NCH, [(0, part1)])
                act.wait_ge(s_d, 2)
                act.activation(prob[:], prob[:], ACT.Exp).then_inc(s_e, 1)


def experts(nc, ctx, ps, E, x12, gate, hh, out, s_o):
    sem = lambda n: ctx.enter_context(nc.semaphore("moe_" + n))
    s_h, s_sl, s_hd, s_z, s_gu, s_acc = map(sem, (
        "hidden_products", "silu", "hidden", "out", "out_used", "summed"))
    sb = lambda n, s: ctx.enter_context(nc.sbuf_tensor("moe_" + n, s, F32))
    silu = sb("silu", [P, B, CHUNK])
    hid = sb("hidden", [P, B, CHUNK])
    gated = sb("gated", [P, B, TPC, C])
    unused = sb("unused", [P, 1])
    unit = lambda e, c, b: B * NCH * e + B * c + b

    def in_order(eng, ahead, behind):
        ahead(0, 0, 0)
        with eng.Fori(0, NE - 1) as e:
            with eng.Fori(0, NCH - 1) as c:
                ahead(e, c, 1)
                behind(e, c, 0)
                ahead(e, c + 1, 0)
                behind(e, c, 1)
            ahead(e, NCH - 1, 1)
            behind(e, NCH - 1, 0)
            ahead(e + 1, 0, 0)
            behind(e, NCH - 1, 1)
        e = NE - 1
        with eng.Fori(0, NCH - 1) as c:
            ahead(e, c, 1)
            behind(e, c, 0)
            ahead(e, c + 1, 0)
            behind(e, c, 1)
        ahead(e, NCH - 1, 1)
        behind(e, NCH - 1, 0)
        behind(e, NCH - 1, 1)

    with nc.Block() as block:
        @block.tensor
        def _(pe):
            def hidden(e, c, b):
                cols = lambda t: t[:, b].rearrange("p (c n) -> p c n", n=CHUNK)[:, c]
                for k in range(2):
                    w = lambda t: t[:, e, k * HID:(k + 1) * HID]
                    out = ps[:, 2 * k + b, :]
                    pe.matmul(out, w(E.w_a), cols(x12), start=True, stop=False)
                    pe.matmul(out, w(E.w_b), cols(x12), start=False, stop=True).then_inc(s_h, 1)

            def output(e, c, b):
                pe.wait_ge(s_hd, unit(e, c, b) + 1)
                pe.wait_ge(s_gu, unit(e, c, b) + 1)
                for t in range(TPC):
                    ins = pe.matmul(ps[:, 4 + b, t * C:(t + 1) * C], hid[:, b, t * P:(t + 1) * P], E.down[:, e],
                                    start=True, stop=True)
                ins.then_inc(s_z, 1)
            in_order(pe, hidden, output)

        @block.scalar
        def _(act):
            act.activation(unused[:], E.down[:, 0, 0:1], ACT.Silu)
            with act.Fori(0, NE) as e:
                with act.Fori(0, NCH) as c:
                    for b in range(B):
                        act.wait_ge(s_h, 2 * unit(e, c, b) + 1)
                        act.activation(silu[:, b], ps[:, b, :], ACT.Silu, scale=E.unscale[:]).then_inc(s_sl, 1)

        @block.vector
        def _(dve):
            dve.sem_inc(s_gu, 2)

            def multiply(e, c, b):
                dve.wait_ge(s_h, 2 * unit(e, c, b) + 2)
                dve.wait_ge(s_sl, unit(e, c, b) + 1)
                dve.scalar_tensor_tensor(hid[:, b], ps[:, 2 + b, :], E.unscale[:], silu[:, b], ALU.mult,
                                         ALU.mult).then_inc(s_hd, 1)

            def weigh(e, c, b):
                dve.wait_ge(s_z, unit(e, c, b) + 1)
                dve.wait_ge(s_acc, unit(e, c, b) + 1)
                gt = gate[:, :, :, :].rearrange("p (c t) b (e n) -> p e c b t n", t=TPC, n=1)[:, e, c, b]
                dve.tensor_tensor(gated[:, b], ps[:, 4 + b, 0:TPC * C].rearrange("p (t n) -> p t n", n=C),
                                  gt.broadcast_to([P, TPC, C]), ALU.mult).then_inc(s_gu, 1)
            in_order(dve, multiply, weigh)

        @block.gpsimd
        def _(pool):
            pool.sem_inc(s_acc, 2)
            with pool.Fori(0, NE) as e:
                with pool.Fori(0, NCH) as c:
                    for b in range(B):
                        pool.wait_ge(s_gu, unit(e, c, b) + 3)
                        pool.wait_ge(s_acc, unit(e, c, b) + 2)
                        rows = hh[:, :, :, :].rearrange("p (c t) b n -> p c b t n", t=TPC)[:, c, b]
                        pool.tensor_tensor(rows, rows, gated[:, b], ALU.add).then_inc(s_acc, 1)
            pool.wait_ge(s_acc, unit(NE, 0, 0) + 2)

        @block.sync
        def _(sp):
            with sp.Fori(0, NCH) as c:
                for b in range(B):
                    sp.wait_ge(s_acc, unit(NE - 1, c, b) + 3)
                    rows = hh[:, :, :, :].rearrange("p (c t) b n -> p c b t n", t=TPC)[:, c, b]
                    sp.dma_start(out[b].rearrange("(c t p) n -> p c t n", p=P, t=TPC)[:, c], rows).then_inc(s_o, 16)
            sp.wait_ge(s_o, 16 * B * NCH)


def moe_columns(i):
    c = Columns()
    c.add("ident", (0, P), np.eye(P, dtype=np.float32))
    c.add("gate_w", (0, P), np.concatenate([i["L0_ffn_gate_w"], np.zeros_like(i["L0_ffn_gate_w"])]))
    c.add("gate_b", (0, P), np.tile(i["L0_ffn_gate_b"], (P, 1)))
    c.add("expert_iota", (0, P), np.tile(np.arange(NE, dtype=np.float32), (P, 1)))
    return c


def layer_columns(i, l):
    c, ff = Columns(), Columns()
    zero = np.zeros((C, C), np.float32)
    w = i["L0_attn_w_qkv"][l]
    rep = lambda a: np.tile(np.asarray(a).reshape(1, -1), (P, 1))
    twice = lambda a: np.tile(np.asarray(a).reshape(-1, 1), (B, 1))
    for k in (c, ff):
        k.add("ident", (0, P), np.eye(P, dtype=np.float32))
    c.add("head_of", (0, P), np.tile(np.repeat(np.eye(NH, dtype=np.float32), HD, 0), (B, 1)))
    c.add("unit_of", (0, P), np.repeat(np.eye(B * NH, dtype=np.float32), HD, 0))
    c.add("batch_of", (0, P), np.repeat(np.eye(B, dtype=np.float32), C, 0))
    c.add("eye", (0, P), np.tile(np.eye(M, dtype=np.float32), (B, 1)))
    for b in range(B):
        one = lambda a: np.concatenate([a if k == b else np.zeros_like(a) for k in range(B)], 0)
        ff.add(f"w1_{b}", (0, P), one(i["L0_attn_w1"][l]))
        for name, m in (("wq", w[:, 0:C]), ("wk", w[:, C:2 * C])):
            c.add(f"{name}_twice{b}", (0, P), one(np.concatenate([m, m], 1)))
    c.add("wq", (0, P), both(w[:, 0:C]))
    c.add("wk", (0, P), both(w[:, C:2 * C]))
    c.add("wv", (0, P), both(w[:, 2 * C:]))
    c.add("w_out", (0, P), both(i["L0_attn_w_out"][l]))
    ff.add("w2", (0, P), i["L0_attn_w2"][l])
    for n in ("ln1_g", "ln1_b", "ln2_g", "ln2_b"):
        (c if "ln1" in n else ff).add(n, (0, P), twice(i["L0_attn_" + n][l]))
    ff.add("b1", (0, P), i["L0_attn_b1"][l][:, None])
    c.add("b_out", (0, P), rep(i["L0_attn_b_out"][l]))
    ff.add("b2", (0, P), rep(i["L0_attn_b2"][l]))
    taps = i["L0_attn_res_w"][l][:, 0, :, 0]
    K = taps.shape[1]
    pad = K // 2
    line = np.zeros((NH, 3 * P), np.float32)
    line[:, P + P // 2 - pad:P + P // 2 - pad + K] = taps
    j, o = np.meshgrid(np.arange(P), np.arange(P), indexing="ij")
    banded = lambda shift: line[:, np.clip(j + shift - o + P + P // 2, 0, 3 * P - 1)]
    near, before, after = (banded(s).transpose(1, 0, 2) for s in (0, -P, P))
    for name, m in (("band", near), ("band_before", before), ("band_after", after)):
        c.add(name, (0, P), m.reshape(P, -1))
    return c, ff


def build(nc, x, bytes_rep, positions_rep, w_img, w_txt, w_att, w_ff, w_moe, w1, w2, w3, h_img, out, cols):
    with ExitStack() as ctx:
        ps = ctx.enter_context(nc.psum_tensor("ps", [P, 8, 512], F32))
        hh = ctx.enter_context(nc.sbuf_tensor("hh", [P, NT, B, C], F32))
        sem = lambda n: ctx.enter_context(nc.semaphore(n))
        s_w = sem("weights_loaded")
        s_h = sem("h_loaded")

        def load(stage, name, src, n, wait=True):
            tile = stage.enter_context(nc.sbuf_tensor(name, list(src.shape), F32))
            with nc.Block() as block:
                @block.sync
                def _(sp):
                    sp.dma_start(tile[:], src).then_inc(s_w, 16)
                    if wait:
                        sp.wait_ge(s_w, 16 * n)
            return tile

        with ExitStack() as stage:
            wt = load(stage, "weights_txt", w_txt, 1)
            text_field(nc, stage, sem, ps, bytes_rep, positions_rep, wt, cols["txt"], hh)
        E = Experts(nc, ctx)
        with ExitStack() as raw:
            E.place(raw)
            with ExitStack() as stage:
                wa = load(stage, "weights_img", w_img, 2, False)
                image_attention(nc, stage, sem, ps, x, wa, cols["img"], h_img, hh, s_h,
                                lambda pe: pe.wait_ge(s_w, 16 * 2), lambda sp: E.load(sp, w1, w2, w3),
                                {"vector": E.split_vector, "scalar": E.split_scalar, "gpsimd": E.split_gpsimd})
        norm = Norm(nc, ctx, "norm")
        norm.run(hh, 0)
        s_l = sem("layer_weights_loaded")
        s_lf = sem("layer_ff_weights_loaded")
        y = ctx.enter_context(nc.sbuf_tensor("y", [P, NT, B, C], F32))
        wm = load(ctx, "weights_moe", w_moe, 3, False)
        with ExitStack() as stage:
            att, ff = (stage.enter_context(nc.sbuf_tensor("weights_" + n, [P, cols[n].width], F32)) for n in ("att", "ff"))
            L = Layer(nc, stage, ps, hh, y, (att, cols["att"]), (ff, cols["ff"]))
            first_norm(nc, stage, norm, y, 0)
            with nc.Block() as block:
                @block.gpsimd
                def _(pool):
                    for name in ("pinv_copied", "pinv_diag"):
                        pool.sem_inc(L.sem(name), 1)

                @block.vector
                def _(dve):
                    dve.memset(L.last[:], 0.0)

                @block.sync
                def _(sp):
                    sp.dma_start(att[:], w_att[0]).then_inc(s_l, 16)
            norm.run(y, 1)
            with nc.Fori(0, 2) as turn:
                attention_layer(L, turn, norm,
                                lambda sp: sp.dma_start(ff[:], w_ff[turn]).then_inc(s_lf, 16),
                                lambda sp: sp.dma_start(att[:], w_att[turn * -1 + 1]).then_inc(s_l, 16),
                                lambda sp, n: wait_alone(sp, (s_l, s_lf)[n], 16 * turn + 16, L.sem("waits_passed")))
            with nc.Block() as block:
                @block.sync
                def _(sp):
                    sp.wait_ge(s_l, 16 * 3)
                    sp.wait_ge(s_w, 16 * 3)
        with ExitStack() as stage:
            x12 = stage.enter_context(nc.sbuf_tensor("x_parts", [P, B, N_TOK], F16))
            gate = stage.enter_context(nc.sbuf_tensor("gate", [P, NT, B, NE], F32))
            route(nc, stage, ps, norm, x12, gate, lambda n: cols["moe"].view(wm, n))
            experts(nc, stage, ps, E, x12, gate, y, out, sem("out_stored"))


def both(a):
    z = np.zeros_like(a)
    return np.block([[a, z], [z, a]])


def image_columns(i):
    c = Columns()
    w, bias = i["L0_tok_qkv_w"], i["L0_tok_qkv_b"]
    pair = np.arange(C) ^ 1
    wq, wk, wv = w[0:C], w[C:2 * C], w[2 * C:3 * C]
    bq, bk, bv = bias[0:C], bias[C:2 * C], bias[2 * C:3 * C]
    all_rows = (0, P)
    c.add("ident", all_rows, np.eye(P, dtype=np.float32))
    for name, m in (("wq", wq), ("wq_pair", wq[pair]), ("wk", wk), ("wk_pair", wk[pair]), ("wv", wv)):
        c.add(name, all_rows, both(m.T))
    c.add("bias", all_rows, np.stack([np.tile(m, B) for m in (bq, bq[pair], bk, bk[pair])], 1))
    c.add("bias_v", all_rows, np.tile(bv, (P, B)))
    c.add("wproj", all_rows, both(i["L0_tok_proj_w"].T))
    c.add("bias_proj", all_rows, np.tile(i["L0_tok_proj_b"], (P, 2)))
    half = HD // 2
    freq = (1.0 / 10000.0 ** (np.arange(0, half, 2, dtype=np.float32) / np.float32(half))).astype(np.float32)
    d = np.arange(C) % HD
    y, xx = np.divmod(np.arange(WIN * WIN), WIN)
    pos = np.where((d < half)[:, None], y[None], xx[None]).astype(np.float32)
    ang = pos * freq[(d % half) // 2][:, None]
    sign = np.where(d % 2 == 0, -1.0, 1.0).astype(np.float32)[:, None]
    c.add("cos", all_rows, np.tile(np.cos(ang), (B, 1)))
    c.add("sin", all_rows, np.tile(np.sin(ang) * sign, (B, 1)))
    c.add("batch_of", all_rows, np.repeat(np.eye(B, dtype=np.float32), C, 0))
    c.add("head_of", all_rows, np.tile(np.repeat(np.eye(NH, dtype=np.float32), HD, 0), (B, 1)))
    return c


def kernel(**inputs):
    import concourse.bacc as bacc
    from concourse.bass_utils import run_bass_kernel_spmd

    i = {k: np.asarray(v) for k, v in inputs.items()}
    layers = [layer_columns(i, l) for l in range(i["L0_attn_ln1_g"].shape[0])]
    cols = {"img": image_columns(i), "txt": text_columns(i), "att": layers[0][0], "ff": layers[0][1], "moe": moe_columns(i)}
    arrays = {
        "x": i["x"],
        "bytes_rep": np.broadcast_to(i["x_txt"], (P, B, S_TXT)),
        "positions_rep": np.broadcast_to(i["fside_BS_continuous_positions"], (P, B, S_TXT)),
        "w_img": cols["img"].array(), "w_txt": cols["txt"].array(),
        "w_att": np.stack([c.array() for c, _ in layers]), "w_ff": np.stack([c.array() for _, c in layers]),
        "w_moe": cols["moe"].array(),
        "w1": i["L0_ffn_w1"], "w2": i["L0_ffn_w2"], "w3": i["L0_ffn_w3"],
    }
    arrays = {n: np.ascontiguousarray(a) for n, a in arrays.items()}
    nc = bacc.Bacc("TRN2", target_bir_lowering=False, num_devices=1)
    args = {n: nc.dram_tensor(n, a.shape, mybir.dt.from_np(a.dtype), kind="ExternalInput").ap()
            for n, a in arrays.items()}
    h_img = nc.dram_tensor("h_img", (B, IMG * IMG, C), F32, kind="Internal").ap()
    out = nc.dram_tensor("out_0_dram", (B, N_TOK, C), F32, kind="ExternalOutput").ap()
    build(nc, **args, h_img=h_img, out=out, cols=cols)
    r = run_bass_kernel_spmd(nc, [arrays], core_ids=[0])
    return r.results[0]["out_0_dram"]
```
